# Optimizing a Trainium2 kernel written in Bass

```python
import numpy as np
import jax
import jax.numpy as jnp

def _softmax(x, axis=-1):
    return jax.nn.softmax(x, axis=axis)

def _gelu(x):
    return jax.nn.gelu(x, approximate=True)

def _silu(x):
    return jax.nn.silu(x)

def _sigmoid(x):
    return jax.nn.sigmoid(x)

def _layernorm(x, axis=-1, eps=1e-05):
    m = jnp.mean(x, axis=axis, keepdims=True)
    v = jnp.var(x, axis=axis, keepdims=True)
    return (x - m) / jnp.sqrt(v + eps)

def _scatter_add(tgt, idx, src, axis=0):
    return tgt.at[idx].add(src)

def _segment_sum(src, seg, n):
    return jax.ops.segment_sum(src, seg, n)
kernel_name = 'mk_lm_tower_d2_tok_ids768_r4_de9b9d'

def setup_inputs(seed: int=0):
    np.random.seed(seed)
    _w = jnp.asarray

    def _rec_inputs():
        import jax
        import jax.numpy as jnp
        _rk = jax.random.key(seed)
        x = jax.random.randint(jax.random.fold_in(_rk, 1), (8, 256), 0, 50226, jnp.int32)
        return x
    x = _rec_inputs()

    def _L0_tok_setup():
        import jax, jax.numpy as jnp
        import numpy as np
        VOCAB = 50257
        EMBED = 192
        B, C = (4, 512)
        key = jax.random.key(seed)
        k1, k2 = jax.random.split(key)
        x = jax.random.randint(k1, (B, C), 0, VOCAB)
        embed_matrix = jax.random.normal(k2, (VOCAB, EMBED), dtype=jnp.float32)
        return {'x': x, 'embed_matrix': embed_matrix}
    _L0_tok_all = _L0_tok_setup()
    _L0_tok_in = {k: v for k, v in _L0_tok_all.items() if k in ('embed_matrix',)}
    del _L0_tok_all

    def _L0_attn_setup():
        import math
        import jax, jax.numpy as jnp
        import numpy as np
        B, L, D_MODEL = (2, 512, 192)
        H = 12
        FEAT = 16
        HEAD_DIM = D_MODEL // H

        def taylor_exp(x):
            d = x.shape[-1]
            rd = math.sqrt(d)
            rrd = math.sqrt(rd)
            r2 = math.sqrt(2.0)
            x2 = (x[..., :, None] * x[..., None, :]).reshape(*x.shape[:-1], d * d) / r2
            ones = jnp.ones(x.shape[:-1] + (1,), dtype=x.dtype)
            return jnp.concatenate([ones, x / rrd, x2 / rd], axis=-1)
        key = jax.random.key(seed)
        k1, k2, k3, k4, k5 = jax.random.split(key, 5)
        s = 0.02
        return {'hidden_states': jax.random.normal(k1, (B, L, D_MODEL), jnp.float32), 'Wq': jax.random.normal(k2, (H * FEAT, D_MODEL), jnp.float32) * s, 'Wk': jax.random.normal(k3, (H * FEAT, D_MODEL), jnp.float32) * s, 'Wv': jax.random.normal(k4, (D_MODEL, D_MODEL), jnp.float32) * s, 'Wo': jax.random.normal(k5, (D_MODEL, D_MODEL), jnp.float32) * s}
    _L0_attn_all = _L0_attn_setup()
    _L0_attn_in = {k: v for k, v in _L0_attn_all.items() if k in ('Wq', 'Wk', 'Wv', 'Wo')}
    del _L0_attn_all

    def _L0_ffn_setup():
        import jax, jax.numpy as jnp
        import numpy as np
        B, T, C = (4, 512, 192)
        E, K = (8, 2)

        def _mlp(x, wfc, wproj):
            h = jnp.square(jax.nn.relu(x @ wfc))
            return h @ wproj
        key = jax.random.key(seed)
        ks = jax.random.split(key, 6)
        s = 0.02
        return {'x': jax.random.normal(ks[0], (B, T, C), jnp.float32), 'w_fc_sh': jax.random.normal(ks[1], (C, C), jnp.float32) * s, 'w_proj_sh': jax.random.normal(ks[2], (C, C), jnp.float32) * s, 'w1': jax.random.normal(ks[3], (E, C, C), jnp.float32) * s, 'w2': jax.random.normal(ks[4], (E, C, C), jnp.float32) * s, 'router_w': jax.random.normal(ks[5], (E, C), jnp.float32) * s, 'balance_bias': jnp.zeros((E,), jnp.float32)}
    _L0_ffn_all = _L0_ffn_setup()
    _L0_ffn_in = {k: v for k, v in _L0_ffn_all.items() if k in ('w_fc_sh', 'w_proj_sh', 'w1', 'w2', 'router_w', 'balance_bias')}
    del _L0_ffn_all

    def _L1_attn_setup():
        import jax, jax.numpy as jnp
        from jax import lax
        import numpy as np
        import math
        H = 192
        INNER = 288
        NH = 8
        DH = INNER // NH
        K = 4
        B = 2
        S = 512

        def _multihead_layernorm(h, norm_w, eps=1e-05):
            b, s, d = h.shape
            hh = h.reshape(b, s, NH, DH).astype(jnp.float32)
            mean = hh.mean(axis=-1, keepdims=True)
            var = ((hh - mean) ** 2).mean(axis=-1, keepdims=True)
            hn = (hh - mean) / jnp.sqrt(var + eps)
            return hn.reshape(b, s, d).astype(h.dtype) * norm_w

        def _mlstm_cell(q, k, v, Wi, bi, Wf, bf, norm_w):
            b, s, d = q.shape
            eps = 1e-06
            qkv_cat = jnp.concatenate([q, k, v], axis=-1)
            ig = qkv_cat @ Wi + bi
            fg = qkv_cat @ Wf + bf
            qh = q.reshape(b, s, NH, DH).transpose(0, 2, 1, 3)
            kh = k.reshape(b, s, NH, DH).transpose(0, 2, 1, 3)
            vh = v.reshape(b, s, NH, DH).transpose(0, 2, 1, 3)
            ig = ig.transpose(0, 2, 1)
            fg = fg.transpose(0, 2, 1)
            log_f = jax.nn.log_sigmoid(fg)
            lf_cs = jnp.concatenate([jnp.zeros((b, NH, 1), log_f.dtype), jnp.cumsum(log_f, axis=-1)], axis=-1)
            log_fg_mat = lf_cs[:, :, 1:, None] - lf_cs[:, :, None, 1:]
            ltr = jnp.tril(jnp.ones((s, s), dtype=bool))
            log_fg_mat = jnp.where(ltr, log_fg_mat, -jnp.inf)
            log_D = log_fg_mat + ig[:, :, None, :]
            max_log_D = lax.stop_gradient(jnp.max(log_D, axis=-1, keepdims=True))
            D = jnp.exp(log_D - max_log_D)
            qk = jnp.einsum('bhsd,bhtd->bhst', qh, kh / math.sqrt(DH))
            C = qk * D
            normalizer = jnp.maximum(jnp.abs(C.sum(axis=-1, keepdims=True)), jnp.exp(-max_log_D)) + eps
            h = jnp.einsum('bhst,bhtd->bhsd', C / normalizer, vh)
            h = h.transpose(0, 2, 1, 3).reshape(b, s, d)
            return _multihead_layernorm(h, norm_w)
        key = jax.random.key(seed)
        ks = jax.random.split(key, 12)
        sc = 0.02
        inp = {'x': jax.random.normal(ks[0], (B, S, H), dtype=jnp.float32), 'W_up': jax.random.normal(ks[1], (H, 2 * INNER), dtype=jnp.float32) * sc, 'conv_w': jax.random.normal(ks[2], (INNER, 1, K), dtype=jnp.float32) * sc, 'conv_b': jnp.zeros((INNER,), dtype=jnp.float32), 'Wq': jax.random.normal(ks[3], (INNER, INNER), dtype=jnp.float32) * sc, 'Wk': jax.random.normal(ks[4], (INNER, INNER), dtype=jnp.float32) * sc, 'Wv': jax.random.normal(ks[5], (INNER, INNER), dtype=jnp.float32) * sc, 'Wi': jnp.zeros((3 * INNER, NH), dtype=jnp.float32), 'bi': jax.random.normal(ks[6], (NH,), dtype=jnp.float32) * 0.1, 'Wf': jnp.zeros((3 * INNER, NH), dtype=jnp.float32), 'bf': jnp.linspace(3.0, 6.0, NH, dtype=jnp.float32), 'norm_w': jnp.ones((INNER,), dtype=jnp.float32), 'skip': jnp.ones((), dtype=jnp.float32), 'W_down': jax.random.normal(ks[7], (INNER, H), dtype=jnp.float32) * sc}
        return inp
    _L1_attn_all = _L1_attn_setup()
    _L1_attn_in = {k: v for k, v in _L1_attn_all.items() if k in ('W_up', 'conv_w', 'conv_b', 'Wq', 'Wk', 'Wv', 'Wi', 'bi', 'Wf', 'bf', 'norm_w', 'skip', 'W_down')}
    del _L1_attn_all

    def _L1_ffn_setup():
        import math
        import jax, jax.numpy as jnp
        import numpy as np
        B, L, D = (8, 1024, 192)
        E = 16
        TOP_K = 2
        F_EXP = 4 * D
        F_SH = F_EXP * 2 // 4
        key = jax.random.key(seed)
        ks = jax.random.split(key, 8)
        s = lambda fan_in: 1.0 / math.sqrt(fan_in)
        return {'hidden_states': jax.random.normal(ks[0], (B, L, D), jnp.float32), 'gate_weight': jax.random.uniform(ks[1], (E, D), jnp.float32, -s(D), s(D)), 'Wg': jax.random.uniform(ks[2], (E, F_EXP, D), jnp.float32, -s(D), s(D)), 'Wu': jax.random.uniform(ks[3], (E, F_EXP, D), jnp.float32, -s(D), s(D)), 'Wd': jax.random.uniform(ks[4], (E, D, F_EXP), jnp.float32, -s(F_EXP), s(F_EXP)), 'Ws_g': jax.random.uniform(ks[5], (F_SH, D), jnp.float32, -s(D), s(D)), 'Ws_u': jax.random.uniform(ks[6], (F_SH, D), jnp.float32, -s(D), s(D)), 'Ws_d': jax.random.uniform(ks[7], (D, F_SH), jnp.float32, -s(F_SH), s(F_SH))}
    _L1_ffn_all = _L1_ffn_setup()
    _L1_ffn_in = {k: v for k, v in _L1_ffn_all.items() if k in ('gate_weight', 'Wg', 'Wu', 'Wd', 'Ws_g', 'Ws_u', 'Ws_d')}
    del _L1_ffn_all
    return {'x': x, 'L0_tok_embed_matrix': _L0_tok_in['embed_matrix'], 'L0_attn_Wq': _L0_attn_in['Wq'], 'L0_attn_Wk': _L0_attn_in['Wk'], 'L0_attn_Wv': _L0_attn_in['Wv'], 'L0_attn_Wo': _L0_attn_in['Wo'], 'L0_ffn_w_fc_sh': _L0_ffn_in['w_fc_sh'], 'L0_ffn_w_proj_sh': _L0_ffn_in['w_proj_sh'], 'L0_ffn_w1': _L0_ffn_in['w1'], 'L0_ffn_w2': _L0_ffn_in['w2'], 'L0_ffn_router_w': _L0_ffn_in['router_w'], 'L0_ffn_balance_bias': _L0_ffn_in['balance_bias'], 'L1_attn_W_up': _L1_attn_in['W_up'], 'L1_attn_conv_w': _L1_attn_in['conv_w'], 'L1_attn_conv_b': _L1_attn_in['conv_b'], 'L1_attn_Wq': _L1_attn_in['Wq'], 'L1_attn_Wk': _L1_attn_in['Wk'], 'L1_attn_Wv': _L1_attn_in['Wv'], 'L1_attn_Wi': _L1_attn_in['Wi'], 'L1_attn_bi': _L1_attn_in['bi'], 'L1_attn_Wf': _L1_attn_in['Wf'], 'L1_attn_bf': _L1_attn_in['bf'], 'L1_attn_norm_w': _L1_attn_in['norm_w'], 'L1_attn_skip': _L1_attn_in['skip'], 'L1_attn_W_down': _L1_attn_in['W_down'], 'L1_ffn_gate_weight': _L1_ffn_in['gate_weight'], 'L1_ffn_Wg': _L1_ffn_in['Wg'], 'L1_ffn_Wu': _L1_ffn_in['Wu'], 'L1_ffn_Wd': _L1_ffn_in['Wd'], 'L1_ffn_Ws_g': _L1_ffn_in['Ws_g'], 'L1_ffn_Ws_u': _L1_ffn_in['Ws_u'], 'L1_ffn_Ws_d': _L1_ffn_in['Ws_d']}

def reference(x, L0_tok_embed_matrix, L0_attn_Wq, L0_attn_Wk, L0_attn_Wv, L0_attn_Wo, L0_ffn_w_fc_sh, L0_ffn_w_proj_sh, L0_ffn_w1, L0_ffn_w2, L0_ffn_router_w, L0_ffn_balance_bias, L1_attn_W_up, L1_attn_conv_w, L1_attn_conv_b, L1_attn_Wq, L1_attn_Wk, L1_attn_Wv, L1_attn_Wi, L1_attn_bi, L1_attn_Wf, L1_attn_bf, L1_attn_norm_w, L1_attn_skip, L1_attn_W_down, L1_ffn_gate_weight, L1_ffn_Wg, L1_ffn_Wu, L1_ffn_Wd, L1_ffn_Ws_g, L1_ffn_Ws_u, L1_ffn_Ws_d):
    import jax
    import jax.numpy as jnp

    def _L0_tok_ref(x, embed_matrix):
        import jax, jax.numpy as jnp
        import numpy as np
        VOCAB = 50257
        EMBED = 192
        B, C = (4, 512)
        return jnp.take(embed_matrix, x, axis=0)

    def _L0_attn_ref(hidden_states, Wq, Wk, Wv, Wo):
        import math
        import jax, jax.numpy as jnp
        import numpy as np
        B, L, D_MODEL = (2, 512, 192)
        H = 12
        FEAT = 16
        HEAD_DIM = D_MODEL // H

        def taylor_exp(x):
            d = x.shape[-1]
            rd = math.sqrt(d)
            rrd = math.sqrt(rd)
            r2 = math.sqrt(2.0)
            x2 = (x[..., :, None] * x[..., None, :]).reshape(*x.shape[:-1], d * d) / r2
            ones = jnp.ones(x.shape[:-1] + (1,), dtype=x.dtype)
            return jnp.concatenate([ones, x / rrd, x2 / rd], axis=-1)
        b, l, d = hidden_states.shape
        q = jnp.einsum('bld,fd->blf', hidden_states, Wq).reshape(b, l, H, FEAT).transpose(0, 2, 1, 3)
        k = jnp.einsum('bld,fd->blf', hidden_states, Wk).reshape(b, l, H, FEAT).transpose(0, 2, 1, 3)
        v = jnp.einsum('bld,fd->blf', hidden_states, Wv).reshape(b, l, H, HEAD_DIM).transpose(0, 2, 1, 3)
        q = taylor_exp(q)
        k = taylor_exp(k)
        k_state = jnp.sum(k, axis=2, keepdims=True) + jnp.cumsum(k, axis=2)
        z = 1.0 / jnp.sum(q * k_state, axis=-1)
        A = jnp.einsum('bhnd,bhmd->bhnm', q, k)
        causal = jnp.tril(jnp.ones((l, l), dtype=A.dtype))
        A_total = A * causal + A
        y = jnp.einsum('bhnm,bhme->bhne', A_total, v) * z[..., None]
        out = y.transpose(0, 2, 1, 3).reshape(b, l, H * HEAD_DIM)
        return jnp.einsum('blf,df->bld', out, Wo)

    def _L0_ffn_ref(x, w_fc_sh, w_proj_sh, w1, w2, router_w, balance_bias):
        import jax, jax.numpy as jnp
        import numpy as np
        B, T, C = (4, 512, 192)
        E, K = (8, 2)

        def _mlp(x, wfc, wproj):
            h = jnp.square(jax.nn.relu(x @ wfc))
            return h @ wproj
        Bx, Tx, Cx = x.shape
        shared = _mlp(x, w_fc_sh, w_proj_sh)
        xf = x.reshape(-1, Cx)
        logits = xf.astype(jnp.float32) @ router_w.T
        scores = jax.nn.sigmoid(logits)
        _, idx = jax.lax.top_k(scores + balance_bias, K)
        tw = jnp.take_along_axis(scores, idx, axis=-1)
        tw = tw / (tw.sum(-1, keepdims=True) + 1e-20)
        combine = (jax.nn.one_hot(idx, E, dtype=tw.dtype) * tw[..., None]).sum(1)
        h = jnp.square(jax.nn.relu(jnp.einsum('nc,ech->neh', xf, w1)))
        y = jnp.einsum('neh,ehc->nec', h, w2)
        routed = jnp.einsum('nec,ne->nc', y, combine)
        return shared + routed.reshape(Bx, Tx, Cx)

    def _L1_attn_ref(x, W_up, conv_w, conv_b, Wq, Wk, Wv, Wi, bi, Wf, bf, norm_w, skip, W_down):
        import jax, jax.numpy as jnp
        from jax import lax
        import numpy as np
        import math
        H = 192
        INNER = 288
        NH = 8
        DH = INNER // NH
        K = 4
        B = 2
        S = 512

        def _multihead_layernorm(h, norm_w, eps=1e-05):
            b, s, d = h.shape
            hh = h.reshape(b, s, NH, DH).astype(jnp.float32)
            mean = hh.mean(axis=-1, keepdims=True)
            var = ((hh - mean) ** 2).mean(axis=-1, keepdims=True)
            hn = (hh - mean) / jnp.sqrt(var + eps)
            return hn.reshape(b, s, d).astype(h.dtype) * norm_w

        def _mlstm_cell(q, k, v, Wi, bi, Wf, bf, norm_w):
            b, s, d = q.shape
            eps = 1e-06
            qkv_cat = jnp.concatenate([q, k, v], axis=-1)
            ig = qkv_cat @ Wi + bi
            fg = qkv_cat @ Wf + bf
            qh = q.reshape(b, s, NH, DH).transpose(0, 2, 1, 3)
            kh = k.reshape(b, s, NH, DH).transpose(0, 2, 1, 3)
            vh = v.reshape(b, s, NH, DH).transpose(0, 2, 1, 3)
            ig = ig.transpose(0, 2, 1)
            fg = fg.transpose(0, 2, 1)
            log_f = jax.nn.log_sigmoid(fg)
            lf_cs = jnp.concatenate([jnp.zeros((b, NH, 1), log_f.dtype), jnp.cumsum(log_f, axis=-1)], axis=-1)
            log_fg_mat = lf_cs[:, :, 1:, None] - lf_cs[:, :, None, 1:]
            ltr = jnp.tril(jnp.ones((s, s), dtype=bool))
            log_fg_mat = jnp.where(ltr, log_fg_mat, -jnp.inf)
            log_D = log_fg_mat + ig[:, :, None, :]
            max_log_D = lax.stop_gradient(jnp.max(log_D, axis=-1, keepdims=True))
            D = jnp.exp(log_D - max_log_D)
            qk = jnp.einsum('bhsd,bhtd->bhst', qh, kh / math.sqrt(DH))
            C = qk * D
            normalizer = jnp.maximum(jnp.abs(C.sum(axis=-1, keepdims=True)), jnp.exp(-max_log_D)) + eps
            h = jnp.einsum('bhst,bhtd->bhsd', C / normalizer, vh)
            h = h.transpose(0, 2, 1, 3).reshape(b, s, d)
            return _multihead_layernorm(h, norm_w)
        xz = x @ W_up
        x_mlstm, z = jnp.split(xz, 2, axis=-1)
        xc = x_mlstm.transpose(0, 2, 1)
        xc = jnp.pad(xc, ((0, 0), (0, 0), (K - 1, 0)))
        xc = lax.conv_general_dilated(xc, conv_w, (1,), 'VALID', dimension_numbers=('NCW', 'OIW', 'NCW'), feature_group_count=INNER)
        xc = (xc + conv_b[None, :, None]).transpose(0, 2, 1)
        x_conv = jax.nn.silu(xc)
        q = x_conv @ Wq
        k = x_conv @ Wk
        v = x_mlstm @ Wv
        h = _mlstm_cell(q, k, v, Wi, bi, Wf, bf, norm_w)
        h = h + skip * x_conv
        h = h * jax.nn.silu(z)
        return h @ W_down

    def _L1_ffn_ref(hidden_states, gate_weight, Wg, Wu, Wd, Ws_g, Ws_u, Ws_d):
        import math
        import jax, jax.numpy as jnp
        import numpy as np
        B, L, D = (8, 1024, 192)
        E = 16
        TOP_K = 2
        F_EXP = 4 * D
        F_SH = F_EXP * 2 // 4
        b, l, d = hidden_states.shape
        n = b * l
        x = hidden_states.reshape(n, d)
        scores = jax.nn.sigmoid(x @ gate_weight.T)
        capacity = math.ceil(n / E * TOP_K)
        topk_score, topk_ids = jax.lax.top_k(scores.T, capacity)
        xg = x[topk_ids]
        gate = jax.nn.silu(jnp.einsum('ecd,efd->ecf', xg, Wg))
        up = jnp.einsum('ecd,efd->ecf', xg, Wu)
        out = jnp.einsum('ecf,edf->ecd', gate * up, Wd)
        out = out * topk_score[..., None]
        y = jnp.zeros((n, d), x.dtype).at[topk_ids.reshape(-1)].add(out.reshape(-1, d))
        y = y.reshape(b, l, d)
        shared = jax.nn.silu(hidden_states @ Ws_g.T) * (hidden_states @ Ws_u.T) @ Ws_d.T
        return y + shared
    h = _L0_tok_ref(x, L0_tok_embed_matrix)
    h = h + _L0_attn_ref(_layernorm(h, axis=-1), L0_attn_Wq, L0_attn_Wk, L0_attn_Wv, L0_attn_Wo)
    h = h + _L0_ffn_ref(_layernorm(h, axis=-1), L0_ffn_w_fc_sh, L0_ffn_w_proj_sh, L0_ffn_w1, L0_ffn_w2, L0_ffn_router_w, L0_ffn_balance_bias)
    h = h + _L1_attn_ref(_layernorm(h, axis=-1), L1_attn_W_up, L1_attn_conv_w, L1_attn_conv_b, L1_attn_Wq, L1_attn_Wk, L1_attn_Wv, L1_attn_Wi, L1_attn_bi, L1_attn_Wf, L1_attn_bf, L1_attn_norm_w, L1_attn_skip, L1_attn_W_down)
    h = h + _L1_ffn_ref(_layernorm(h, axis=-1), L1_ffn_gate_weight, L1_ffn_Wg, L1_ffn_Wu, L1_ffn_Wd, L1_ffn_Ws_g, L1_ffn_Ws_u, L1_ffn_Ws_d)
    return h

_drawn_inputs = setup_inputs


def setup_inputs(seed=0):
    import zlib

    import numpy as np

    out = dict(_drawn_inputs(seed))
    spreads = {'L0_ffn_balance_bias': (0.0, 0.326),
     'L1_attn_conv_b': (0.0, 0.8),
     'L1_attn_Wi': (0.0, 0.8),
     'L1_attn_Wf': (0.0, 0.8),
     'L1_attn_norm_w': (1.0, 0.6)}
    factors = {'L0_attn_Wq': 8.0,
     'L0_attn_Wk': 8.0,
     'L0_attn_Wv': 6.345,
     'L0_attn_Wo': 6.144,
     'L0_ffn_w1': 2.725,
     'L0_ffn_router_w': 3.688,
     'L1_attn_W_up': 8.0,
     'L1_attn_conv_w': 8.0,
     'L1_attn_Wq': 8.0,
     'L1_attn_Wk': 8.0,
     'L1_attn_Wv': 8.0,
     'L1_attn_bi': 26.347,
     'L1_attn_bf': 8.0,
     'L1_attn_W_down': 8.0,
     'L1_ffn_gate_weight': 3.385,
     'L1_ffn_Wg': 3.273,
     'L1_ffn_Wu': 3.184,
     'L1_ffn_Wd': 3.175,
     'L1_ffn_Ws_g': 3.334,
     'L1_ffn_Ws_u': 3.226,
     'L1_ffn_Ws_d': 3.247}
    for name, (base, spread) in spreads.items():
        noise = np.random.default_rng([zlib.crc32(name.encode()), seed]).standard_normal(out[name].shape)
        drawn = base * np.exp(spread * noise) if base else spread * noise
        out[name] = jnp.asarray(drawn.astype(out[name].dtype))
    for name, factor in factors.items():
        out[name] = (out[name] * factor).astype(out[name].dtype)
    return out
```

```python
from contextlib import ExitStack

import concourse.bass as bass
from concourse import mybir

ALU = mybir.AluOpType
ACT = mybir.ActivationFunctionType
AX_X = mybir.AxisListType.X
F32 = mybir.dt.float32
BF16 = mybir.dt.bfloat16
F16 = mybir.dt.float16
I32 = mybir.dt.int32

P = 128
B, T = 8, 256
N = B * T
NT = N // P
TT = T // P
D = 192
C = 96
KD = D // C
LN_EPS = 1e-5

AH, AF = 12, 16
AHC = C // AF
AOUT = C + AHC
ASTEP = AOUT + AF

E0 = 8
E0A = E0 + 1

INNER, MH, MD = 288, 8, 36
KI = INNER // C
MG, MGH = 3, 3
GR = MGH * MD
MOUT = GR + MGH
MSTEP = MOUT + MD
CONV_K = 4
GATE_W = 40
TRI = T + P

E1, F1, FS = 16, 768, 384
CAP = 256
KF, KS = F1 // P, FS // P
XROW = D + E1
ROUNDS = 15


def over(eng, sem, value):
    assert isinstance(value, int) or value.min_val >= 0
    if not isinstance(value, int) or value > 0:
        eng.wait_ge(sem, value)


def pass_gate(eng, m):
    eng.sem_inc(m.gate, 1)


class Steps:

    def __init__(self, eng, sem, per, b):
        self.eng, self.sem, self.per, self.b, self.n = eng, sem, per, b, 0

    def mark(self, ins):
        ins.then_inc(self.sem, 1)
        self.n += 1
        assert self.n <= self.per
        return self.n

    def wait(self, k=None):
        self.eng.wait_ge(self.sem, self.b * self.per + (self.n if k is None else k))

    def end(self):
        assert self.n == self.per, (self.n, self.per)


def pipeline(eng, front, main, back, n=B):
    front(0, 0)
    main(0, 0, (1, 1), None)
    main(1, 1, (2, 0), (0, 0))
    with eng.Fori(1, n // 2 - 1) as j:
        main(j * 2, 0, (j * 2 + 1, 1), (j * 2 - 1, 1))
        main(j * 2 + 1, 1, (j * 2 + 2, 0), (j * 2, 0))
    main(n - 2, 0, (n - 1, 1), (n - 3, 1))
    main(n - 1, 1, None, (n - 2, 0))
    back(n - 1, 1)


def pipeline_ahead(eng, early, late, main, back):
    early(0, 0)
    late(0, 0, (1, 1))
    main(0, 0, (1, 1), (2, 0), None)
    main(1, 1, (2, 0), (3, 1), (0, 0))
    with eng.Fori(1, B // 2 - 1) as j:
        main(j * 2, 0, (j * 2 + 1, 1), (j * 2 + 2, 0), (j * 2 - 1, 1))
        main(j * 2 + 1, 1, (j * 2 + 2, 0), (j * 2 + 3, 1), (j * 2, 0))
    main(B - 2, 0, (B - 1, 1), None, (B - 3, 1))
    main(B - 1, 1, None, None, (B - 2, 0))
    back(B - 1, 1)


def tiles(h, b):
    if isinstance(b, int):
        return h[:, TT * b:TT * b + TT, :]
    return h[:, bass.ds(b * TT, TT), :]


class Norm:

    def __init__(self, m, stage):
        self.m = m
        sem = m.sem
        self.root_in = sem(f"s{stage}_variance_ready")
        self.root = sem(f"s{stage}_rstd_ready")
        self.xn = sem(f"s{stage}_xn_ready")
        self.turned = sem(f"s{stage}_xn_turned")
        self.xt_ready = sem(f"s{stage}_xt_ready")
        self.stats_steps = sem(f"s{stage}_norm_stats_steps")
        self.apply_steps = sem(f"s{stage}_norm_apply_steps")

    def dve_stats(self, dve, b, s):
        m = self.m
        st = Steps(dve, self.stats_steps, 2 * TT, b)
        h = tiles(m.h, b)
        for t in range(TT):
            st.mark(dve.bn_stats(m.stats[:, s, t, :], h[:, t, :]))
        for t in range(TT):
            st.wait(t + 1)
            pass_gate(dve, m)
            st.mark(dve.bn_aggr(m.moments[:, s, t, :], m.stats[:, s, t, :]))
        st.end()
        st.wait()
        dve.tensor_scalar(m.vareps[:, s, :], m.moments[:, s, :, 1], LN_EPS, None, ALU.add).then_inc(self.root_in, 1)

    def dve_apply(self, dve, b, s):
        m = self.m
        st = Steps(dve, self.apply_steps, TT, b)
        h = tiles(m.h, b)
        dve.wait_ge(self.root, b + 1)
        over(dve, self.turned, b - 1)
        for t in range(TT):
            st.mark(dve.tensor_scalar(m.xn[:, s, t, :], h[:, t, :], m.moments[:, s, t, 0:1], m.rstd[:, s, t:t + 1],
                                      ALU.subtract, ALU.mult))
        st.end()
        st.wait()
        dve.sem_inc(self.xn, 1)

    def dve(self, dve, b, s):
        self.dve_stats(dve, b, s)
        self.dve_apply(dve, b, s)

    def pool(self, pool, b, s):
        m = self.m
        pool.wait_ge(self.root_in, b + 1)
        pool.tensor_tensor(m.rstd[:, s, :], m.vareps[:, s, :], m.neg_half[:, 0:TT], ALU.pow).then_inc(self.root, 1)

    def pe(self, pe, b, s, bank):
        m = self.m
        pe.wait_ge(self.xn, b + 1)
        out = bank[0:C, :].rearrange("p (k n) -> p k n", k=KD)
        for t in range(TT):
            for k in range(KD):
                last = pe.transpose(out[:, k, t * P:(t + 1) * P], m.xn[:, s, t, k * C:(k + 1) * C], m.ident[:, :])
        last.then_inc(self.turned, 1)

    def act(self, act, b, s, bank, xt):
        act.wait_ge(self.turned, b + 1)
        act.activation(xt, bank[0:C, :].rearrange("p (k n) -> p k n", k=KD), ACT.Copy).then_inc(self.xt_ready, 1)


class Memory:

    def __init__(self, nc, ctx):
        self.nc, self.ctx, self.stage_sems = nc, ctx, []

    def lasting_sem(self, name):
        return self.ctx.enter_context(self.nc.semaphore(name))

    def sem(self, name):
        self.stage_sems.append(self.nc.alloc_semaphore(name))
        return self.stage_sems[-1]

    def end_stage(self):
        self.nc.clear_and_free_semaphores(self.stage_sems)
        self.nc.all_engine_barrier()
        self.stage_sems = []

    def sb(self, name, shape, dt=F32):
        return self.ctx.enter_context(self.nc.sbuf_tensor(name, shape, dt))


def taylor_attention(nc, m, w, a):
    sem = m.sem
    with ExitStack() as ctx:
        def sb(name, shape, dt=F32):
            return ctx.enter_context(nc.sbuf_tensor("ta_" + name, shape, dt))

        qT = sb("qT", [C, 2, KD, T])
        kT = sb("kT", [C, 2, KD, T])
        qm = sb("qm", [C, 2, AH, T])
        VW = AH * AOUT + AHC * AF + AF
        v_diag = sb("v_diag", [P, 2, TT, VW])
        sq = sb("sq", [P, 3, TT, T])
        o_sb = sb("o_sb", [P, 2, KD, T])
        rz = sb("rz", [P, 2, KD, T])
        o_norm = sb("o_norm", [C, 2, KD, T])
        turn, pq, pk, pv, ps0, ps1, po0, po1 = m.banks
        pscore, pout = (ps0, ps1), (po0, po1)

        norm = Norm(m, 1)
        qk_proj = sem("ta_qk_projected")
        v_proj = sem("ta_v_projected")
        q_copied = sem("ta_q_copied")
        k_copied = sem("ta_k_copied")
        q_masked = sem("ta_q_masked")
        v_spread = sem("ta_v_spread")
        v_clear = sem("ta_v_diag_cleared")
        scored = sem("ta_scored")
        squared = sem("ta_squared")
        weighted = sem("ta_weighted")
        summed = sem("ta_summed")
        o_copied = sem("ta_o_copied")
        z_inv = sem("ta_sums_inverted")
        z_bcast = sem("ta_sums_broadcast")
        o_normed = sem("ta_o_normed")
        projected = sem("ta_projected")
        h_added = sem("ta_h_added")

        def diag(tile, c, off, width):
            at = c * AHC * AOUT + off
            step = ASTEP if width == AF else AOUT + 1
            return tile[:, at:at + AHC * step].rearrange("p (i w) -> p i w", w=step)[:, :, 0:width]

        with nc.Block() as block:
            @block.sync
            def _(sp):
                for stage in range(4):
                    for dst, src in m.loads[stage]:
                        sp.dma_start(dst, src).then_inc(m.loaded[stage], 16)

            @block.gpsimd
            def _(pool):
                m.wait_load(pool, 0)
                for t in range(NT):
                    pool.indirect_dma_start(m.h[:, t, :], None, a["embed"][:, :],
                                            bass.IndirectOffsetOnAxis(ap=m.ids[:, t:t + 1], axis=0)).then_inc(m.gathers[t], 16)
                pool.wait_ge(v_clear, 1)
                for t in range(TT):
                    pool.wait_ge(m.gathers[t], 16)
                pool.sem_inc(m.gathered, 1)
                norm.pool(pool, 0, 0)
                for t in range(TT, NT):
                    pool.wait_ge(m.gathers[t], 16)
                pool.sem_inc(m.gathered, 1)
                m.wait_load(pool, 1)

                def front(b, s):
                    if not isinstance(b, int) or b > 0:
                        norm.pool(pool, b, s)
                    pool.wait_ge(q_copied, b + 1)
                    over(pool, scored, AH * (b - 1))
                    pass_gate(pool, m)
                    for hd in range(AH):
                        ins = pool.tensor_scalar(qm[:, s, hd, :], qT[:, s, hd // AHC, :],
                                                 m.head_mask[:, hd % AHC:hd % AHC + 1], 1.0, ALU.mult, ALU.mult)
                        if hd % AHC == AHC - 1:
                            ins.then_inc(q_masked, 1)

                def main(b, s, nxt, prev):
                    if nxt:
                        front(*nxt)

                pipeline(pool, front, main, lambda b, s: None)

            @block.tensor
            def _(pe):
                m.wait_load(pe, 1)

                def turn_in(b, s):
                    over(pe, o_normed, 2 * (b - 1))
                    norm.pe(pe, b, s, turn)

                def project(b, s):
                    pe.wait_ge(norm.xt_ready, b + 1)
                    over(pe, q_copied, b)
                    for bank, wt in ((pq, m.wqT), (pk, m.wkT)):
                        if bank is pk:
                            over(pe, k_copied, b)
                        for c in range(KD):
                            for k in range(KD):
                                last = pe.matmul(bank[0:C, c * T:(c + 1) * T], wt[:, k, c * C:(c + 1) * C],
                                                 m.xt[:, s, k, :], start=(k == 0), stop=(k == KD - 1))
                        last.then_inc(qk_proj, 1)
                    over(pe, v_spread, b)
                    over(pe, h_added, b - 1)
                    for t in range(TT):
                        for k in range(KD):
                            last = pe.matmul(pv[:, t * D:(t + 1) * D], m.xt[:, s, k, t * P:(t + 1) * P],
                                             m.wvT[:, k, :], start=(k == 0), stop=(k == KD - 1))
                    last.then_inc(v_proj, 1)

                def broadcast_sums(b, s):
                    pe.wait_ge(z_inv, b + 1)
                    over(pe, norm.xt_ready, b + 2 if not isinstance(b, int) or b < B - 1 else B)
                    for c in range(KD):
                        last = pe.matmul(turn[0:C, c * T:(c + 1) * T], m.sum_rows[C:AOUT, :], rz[C:AOUT, s, c, :],
                                         start=True, stop=True)
                    last.then_inc(z_bcast, 1)

                def out_project(b, s):
                    pe.wait_ge(o_normed, 2 * b + 2)
                    over(pe, v_spread, b + 2 if not isinstance(b, int) or b < B - 1 else B)
                    for t in range(TT):
                        for c in range(KD):
                            last = pe.matmul(pv[:, t * D:(t + 1) * D], o_norm[:, s, c, t * P:(t + 1) * P],
                                             m.woT[:, c, :], start=(c == 0), stop=(c == KD - 1))
                    last.then_inc(projected, 1)

                def front(b, s):
                    turn_in(b, s)
                    project(b, s)

                def back(b, s):
                    broadcast_sums(b, s)
                    out_project(b, s)

                def score(b, s, hd):
                    n = AH * b + hd
                    over(pe, squared, n - 1)
                    for t in range(TT):
                        last = pe.matmul(pscore[hd % 2][:, t * T:(t + 1) * T],
                                         kT[:, s, hd // AHC, t * P:(t + 1) * P], qm[:, s, hd, :],
                                         start=True, stop=True)
                    last.then_inc(scored, 1)

                def attend(b, s, hd):
                    c = hd // AHC
                    pe.wait_ge(weighted, AH * b + hd + 1)
                    if hd % AHC == 0:
                        over(pe, o_copied, 2 * b - 1 + c)
                    for t in range(TT):
                        last = pe.matmul(pout[c][0:AOUT, 0:T], v_diag[:, s, t, hd * AOUT:(hd + 1) * AOUT],
                                         sq[:, hd % 3, t, :], start=(hd % AHC == 0 and t == 0),
                                         stop=(hd % AHC == AHC - 1 and t == TT - 1))
                    last.then_inc(summed, 1)

                def main(b, s, nxt, prev):
                    for hd in range(AH):
                        if hd % AHC == 0:
                            pe.wait_ge(q_masked, 2 * b + hd // AHC + 1)
                        if hd == 0:
                            pe.wait_ge(k_copied, b + 1)
                            pe.wait_ge(v_spread, b + 1)
                            pe.wait_ge(v_clear, 2 + 2 * TT * KD)
                        score(b, s, hd)
                        if hd >= 2:
                            attend(b, s, hd - 2)
                        if hd == 3 and prev:
                            broadcast_sums(*prev)
                        if hd == 5 and prev:
                            out_project(*prev)
                        if hd == 6 and nxt:
                            turn_in(*nxt)
                        if hd == 8 and nxt:
                            project(*nxt)
                    attend(b, s, AH - 2)
                    attend(b, s, AH - 1)

                pipeline(pe, front, main, back)

            @block.scalar
            def _(act):
                def copy_xt(b, s):
                    over(act, v_proj, b - 1)
                    norm.act(act, b, s, turn, m.xt[:, s, :, :])

                def copy_qk(b, s):
                    over(act, q_masked, 2 * (b - 1))
                    act.wait_ge(qk_proj, 2 * b + 1)
                    act.activation(qT[:, s, :, :], pq[0:C, :].rearrange("p (c n) -> p c n", c=KD),
                                   ACT.Copy).then_inc(q_copied, 1)
                    act.wait_ge(qk_proj, 2 * b + 2)
                    over(act, scored, AH * (b - 1))
                    act.activation(kT[:, s, :, :], pk[0:C, :].rearrange("p (c n) -> p c n", c=KD),
                                   ACT.Copy).then_inc(k_copied, 1)

                def copy_out(b, s, c):
                    act.wait_ge(summed, AH * b + AHC * (c + 1))
                    over(act, o_normed, 2 * (b - 1))
                    act.activation(o_sb[0:AOUT, s, c, :], pout[c][0:AOUT, 0:T], ACT.Copy).then_inc(o_copied, 1)

                def front(b, s):
                    copy_xt(b, s)
                    copy_qk(b, s)

                def square(b, s, hd):
                    n = AH * b + hd
                    act.wait_ge(scored, n + 1)
                    over(act, summed, n - 2)
                    act.activation(sq[:, hd % 3, :, :], pscore[hd % 2][:, :].rearrange("p (t n) -> p t n", t=TT),
                                   ACT.Square, bias=1.0, scale=0.25).then_inc(squared, 1)

                def main(b, s, nxt, prev):
                    for hd in range(AH):
                        square(b, s, hd)
                        if hd == 8:
                            copy_out(b, s, 0)
                        if hd == 6 and nxt:
                            copy_xt(*nxt)
                        if hd == 10 and nxt:
                            copy_qk(*nxt)
                    copy_out(b, s, 1)

                pipeline(act, front, main, lambda b, s: None)

            @block.vector
            def _(dve):
                dve.memset(m.neg_half[:, :], -0.5).then_inc(v_clear, 1)
                dve.memset(v_diag[:, :, :, :], 0.0).then_inc(v_clear, 1)
                dve.wait_ge(v_clear, 2)
                for s in range(2):
                    for t in range(TT):
                        for c in range(KD):
                            dve.memset(diag(v_diag[:, s, t, :], c, C, 1), 1.0).then_inc(v_clear, 1)
                dve.wait_ge(m.gathered, 1)

                def spread(b, s):
                    dve.wait_ge(v_clear, 2 + 2 * TT * KD)
                    dve.wait_ge(v_proj, b + 1)
                    over(dve, summed, AH * (b - 1))
                    for t in range(TT):
                        for c in range(KD):
                            at = t * D + c * C
                            ins = dve.tensor_copy(diag(v_diag[:, s, t, :], c, 0, AF),
                                                  pv[:, at:at + C].rearrange("p (i w) -> p i w", w=AF))
                    ins.then_inc(v_spread, 1)

                def invert(b, s):
                    dve.wait_ge(o_copied, 2 * b + 2)
                    over(dve, z_bcast, b - 1)
                    dve.reciprocal(rz[C:AOUT, s, :, :], o_sb[C:AOUT, s, :, :]).then_inc(z_inv, 1)

                def normalise(b, s):
                    dve.wait_ge(z_bcast, b + 1)
                    over(dve, projected, b - 1)
                    for c in range(KD):
                        dve.tensor_tensor(o_norm[:, s, c, :], o_sb[0:C, s, c, :], turn[0:C, c * T:(c + 1) * T],
                                          ALU.mult).then_inc(o_normed, 1)

                def add(b, s):
                    dve.wait_ge(projected, b + 1)
                    h = tiles(m.h, b)
                    dve.tensor_tensor(h, h, pv[:, 0:TT * D].rearrange("p (t n) -> p t n", t=TT),
                                      ALU.add).then_inc(h_added, 1)

                def front(b, s):
                    norm.dve(dve, b, s)
                    m.wait_load(dve, 1)
                    spread(b, s)
                    dve.wait_ge(m.gathered, 2)

                def back(b, s):
                    invert(b, s)
                    normalise(b, s)
                    add(b, s)

                def main(b, s, nxt, prev):
                    for hd in range(AH):
                        n = AH * b + hd
                        dve.wait_ge(squared, n + 1)
                        dve.scalar_tensor_tensor(out=sq[:, hd % 3, :, :], in0=sq[:, hd % 3, :, :], scalar=1.0,
                                                 in1=m.causal[:, :, :], op0=ALU.add, op1=ALU.mult).then_inc(weighted, 1)
                        if hd == 0 and prev:
                            invert(*prev)
                        if hd == 3 and prev:
                            normalise(*prev)
                        if hd == 3 and nxt:
                            norm.dve_stats(dve, *nxt)
                        if hd == 4 and nxt:
                            norm.dve_apply(dve, *nxt)
                        if hd == 5 and prev:
                            add(*prev)
                        if hd == 9 and nxt:
                            spread(*nxt)

                pipeline(dve, front, main, back)


def wide(ap, axis, n):
    u = ap.unsqueeze(axis)
    shape = list(u.shape)
    shape[axis] = n
    return u.broadcast_to(shape)


def shared_and_routed_experts(nc, m):
    sem = m.sem
    with ExitStack() as ctx:
        def sb(name, shape, dt=F32):
            return ctx.enter_context(nc.sbuf_tensor("re_" + name, shape, dt))

        relu = sb("relu", [C, 2, KD, T])
        hid = sb("hid", [C, 2, KD, T])
        expn = sb("expn", [P, 2, TT, E0])
        score = sb("score", [P, 2, TT, E0])
        biased = sb("biased", [P, 2, TT, E0])
        found = sb("found", [P, 2, TT, E0])
        cand = sb("cand", [P, 2, TT, E0])
        pick1 = sb("pick1", [P, 2, TT, E0])
        pick2 = sb("pick2", [P, 2, TT, E0])
        best = sb("best", [P, 2, TT])
        total = sb("total", [P, 2, TT])
        comb = sb("comb", [P, 2, TT, E0])
        turn, plog, pf0, pf1, py0, py1 = m.banks[0:6]
        pfc, pproj = (pf0, pf1), (py0, py1)

        norm = Norm(m, 2)
        logits = sem("re_logits_ready")
        exped = sem("re_exp_ready")
        route_steps = sem("re_route_steps")
        fc_done = sem("re_fc_done")
        relu_done = sem("re_relu_done")
        hid_done = sem("re_hid_done")
        proj_done = sem("re_proj_done")
        combined = sem("re_combined")
        ORDER = [E0] + list(range(E0))
        ROUTE = 20
        PER = 1 + TT * E0

        with nc.Block() as block:
            @block.gpsimd
            def _(pool):
                def front(b, s):
                    norm.pool(pool, b, s)

                def main(b, s, nxt, prev):
                    if nxt:
                        front(*nxt)

                pipeline(pool, front, main, lambda b, s: None)

            @block.tensor
            def _(pe):
                m.wait_load(pe, 2)

                def turn_in(b, s):
                    over(pe, norm.xt_ready, b)
                    norm.pe(pe, b, s, turn)

                def route(b, s):
                    pe.wait_ge(norm.xt_ready, b + 1)
                    over(pe, exped, b)
                    for t in range(TT):
                        for k in range(KD):
                            last = pe.matmul(plog[:, t * E0:(t + 1) * E0], m.xt[:, s, k, t * P:(t + 1) * P],
                                             m.wrT[:, k, :], start=(k == 0), stop=(k == KD - 1))
                    last.then_inc(logits, 1)

                def front(b, s):
                    turn_in(b, s)
                    route(b, s)

                def fc(b, s, i):
                    n = E0A * b + i
                    over(pe, relu_done, n - 1)
                    for c in range(KD):
                        for k in range(KD):
                            at = ORDER[i] * D + c * C
                            last = pe.matmul(pfc[i % 2][0:C, c * T:(c + 1) * T], m.w1[:, k, at:at + C],
                                             m.xt[:, s, k, :], start=(k == 0), stop=(k == KD - 1))
                    last.then_inc(fc_done, 1)

                def proj(b, s, i):
                    pe.wait_ge(hid_done, E0A * b + i + 1)
                    over(pe, combined, PER * b + (1 + TT * (i - 2)) if i >= 2 else PER * (b - 1) + 1 + TT * (E0A + i - 3))
                    for t in range(TT):
                        for c in range(KD):
                            last = pe.matmul(pproj[i % 2][:, t * D:(t + 1) * D], hid[:, i % 2, c, t * P:(t + 1) * P],
                                             m.w2[:, ORDER[i], c, :], start=(c == 0), stop=(c == KD - 1))
                    last.then_inc(proj_done, 1)

                def main(b, s, nxt, prev):
                    for i in range(E0A):
                        fc(b, s, i)
                        if i >= 1:
                            proj(b, s, i - 1)
                        if i == 3 and nxt:
                            turn_in(*nxt)
                        if i == 5 and nxt:
                            route(*nxt)
                    proj(b, s, E0A - 1)

                pipeline(pe, front, main, lambda b, s: None)

            @block.scalar
            def _(act):
                def copy_xt(b, s):
                    over(act, fc_done, E0A * (b - 1))
                    norm.act(act, b, s, turn, m.xt[:, s, :, :])

                def exp_logits(b, s):
                    act.wait_ge(logits, b + 1)
                    over(act, route_steps, ROUTE * (b - 1))
                    act.activation(expn[:, s, :, :], plog[:, 0:TT * E0].rearrange("p (t e) -> p t e", t=TT),
                                   ACT.Exp, scale=-1.0).then_inc(exped, 1)

                def front(b, s):
                    copy_xt(b, s)
                    exp_logits(b, s)

                def main(b, s, nxt, prev):
                    for i in range(E0A):
                        n = E0A * b + i
                        act.wait_ge(fc_done, n + 1)
                        over(act, hid_done, n - 1)
                        act.activation(relu[:, i % 2, :, :], pfc[i % 2][0:C, :].rearrange("p (c n) -> p c n", c=KD),
                                       ACT.Relu).then_inc(relu_done, 1)
                        if i == 4 and nxt:
                            copy_xt(*nxt)
                        if i == 6 and nxt:
                            exp_logits(*nxt)

                pipeline(act, front, main, lambda b, s: None)

            @block.vector
            def _(dve):
                m.wait_load(dve, 2)

                def pick(st, src, out, s):
                    st.mark(dve.tensor_reduce(best[:, s, :], src, AX_X, ALU.max))
                    st.wait()
                    st.mark(dve.tensor_tensor(found[:, s, :, :], src, wide(best[:, s, :], 2, E0), ALU.is_equal))
                    st.wait()
                    st.mark(dve.tensor_tensor(cand[:, s, :, :], found[:, s, :, :], m.rank8[:, :, :], ALU.mult))
                    st.wait()
                    st.mark(dve.tensor_reduce(best[:, s, :], cand[:, s, :, :], AX_X, ALU.max))
                    st.wait()
                    st.mark(dve.tensor_tensor(out, cand[:, s, :, :], wide(best[:, s, :], 2, E0), ALU.is_equal))
                    st.wait()

                def route(b, s):
                    dve.wait_ge(exped, b + 1)
                    st = Steps(dve, route_steps, ROUTE, b)
                    sc, bi = score[:, s, :, :], biased[:, s, :, :]
                    st.mark(dve.tensor_scalar(sc, expn[:, s, :, :], 1.0, None, ALU.add))
                    st.wait()
                    st.mark(dve.reciprocal(sc, sc))
                    st.wait()
                    st.mark(dve.tensor_tensor(bi, sc, m.bias8[:, :, :], ALU.add))
                    st.wait()
                    pick(st, bi, pick1[:, s, :, :], s)
                    st.mark(dve.scalar_tensor_tensor(out=bi, in0=pick1[:, s, :, :], scalar=-1e30, in1=bi,
                                                     op0=ALU.mult, op1=ALU.add))
                    st.wait()
                    pick(st, bi, pick2[:, s, :, :], s)
                    st.mark(dve.tensor_tensor(found[:, s, :, :], pick1[:, s, :, :], pick2[:, s, :, :], ALU.add))
                    st.wait()
                    st.mark(dve.tensor_tensor(found[:, s, :, :], found[:, s, :, :], sc, ALU.mult))
                    st.wait()
                    st.mark(dve.tensor_reduce(total[:, s, :], found[:, s, :, :], AX_X, ALU.add))
                    st.wait()
                    st.mark(dve.tensor_scalar(total[:, s, :], total[:, s, :], 1e-20, None, ALU.add))
                    st.wait()
                    st.mark(dve.reciprocal(total[:, s, :], total[:, s, :]))
                    st.wait()
                    st.mark(dve.tensor_tensor(comb[:, s, :, :], found[:, s, :, :], wide(total[:, s, :], 2, E0), ALU.mult))
                    st.end()

                def front(b, s):
                    norm.dve(dve, b, s)
                    route(b, s)

                def combine(b, s, i, st):
                    h = tiles(m.h, b)
                    dve.wait_ge(proj_done, E0A * b + i + 1)
                    y = pproj[i % 2][:, 0:TT * D].rearrange("p (t n) -> p t n", t=TT)
                    if i == 0:
                        st.mark(dve.tensor_tensor(h, h, y, ALU.add))
                        return
                    if i == 1:
                        dve.wait_ge(route_steps, ROUTE * (b + 1))
                    st.wait()
                    for t in range(TT):
                        st.mark(dve.scalar_tensor_tensor(out=h[:, t, :], in0=y[:, t, :],
                                                         scalar=comb[:, s, t, ORDER[i]:ORDER[i] + 1],
                                                         in1=h[:, t, :], op0=ALU.mult, op1=ALU.add))

                def main(b, s, nxt, prev):
                    st = Steps(dve, combined, PER, b)
                    for i in range(E0A):
                        n = E0A * b + i
                        dve.wait_ge(relu_done, n + 1)
                        over(dve, proj_done, n - 1)
                        dve.tensor_tensor(hid[:, i % 2, :, :], relu[:, i % 2, :, :], relu[:, i % 2, :, :],
                                          ALU.mult).then_inc(hid_done, 1)
                        if i >= 1:
                            combine(b, s, i - 1, st)
                        if i == 0 and nxt:
                            norm.dve_stats(dve, *nxt)
                        if i == 1 and nxt:
                            norm.dve_apply(dve, *nxt)
                        if i == 7 and nxt:
                            route(*nxt)
                    combine(b, s, E0A - 1, st)
                    st.end()

                pipeline(dve, front, main, lambda b, s: None)


def mlstm(nc, m):
    sem = m.sem
    with ExitStack() as ctx:
        def sb(name, shape, dt=F32):
            return ctx.enter_context(nc.sbuf_tensor("ml_" + name, shape, dt))

        XP = CONV_K - 1 + T
        xm = sb("xm", [C, 2, KI, XP])
        xc = sb("xc", [C, KI, T])
        xconv = sb("xconv", [C, 2, KI, T])
        skipped = sb("skipped", [C, 2, KI, T])
        z = sb("z", [C, 2, KI, T])
        zact = sb("zact", [C, 2, KI, T])
        qT = sb("qT", [GR, MG, T])
        kT = sb("kT", [GR, 2, MG, T])
        qm = sb("qm", [GR, 2, MH, T])
        v_diag = sb("v_diag", [P, 2, TT, MH * MOUT + MOUT + 1])
        gw = sb("gw", [C, 2, KI, GATE_W])
        gates = sb("gates", [GATE_W, T])
        nabs = sb("nabs", [GATE_W, T])
        lnf = sb("lnf", [GATE_W, T])
        ones = sb("ones", [GATE_W, T])
        cs = sb("cs", [MH, T])
        top = sb("top", [MH, T])
        rest1 = sb("rest1", [MH, T])
        rest2 = sb("rest2", [MH, T])
        mid = sb("mid", [MH, T], BF16)
        mld = sb("mld", [MH, T])
        parts = sb("parts", [C, 2, T], BF16)
        rows = sb("rows", [64, 2, T])
        cols = sb("cols", [P, 2, TT, 64])
        decay = sb("decay", [P, 3, TRI])
        ct = sb("ct", [P, 3, TRI])
        ot = sb("ot", [MOUT, 2, MG, T])
        den = sb("den", [P, TT, 9])
        rden = sb("rden", [P, TT, 9])
        hn = sb("hn", [P, TT, 9, MD])
        hc = sb("hc", [P, TT, 9, MD])
        hsq = sb("hsq", [P, TT, 9, MD])
        hsum = sb("hsum", [P, TT, 9])
        hvar = sb("hvar", [P, TT * 9])
        hrstd = sb("hrstd", [P, TT * 9])
        hln = sb("hln", [P, TT, INNER])
        gated = sb("gated", [C, KI, T])
        misc, w0, w1, pa0, pa1, ps0, ps1, po = m.banks
        parg, pscore = (pa0, pa1), (ps0, ps1)

        norm = Norm(m, 3)
        setup = sem("ml_setup")
        gw_made = sem("ml_gate_weights_made")
        gw_copied = sem("ml_gate_weights_copied")
        up_done = sem("ml_up_done")
        x_copied = sem("ml_x_copied")
        z_copied = sem("ml_z_copied")
        conv_steps = sem("ml_conv_steps")
        x_act = sem("ml_x_activated")
        z_act = sem("ml_z_activated")
        x_skip = sem("ml_x_skipped")
        gates_done = sem("ml_gates_projected")
        gate_steps = sem("ml_gate_steps")
        f_abs = sem("ml_f_abs")
        f_exp = sem("ml_f_exp")
        f_ln = sem("ml_f_ln")
        mld_ready = sem("ml_max_log_d_ready")
        e_ready = sem("ml_floor_ready")
        parts_ready = sem("ml_parts_ready")
        rows_turned = sem("ml_rows_turned")
        cols_ready = sem("ml_cols_ready")
        qk_done = sem("ml_qk_projected")
        q_copied = sem("ml_q_copied")
        k_copied = sem("ml_k_copied")
        q_masked = sem("ml_q_masked")
        v_done = sem("ml_v_projected")
        v_spread = sem("ml_v_spread")
        argued = sem("ml_args_ready")
        scored = sem("ml_scored")
        decayed = sem("ml_decayed")
        weighted = sem("ml_weighted")
        summed = sem("ml_summed")
        o_copied = sem("ml_o_copied")
        o_turned = sem("ml_o_turned")
        head_steps = sem("ml_head_norm_steps")
        head_var = sem("ml_head_var")
        head_rstd = sem("ml_head_rstd")
        hln_ready = sem("ml_head_norm_ready")
        hln_turned = sem("ml_head_norm_turned")
        out_steps = sem("ml_out_steps")
        gated_ready = sem("ml_gated_ready")
        down_done = sem("ml_down_done")
        h_added = sem("ml_h_added")
        CONV, GATE, HEAD, OUTS = KI * CONV_K, 10, 13, KI
        SETUP = 8

        def diag(tile, g, off, width):
            heads = min(MGH, MH - g * MGH)
            at = g * MGH * MOUT + off
            step = MSTEP if width == MD else MOUT + 1
            return tile[:, at:at + heads * step].rearrange("p (i w) -> p i w", w=step)[:, :, 0:width]

        with nc.Block() as block:
            @block.gpsimd
            def _(pool):
                pool.memset(v_diag[:, :, :, :], 0.0).then_inc(setup, 1)
                pool.memset(xm[:, :, :, 0:CONV_K - 1], 0.0).then_inc(setup, 1)
                pool.memset(parts[:, :, :], 0.0).then_inc(setup, 1)
                pool.memset(rows[:, :, :], 0.0).then_inc(setup, 1)
                pool.memset(ones[:, :], 1.0).then_inc(setup, 1)
                pool.wait_ge(setup, 5)
                for s in range(2):
                    for t in range(TT):
                        for g in range(MG):
                            pool.memset(diag(v_diag[:, s, t, :], g, GR, 1), 1.0).then_inc(setup, 1)
                m.wait_load(pool, 3)

                def skip(b, s):
                    pool.wait_ge(x_act, b + 1)
                    over(pool, out_steps, OUTS * (b - 1))
                    pass_gate(pool, m)
                    pool.tensor_scalar(skipped[:, s, :, :], xconv[:, s, :, :], m.skip[:, 0:1], 1.0,
                                       ALU.mult, ALU.mult).then_inc(x_skip, 1)

                def mask(b, s):
                    pool.wait_ge(q_copied, b + 1)
                    over(pool, scored, MH * (b - 1))
                    pass_gate(pool, m)
                    for hd in range(MH):
                        ins = pool.tensor_scalar(qm[:, s, hd, :], qT[:, hd // MGH, :],
                                                 m.head_mask36[:, hd % MGH:hd % MGH + 1], 1.0, ALU.mult, ALU.mult)
                    ins.then_inc(q_masked, 1)

                def early(b, s):
                    norm.pool(pool, b, s)

                def late(b, s, ahead):
                    skip(b, s)
                    early(*ahead)
                    mask(b, s)

                def back(b, s):
                    pool.wait_ge(head_var, b + 1)
                    pool.tensor_tensor(hrstd[:, :], hvar[:, :], m.neg_half[:, 0:TT * 9], ALU.pow).then_inc(head_rstd, 1)

                def main(b, s, nxt, ahead, prev):
                    if prev:
                        back(*prev)
                    if nxt:
                        skip(*nxt)
                    if ahead:
                        early(*ahead)
                    if nxt:
                        mask(*nxt)

                pipeline_ahead(pool, early, late, main, back)

            @block.tensor
            def _(pe):
                m.wait_load(pe, 3)
                for part, turned in enumerate(((m.wq_turned, m.wk_turned), (m.wv_turned,))):
                    for i in range(KI):
                        o = w0[0:C, (part * KI + i) * GATE_W:(part * KI + i + 1) * GATE_W]
                        n = len(turned) * KI
                        for j in range(n):
                            wt, k = turned[j // KI], j % KI
                            row = (2 * KI if part else 0) + j
                            last = pe.matmul(o, wt[:, k, i * C:(i + 1) * C], m.wgate[:, row, :],
                                             start=(j == 0), stop=(j == n - 1))
                last.then_inc(gw_made, 1)

                def turn_in(b, s):
                    over(pe, q_copied, b)
                    over(pe, h_added, b - 2 if not isinstance(b, int) or b > 2 else 0)
                    norm.pe(pe, b, s, misc)

                def up(b, s):
                    pe.wait_ge(norm.xt_ready, b + 1)
                    over(pe, v_spread, b)
                    if isinstance(b, int) and b == 0:
                        pe.wait_ge(gw_copied, 1)
                    for pair, bank in enumerate((w0, w1, misc)):
                        for j in range(2):
                            i = 2 * pair + j
                            for k in range(KD):
                                last = pe.matmul(bank[0:C, j * T:(j + 1) * T], m.wup[:, k, i * C:(i + 1) * C],
                                                 m.xt[:, s, k, :], start=(k == 0), stop=(k == KD - 1))
                        last.then_inc(up_done, 1)

                def gate_proj(b, s):
                    pe.wait_ge(x_act, b + 1)
                    pe.wait_ge(z_copied, 2 * b + 2)
                    over(pe, cols_ready, b)
                    for j in range(2 * KI):
                        part, i = j // KI, j % KI
                        rhs = xm[:, s, i, CONV_K - 1:XP] if part else xconv[:, s, i, :]
                        last = pe.matmul(misc[0:GATE_W, 0:T], gw[:, part, i, :], rhs,
                                         start=(j == 0), stop=(j == 2 * KI - 1))
                    last.then_inc(gates_done, 1)

                def qk(b, s, between=None):
                    for pair, bank in enumerate((misc, w0, w1)):
                        if pair == 0:
                            pe.wait_ge(gate_steps, GATE * b + 1)
                        if pair == 1:
                            if between:
                                between()
                            over(pe, out_steps, OUTS * (b - 1))
                        for j in range(2):
                            g = (2 * pair + j) % MG
                            wt = m.wq if 2 * pair + j < MG else m.wk
                            for i in range(KI):
                                last = pe.matmul(bank[0:GR, j * T:(j + 1) * T], wt[:, i, g * GR:(g + 1) * GR],
                                                 xconv[:, s, i, :], start=(i == 0), stop=(i == KI - 1))
                        last.then_inc(qk_done, 1)

                def v(b, s):
                    pe.wait_ge(k_copied, b + 1)
                    for t, bank in enumerate((w0, w1)):
                        at = CONV_K - 1 + t * P
                        for i in range(KI):
                            last = pe.matmul(bank[:, 0:INNER], xm[:, s, i, at:at + P], m.wv[:, i, :],
                                             start=(i == 0), stop=(i == KI - 1))
                    last.then_inc(v_done, 1)

                def turn_rows(b, s):
                    pe.wait_ge(e_ready, b + 1)
                    pe.wait_ge(gate_steps, GATE * b + GATE)
                    pe.wait_ge(z_copied, 2 * b + 4 if not isinstance(b, int) or b < B - 1 else 2 * B)
                    over(pe, h_added, b - 1)
                    pass_gate(pe, m)
                    for t in range(TT):
                        last = pe.transpose(misc[:, t * 64:(t + 1) * 64], rows[:, s, t * P:(t + 1) * P], m.ident[0:64, 0:64])
                    last.then_inc(rows_turned, 1)

                def turn_out(b, s):
                    pe.wait_ge(o_copied, MG * (b + 1))
                    pe.wait_ge(z_copied, 2 * b + 5 if not isinstance(b, int) or b < B - 2 else 2 * B)
                    over(pe, out_steps, OUTS * b)
                    for t, bank in enumerate((w0, w1)):
                        for g in range(MG):
                            last = pe.transpose(bank[:, g * MOUT:(g + 1) * MOUT], ot[:, s, g, t * P:(t + 1) * P],
                                                m.ident[0:MOUT, 0:MOUT])
                    last.then_inc(o_turned, 1)

                def turn_back(b, s):
                    pe.wait_ge(hln_ready, b + 1)
                    for i in range(KI):
                        for t in range(TT):
                            o = (w0 if i < 2 else w1)[0:C, (i % 2) * T + t * P:(i % 2) * T + (t + 1) * P]
                            last = pe.transpose(o, hln[:, t, i * C:(i + 1) * C], m.ident[:, :])
                    last.then_inc(hln_turned, 1)

                def down(b, s):
                    pe.wait_ge(gated_ready, b + 1)
                    pe.wait_ge(q_copied, b + 3 if not isinstance(b, int) or b < B - 2 else B)
                    over(pe, h_added, b)
                    for t in range(TT):
                        for i in range(KI):
                            last = pe.matmul(misc[:, t * D:(t + 1) * D], gated[:, i, t * P:(t + 1) * P],
                                             m.wdown[:, i, :], start=(i == 0), stop=(i == KI - 1))
                    last.then_inc(down_done, 1)

                def early(b, s):
                    turn_in(b, s)
                    up(b, s)

                def late(b, s, ahead):
                    gate_proj(b, s)
                    qk(b, s)
                    v(b, s)
                    early(*ahead)
                    turn_rows(b, s)

                def back(b, s):
                    turn_out(b, s)
                    turn_back(b, s)
                    down(b, s)

                def argue(b, s, hd):
                    n = MH * b + hd
                    over(pe, decayed, 2 * (n - 1))
                    o = parg[hd % 2]
                    pe.matmul(o[:, 0:T], m.pick_head[:, hd, :], parts[:, s, :], start=True, stop=False,
                              skip_group_check=True)
                    pe.matmul(o[:, T:TRI], m.pick_head[:, hd, :], parts[:, s, P:T], start=False, stop=False,
                              skip_group_check=True)
                    pe.matmul(o[:, 0:P], m.ident_bf[:, :], m.future[:, :], start=False, stop=False,
                              skip_group_check=True)
                    pe.matmul(o[:, T:TRI], m.ident_bf[:, :], m.future[:, :], start=False, stop=True,
                              skip_group_check=True).then_inc(argued, 1)

                def score(b, s, hd):
                    n = MH * b + hd
                    over(pe, weighted, n - 1)
                    g = hd // MGH
                    pe.matmul(pscore[hd % 2][:, 0:T], kT[:, s, g, 0:P], qm[:, s, hd, :], start=True, stop=True)
                    pe.matmul(pscore[hd % 2][:, T:TRI], kT[:, s, g, P:T], qm[:, s, hd, P:T],
                              start=True, stop=True).then_inc(scored, 1)

                def attend(b, s, hd):
                    g = hd // MGH
                    pe.wait_ge(weighted, MH * b + hd + 1)
                    if hd % MGH == 0:
                        over(pe, o_copied, MG * b + g)
                    end = hd % MGH == MGH - 1 or hd == MH - 1
                    va = v_diag[:, s, :, hd * MOUT:(hd + 1) * MOUT]
                    pe.matmul(po[0:MOUT, 0:T], va[:, 0, :], ct[:, hd % 3, 0:T], start=(hd % MGH == 0), stop=False,
                              skip_group_check=True)
                    pe.matmul(po[0:MOUT, P:T], va[:, 1, :], ct[:, hd % 3, T:TRI], start=False, stop=end,
                              skip_group_check=True).then_inc(summed, 1)

                def main(b, s, nxt, ahead, prev):
                    pe.wait_ge(q_masked, b + 1)
                    pe.wait_ge(cols_ready, b + 1)
                    pe.wait_ge(parts_ready, b + 1)
                    pe.wait_ge(v_spread, b + 1)
                    pe.wait_ge(setup, 5 + 2 * TT * MG)
                    for hd in range(MH):
                        argue(b, s, hd)
                        score(b, s, hd)
                        if hd >= 2:
                            attend(b, s, hd - 2)
                        if hd == 0 and prev:
                            turn_out(*prev)
                        if hd == 3 and nxt:
                            gate_proj(*nxt)
                        if hd == 4 and prev and not nxt:
                            turn_back(*prev)
                        if hd == 4 and nxt:
                            qk(*nxt, between=(lambda: turn_back(*prev)) if prev else None)
                        if hd == 5 and nxt:
                            v(*nxt)
                        if hd == 5 and prev:
                            down(*prev)
                        if hd == 6 and ahead:
                            turn_in(*ahead)
                        if hd == 7 and ahead:
                            up(*ahead)
                    attend(b, s, MH - 2)
                    attend(b, s, MH - 1)
                    if nxt:
                        turn_rows(*nxt)

                pipeline_ahead(pe, early, late, main, back)

            @block.scalar
            def _(act):
                act.wait_ge(gw_made, 1)
                act.activation(gw[:, :, :, :], w0[0:C, 0:2 * KI * GATE_W].rearrange("p (a b c) -> p a b c", a=2, b=KI),
                               ACT.Copy).then_inc(gw_copied, 1)

                def pair(bank, rows_, n=2):
                    return bank[0:rows_, 0:n * T].rearrange("p (j n) -> p j n", j=n)

                def copy_up(b, s):
                    over(act, v_done, b - 1)
                    act.wait_ge(up_done, 3 * b + 1)
                    act.activation(xm[:, s, 0:2, CONV_K - 1:XP], pair(w0, C), ACT.Copy)
                    act.wait_ge(up_done, 3 * b + 2)
                    act.activation(xm[:, s, 2, CONV_K - 1:XP], w1[0:C, 0:T], ACT.Copy).then_inc(x_copied, 1)
                    over(act, z_act, b - 1)
                    act.activation(z[:, s, 0, :], w1[0:C, T:2 * T], ACT.Copy).then_inc(z_copied, 1)
                    act.wait_ge(up_done, 3 * b + 3)
                    act.activation(z[:, s, 1:3, :], pair(misc, C), ACT.Copy).then_inc(z_copied, 1)

                def activate_x(b, s):
                    act.wait_ge(conv_steps, CONV * (b + 1))
                    over(act, x_skip, b - 1)
                    over(act, qk_done, 3 * (b - 1))
                    act.activation(xconv[:, s, :, :], xc[:, :, :], ACT.Silu).then_inc(x_act, 1)

                def activate_z(b, s):
                    act.wait_ge(z_copied, 2 * b + 2)
                    over(act, gated_ready, b - 1)
                    act.activation(zact[:, s, :, :], z[:, s, :, :], ACT.Silu).then_inc(z_act, 1)

                def copy_qk(b, s):
                    over(act, q_masked, b)
                    act.wait_ge(qk_done, 3 * b + 1)
                    act.activation(qT[:, 0:2, :], pair(misc, GR), ACT.Copy)
                    act.wait_ge(qk_done, 3 * b + 2)
                    act.activation(qT[:, 2, :], w0[0:GR, 0:T], ACT.Copy).then_inc(q_copied, 1)
                    over(act, scored, MH * (b - 1))
                    act.activation(kT[:, s, 0, :], w0[0:GR, T:2 * T], ACT.Copy, scale=MD ** -0.5)
                    act.wait_ge(qk_done, 3 * b + 3)
                    act.activation(kT[:, s, 1:3, :], pair(w1, GR), ACT.Copy, scale=MD ** -0.5).then_inc(k_copied, 1)

                def log_forget(b, s):
                    act.wait_ge(f_abs, b + 1)
                    act.activation(lnf[32:GATE_W, :], nabs[32:GATE_W, :], ACT.Exp).then_inc(f_exp, 1)
                    act.wait_ge(f_exp, b + 1)
                    act.activation(lnf[32:GATE_W, :], lnf[32:GATE_W, :], ACT.Ln, bias=1.0).then_inc(f_ln, 1)

                def floor(b, s):
                    act.wait_ge(mld_ready, b + 1)
                    over(act, rows_turned, b - 1)
                    act.activation(rows[32:GATE_W, s, :], mld[:, :], ACT.Exp, scale=-1.0).then_inc(e_ready, 1)

                def copy_cols(b, s):
                    act.wait_ge(rows_turned, b + 1)
                    over(act, head_steps, HEAD * (b - 1))
                    act.activation(cols[:, s, :, :], misc[:, 0:TT * 64].rearrange("p (t n) -> p t n", t=TT),
                                   ACT.Copy).then_inc(cols_ready, 1)

                def copy_xt(b, s):
                    over(act, up_done, 3 * (b - 1))
                    norm.act(act, b, s, misc, m.xt[:, s, :, :])

                def early(b, s):
                    copy_xt(b, s)
                    copy_up(b, s)

                def late(b, s, ahead):
                    activate_x(b, s)
                    log_forget(b, s)
                    copy_qk(b, s)
                    floor(b, s)
                    early(*ahead)
                    copy_cols(b, s)

                def decays(b, s, hd):
                    n = MH * b + hd
                    act.wait_ge(argued, n + 1)
                    over(act, weighted, n - 2)
                    act.activation(decay[:, hd % 3, 0:T], parg[hd % 2][:, 0:T], ACT.Exp,
                                   bias=cols[:, s, 0, hd:hd + 1]).then_inc(decayed, 1)
                    act.activation(decay[:, hd % 3, T:TRI], parg[hd % 2][:, T:TRI], ACT.Exp,
                                   bias=cols[:, s, 1, hd:hd + 1]).then_inc(decayed, 1)

                def copy_out(b, s, g):
                    act.wait_ge(summed, MH * b + min(MGH * (g + 1), MH))
                    over(act, o_turned, b - 1)
                    act.activation(ot[:, s, g, :], po[0:MOUT, 0:T], ACT.Copy).then_inc(o_copied, 1)

                def main(b, s, nxt, ahead, prev):
                    act.wait_ge(cols_ready, b + 1)
                    for hd in range(MH):
                        decays(b, s, hd)
                        if hd == 1 and nxt:
                            activate_x(*nxt)
                        if hd == 1:
                            activate_z(b, s)
                        if hd == 3 and nxt:
                            log_forget(*nxt)
                        if hd == 4:
                            copy_out(b, s, 0)
                        if hd == 4 and nxt:
                            copy_qk(*nxt)
                        if hd == 5 and nxt:
                            floor(*nxt)
                        if hd == 7:
                            copy_out(b, s, 1)
                        if hd == 6 and ahead:
                            copy_xt(*ahead)
                        if hd == 7 and ahead:
                            copy_up(*ahead)
                    copy_out(b, s, 2)
                    if nxt:
                        copy_cols(*nxt)

                pipeline_ahead(act, early, late, main, lambda b, s: None)

            @block.vector
            def _(dve):
                m.wait_load(dve, 3)
                dve.wait_ge(setup, 5 + 2 * TT * MG)

                def conv(b, s):
                    dve.wait_ge(x_copied, b + 1)
                    over(dve, x_act, b)
                    st = Steps(dve, conv_steps, CONV, b)
                    for j in range(CONV_K):
                        for i in range(KI):
                            src = xm[:, s, i, j:j + T]
                            if j == 0:
                                st.mark(dve.tensor_scalar(xc[:, i, :], src, m.conv_w[:, i, j:j + 1],
                                                          m.conv_b[:, i:i + 1], ALU.mult, ALU.add))
                            else:
                                st.wait(st.n - KI + 1)
                                st.mark(dve.scalar_tensor_tensor(out=xc[:, i, :], in0=src,
                                                                 scalar=m.conv_w[:, i, j:j + 1], in1=xc[:, i, :],
                                                                 op0=ALU.mult, op1=ALU.add))
                    st.end()

                def gate_logs(b, s):
                    dve.wait_ge(gates_done, b + 1)
                    st = Steps(dve, gate_steps, GATE, b)
                    st.mark(dve.tensor_scalar(gates[:, :], misc[0:GATE_W, 0:T], m.gate_b[:, 0:1], None, ALU.add))
                    st.wait()
                    f = gates[32:GATE_W, :]
                    dve.scalar_tensor_tensor(out=nabs[32:GATE_W, :], in0=f, scalar=-1.0, in1=f, op0=ALU.mult,
                                             op1=ALU.min).then_inc(f_abs, 1)
                    return st

                def gate_scans(b, s):
                    st = Steps(dve, gate_steps, GATE, b)
                    st.n = 1
                    f = gates[32:GATE_W, :]
                    dve.wait_ge(f_ln, b + 1)
                    st.mark(dve.scalar_tensor_tensor(out=lnf[32:GATE_W, :], in0=f, scalar=0.0, in1=lnf[32:GATE_W, :],
                                                     op0=ALU.min, op1=ALU.subtract))
                    st.wait()
                    st.mark(dve.tensor_tensor_scan(cs[:, :], ones[32:GATE_W, :], lnf[32:GATE_W, :], 0.0,
                                                   ALU.mult, ALU.add))
                    st.wait()
                    over(dve, rows_turned, b - 1)
                    a = rows[0:MH, s, :]
                    st.mark(dve.tensor_tensor(a, gates[0:MH, :], cs[:, :], ALU.subtract))
                    st.wait()
                    st.mark(dve.tensor_tensor_scan(top[:, :], a, a, -3e38, ALU.max, ALU.max))
                    st.wait()
                    over(dve, e_ready, b)
                    st.mark(dve.tensor_tensor(mld[:, :], cs[:, :], top[:, :], ALU.add))
                    st.wait()
                    dve.tensor_scalar(mld[:, :], mld[:, :], -87.0, None, ALU.max).then_inc(mld_ready, 1)
                    over(dve, argued, MH * (b - 1))
                    st.mark(dve.tensor_scalar(parts[0:MH, s, :], top[:, :], -1.0, None, ALU.mult))
                    st.wait()
                    st.mark(dve.scalar_tensor_tensor(out=rest1[:, :], in0=top[:, :], scalar=-1.0,
                                                     in1=parts[0:MH, s, :], op0=ALU.mult, op1=ALU.subtract))
                    st.wait()
                    dve.tensor_copy(parts[32:32 + MH, s, :], rest1[:, :])
                    st.mark(dve.tensor_copy(mid[:, :], rest1[:, :]))
                    st.wait()
                    st.mark(dve.tensor_tensor(rest2[:, :], rest1[:, :], mid[:, :], ALU.subtract))
                    st.wait()
                    dve.tensor_copy(parts[64:64 + MH, s, :], rest2[:, :]).then_inc(parts_ready, 1)
                    st.end()

                def spread(b, s):
                    dve.wait_ge(v_done, b + 1)
                    over(dve, summed, MH * (b - 1))
                    for t, bank in enumerate((w0, w1)):
                        for g in range(MG):
                            cols_ = min(GR, INNER - g * GR)
                            ins = dve.tensor_copy(diag(v_diag[:, s, t, :], g, 0, MD),
                                                  bank[:, g * GR:g * GR + cols_].rearrange("p (i w) -> p i w", w=MD))
                    ins.then_inc(v_spread, 1)

                def head_stats(b, s):
                    dve.wait_ge(o_turned, b + 1)
                    st = Steps(dve, head_steps, HEAD, b)
                    for t, bank in enumerate((w0, w1)):
                        raw = bank[:, 0:MG * MOUT].rearrange("p (g w) -> p g w", g=MG)
                        st.mark(dve.scalar_tensor_tensor(
                            out=den[:, t, :].rearrange("p (g i) -> p g i", g=MG), in0=raw[:, :, GR:MOUT], scalar=-1.0,
                            in1=cols[:, s, t, 32:41].rearrange("p (g i) -> p g i", g=MG),
                            op0=ALU.mult, op1=ALU.max))
                    for t, bank in enumerate((w0, w1)):
                        raw = bank[:, 0:MG * MOUT].rearrange("p (g w) -> p g w", g=MG)
                        st.wait(t + 1)
                        d = den[:, t, :].rearrange("p (g i) -> p g i", g=MG)
                        st.mark(dve.tensor_tensor(d, raw[:, :, GR:MOUT], d, ALU.max))
                    st.wait()
                    st.mark(dve.tensor_scalar(den[:, :, :], den[:, :, :], 1e-6, None, ALU.add))
                    st.wait()
                    st.mark(dve.reciprocal(rden[:, :, :], den[:, :, :]))
                    st.wait()
                    for t, bank in enumerate((w0, w1)):
                        raw = bank[:, 0:MG * MOUT].rearrange("p (g w) -> p g w", g=MG)[:, :, 0:GR]
                        st.mark(dve.tensor_tensor(hn[:, t, :, :].rearrange("p (g i) c -> p g i c", g=MG),
                                                  raw.rearrange("p g (i c) -> p g i c", c=MD),
                                                  wide(rden[:, t, :].rearrange("p (g i) -> p g i", g=MG), 3, MD),
                                                  ALU.mult))

                def head_center(b, s):
                    st = Steps(dve, head_steps, HEAD, b)
                    st.n = 8
                    st.wait()
                    st.mark(dve.tensor_reduce(hsum[:, :, :], hn[:, :, :, :], AX_X, ALU.add))
                    st.wait()
                    flat = lambda x: x[:, :, :, :].rearrange("p t g c -> p (t g) c")
                    st.mark(dve.scalar_tensor_tensor(
                        out=flat(hc), in0=wide(hsum[:, :, :].rearrange("p t g -> p (t g)"), 2, MD), scalar=-1.0 / MD,
                        in1=flat(hn), op0=ALU.mult, op1=ALU.add))
                    st.wait()
                    st.mark(dve.tensor_tensor(flat(hsq), flat(hc), flat(hc), ALU.mult))
                    st.wait()
                    st.mark(dve.tensor_reduce(hsum[:, :, :], hsq[:, :, :, :], AX_X, ALU.add))
                    st.wait()
                    dve.tensor_scalar(hvar[:, :], hsum[:, :, :].rearrange("p t g -> p (t g)"), 1.0 / MD, LN_EPS,
                                      ALU.mult, ALU.add).then_inc(head_var, 1)

                def head_scale(b, s):
                    st = Steps(dve, head_steps, HEAD, b)
                    st.n = HEAD - 1
                    dve.wait_ge(head_rstd, b + 1)
                    over(dve, hln_turned, b)
                    rs = hrstd[:, :].rearrange("p (t g) -> p t g", t=TT)[:, :, 0:MH]
                    st.mark(dve.tensor_tensor(hln[:, :, :].rearrange("p t (g c) -> p t g c", c=MD),
                                              hc[:, :, 0:MH, :], wide(rs, 3, MD), ALU.mult))
                    st.end()
                    st.wait()
                    dve.sem_inc(hln_ready, 1)

                def gate_out(b, s):
                    dve.wait_ge(hln_turned, b + 1)
                    dve.wait_ge(x_skip, b + 1)
                    dve.wait_ge(z_act, b + 1)
                    over(dve, down_done, b)
                    st = Steps(dve, out_steps, OUTS, b)
                    for i in range(KI):
                        src = (w0 if i < 2 else w1)[0:C, (i % 2) * T:(i % 2 + 1) * T]
                        st.mark(dve.scalar_tensor_tensor(out=gated[:, i, :], in0=src, scalar=m.norm_w[:, i:i + 1],
                                                         in1=skipped[:, s, i, :], op0=ALU.mult, op1=ALU.add))
                    st.end()
                    st.wait()
                    dve.tensor_tensor(gated[:, :, :], gated[:, :, :], zact[:, s, :, :], ALU.mult).then_inc(gated_ready, 1)

                def add(b, s):
                    dve.wait_ge(down_done, b + 1)
                    h = tiles(m.h, b)
                    dve.tensor_tensor(h, h, misc[:, 0:TT * D].rearrange("p (t n) -> p t n", t=TT),
                                      ALU.add).then_inc(h_added, 1)

                def early(b, s):
                    norm.dve(dve, b, s)
                    conv(b, s)

                def late(b, s, ahead):
                    gate_logs(b, s)
                    gate_scans(b, s)
                    spread(b, s)
                    early(*ahead)

                def back(b, s):
                    head_stats(b, s)
                    head_center(b, s)
                    head_scale(b, s)
                    gate_out(b, s)
                    add(b, s)

                def main(b, s, nxt, ahead, prev):
                    for hd in range(MH):
                        n = MH * b + hd
                        dve.wait_ge(decayed, 2 * n + 2)
                        dve.wait_ge(scored, n + 1)
                        over(dve, summed, n - 2)
                        dve.tensor_tensor(ct[:, hd % 3, :], pscore[hd % 2][:, 0:TRI], decay[:, hd % 3, :],
                                          ALU.mult).then_inc(weighted, 1)
                        if hd == 0 and prev:
                            head_stats(*prev)
                        if hd == 1 and prev:
                            head_center(*prev)
                        if hd == 3 and nxt:
                            gate_logs(*nxt)
                        if hd == 3 and prev:
                            head_scale(*prev)
                        if hd == 3 and prev:
                            gate_out(*prev)
                        if hd == 4 and nxt:
                            gate_scans(*nxt)
                        if hd == 4 and ahead:
                            norm.dve_stats(dve, *ahead)
                        if hd == 5 and ahead:
                            norm.dve_apply(dve, *ahead)
                        if hd == 5 and prev:
                            add(*prev)
                        if hd == 6 and nxt:
                            spread(*nxt)
                        if hd == 7 and ahead:
                            conv(*ahead)
                pipeline_ahead(dve, early, late, main, back)


def expert_choice(nc, m, a, out):
    sem = m.sem
    ROWS = out.rearrange("(t p) d -> p t d", p=P)
    XROWS = a["xrows"].rearrange("(t p) d -> p t d", p=P)
    with ExitStack() as ctx:
        def sb(name, shape, dt=F32):
            return ctx.enter_context(nc.sbuf_tensor("ec_" + name, shape, dt))

        xt_all = sb("xt_all", [C, KD, N])
        expn = sb("expn", [P, 2, TT, E1])
        srow = sb("srow", [P, 2, TT, E1])
        score = sb("score", [P, NT, E1])
        thr = sb("thr", [P, E1], I32)
        trial = sb("trial", [P, 3, E1], I32)
        above = sb("above", [P, NT, 3, E1], BF16)
        enough = sb("enough", [P, 3, E1])
        passed = sb("passed", [P, E1])
        grow = sb("grow", [P, E1], I32)
        gt = sb("gt", [P, NT, E1], BF16)
        eq = sb("eq", [P, NT, E1], BF16)
        sel = sb("sel", [P, NT, E1], BF16)
        room = sb("room", [P, E1])
        place = sb("place", [P, NT, E1])
        ones = sb("ones", [P, P], BF16)
        onehot = sb("onehot", [P, NT, CAP], BF16)
        ids = sb("ids", [P, 2, TT], I32)
        xg = sb("xg", [P, 2, TT, XROW])
        topscore = sb("topscore", [P, 2, TT])
        xgt = sb("xgt", [C, 2, KD, CAP])
        wgu = sb("wgu", [C, 2, 2, KD, F1])
        wd = sb("wd", [P, 2, KF, D])
        silu = sb("silu", [P, 2, T])
        act_s = sb("act_s", [P, 2, KS, T])
        act_e = sb("act_e", [P, 2, KF, CAP])
        y = sb("y", [P, 2, TT, D])
        turn, pl, pg0, pg1, pd0, pd1, pd2, pd3 = m.banks
        pgu = (pg0, pg1)

        m.gate1T = m.load("gate1T", [C, KD, E1], stage=4, sb=sb)
        m.ws_gu = m.load("ws_gu", [C, 2, KD, FS], stage=4, sb=sb)
        m.ws_d = m.load("ws_d", [P, KS, D], stage=4, sb=sb)
        m.below = m.load("below", [P, P], BF16, stage=4, sb=sb)
        m.token_id = m.load("token_id", [P, NT, 1], F16, stage=4, sb=sb)
        m.bits = m.load("bits", [P, 3, E1], I32, stage=4, sb=sb)
        m.bit_value = m.load("bit_value", [P, 1], stage=4, sb=sb)
        m.iota1 = m.load("iota1", [P, CAP], BF16, stage=4, sb=sb)

        norm = Norm(m, 4)
        setup = sem("ec_setup")
        logits = sem("ec_logits")
        exped = sem("ec_exp_ready")
        score_steps = sem("ec_score_steps")
        scored = sem("ec_scored")
        xt_kept = sem("ec_xt_kept")
        x_stored = [sem(f"ec_x_stored{s}") for s in range(2)]
        s_stored = [sem(f"ec_scores_stored{s}") for s in range(2)]
        sh_gu = sem("ec_shared_gate_up")
        sh_silu = sem("ec_shared_silu")
        sh_act = sem("ec_shared_act")
        sh_down = sem("ec_shared_down")
        sh_y = sem("ec_shared_y")
        y_stored = [sem(f"ec_y_stored{s}") for s in range(2)]
        compared = sem("ec_compared")
        counted = sem("ec_counted")
        round_steps = sem("ec_round_steps")
        bit_scaled = sem("ec_bit_scaled")
        place_ready = sem("ec_place_ready")
        picked = sem("ec_picked")
        prefixed = sem("ec_prefixed")
        placed = sem("ec_placed")
        hot = sem("ec_onehot_ready")
        id_sums = sem("ec_id_sums")
        id_ready = sem("ec_ids_ready")
        x_gathered = [sem(f"ec_gathered{s}") for s in range(2)]
        xg_turned = sem("ec_xg_turned")
        xgt_ready = sem("ec_xgt_ready")
        score_ready = sem("ec_topscore_ready")
        gu_done = sem("ec_gate_up")
        silu_done = sem("ec_silu")
        act_done = sem("ec_act")
        down_done = sem("ec_down")
        y_ready = sem("ec_y_ready")
        y_added = [sem(f"ec_y_added{s}") for s in range(2)]
        wgu_in = [sem(f"ec_wgu_loaded{s}") for s in range(2)]
        wd_in = [sem(f"ec_wd_loaded{s}") for s in range(2)]
        SCORE = 2
        ROUND = 6
        used = lambda b, s: (b - s) * 8

        def by_pairs(eng, body, n):
            with eng.Fori(0, n // 2) as j:
                body(j * 2, 0)
                body(j * 2 + 1, 1)

        def rounds_of(b):
            return 1 if isinstance(b, int) and b == B - 1 else 2

        with nc.Block() as block:
            @block.sync
            def _(sp):
                def load_weights(e, s):
                    wg_src = a["wgu"][bass.ds(e, 1), :, :] if not isinstance(e, int) else a["wgu"][e:e + 1, :, :]
                    wd_src = a["wd"][bass.ds(e, 1), :, :] if not isinstance(e, int) else a["wd"][e:e + 1, :, :]
                    sp.dma_start(wgu[:, s, :, :, :].rearrange("p a k f -> p (a k f)"),
                                 wg_src.rearrange("e p f -> p (e f)")).then_inc(wgu_in[s], 16)
                    sp.dma_start(wd[:, s, :, :].rearrange("p k d -> p (k d)"),
                                 wd_src.rearrange("e p f -> p (e f)")).then_inc(wd_in[s], 16)

                def store_rows(b, s):
                    sp.wait_ge(norm.xn, b + 1)
                    sp.dma_start(tiles(XROWS, b)[:, :, 0:D], m.xn[:, s, :, :]).then_inc(x_stored[s], 16)
                    sp.wait_ge(scored, b + 1)
                    sp.dma_start(tiles(XROWS, b)[:, :, D:XROW], srow[:, s, :, :]).then_inc(s_stored[s], 16)

                def store_y(b, s):
                    sp.wait_ge(sh_y, b + 1)
                    sp.dma_start(tiles(ROWS, b), y[:, s, :, :]).then_inc(y_stored[s], 16)

                for dst, src in m.loads[4]:
                    sp.dma_start(dst, src).then_inc(m.loaded[4], 16)
                by_pairs(sp, store_rows, B)
                for e in range(2):
                    load_weights(e, e)
                by_pairs(sp, store_y, B)

                def refill(e, s):
                    sp.wait_ge(down_done, e + 1)
                    load_weights(e + 2, s)

                by_pairs(sp, refill, E1 - 2)

            @block.gpsimd
            def _(pool):
                pool.memset(thr[:, :], 0).then_inc(setup, 1)
                pool.memset(ones[:, :], 1.0).then_inc(setup, 1)

                def keep(b, s):
                    norm.pool(pool, b, s)
                    pool.wait_ge(norm.xt_ready, b + 1)
                    at = b * T
                    dst = xt_all[:, :, bass.ds(at, T)] if not isinstance(b, int) else xt_all[:, :, at:at + T]
                    pool.tensor_copy(dst, m.xt[:, s, :, :]).then_inc(xt_kept, 1)

                keep(0, 0)
                keep(1, 1)
                with pool.Fori(1, B // 2) as j:
                    keep(j * 2, 0)
                    keep(j * 2 + 1, 1)

                def gather(e, s):
                    pool.wait_ge(id_ready, e + 1)
                    if isinstance(e, int) and e == 0:
                        for k in range(2):
                            pool.wait_ge(x_stored[k], 8 * B)
                            pool.wait_ge(s_stored[k], 8 * B)
                    over(pool, xg_turned, e - 1)
                    over(pool, score_ready, e - 1)
                    pass_gate(pool, m)
                    for t in range(TT):
                        pool.indirect_dma_start(xg[:, s, t, :], None, a["xrows"][:, :],
                                                bass.IndirectOffsetOnAxis(ap=ids[:, s, t:t + 1], axis=0)
                                                ).then_inc(x_gathered[s], 16)

                def scatter(e, s):
                    pool.wait_ge(y_ready, e + 1)
                    if isinstance(e, int) and e == 0:
                        for k in range(2):
                            pool.wait_ge(y_stored[k], 8 * B)
                    else:
                        pool.wait_ge(y_added[1 - s], (e + s) * 16)
                    pass_gate(pool, m)
                    for t in range(TT):
                        pool.indirect_dma_start(out[:, :], bass.IndirectOffsetOnAxis(ap=ids[:, s, t:t + 1], axis=0),
                                                y[:, s, t, :], None, compute_op=ALU.add).then_inc(y_added[s], 16)

                def main(e, s, nxt, prev):
                    if nxt:
                        gather(*nxt)
                    scatter(e, s)

                pipeline(pool, gather, main, lambda e, s: None, E1)
                for s in range(2):
                    pool.wait_ge(y_added[s], 16 * E1)

            @block.tensor
            def _(pe):
                m.wait_load(pe, 4)
                pe.wait_ge(setup, 2)

                def turn_x(b, s):
                    over(pe, norm.xt_ready, b)
                    norm.pe(pe, b, s, turn)

                def choose(b, s):
                    pe.wait_ge(norm.xt_ready, b + 1)
                    over(pe, exped, b)
                    for t in range(TT):
                        for k in range(KD):
                            last = pe.matmul(pl[:, t * E1:(t + 1) * E1], m.xt[:, s, k, t * P:(t + 1) * P],
                                             m.gate1T[:, k, :], start=(k == 0), stop=(k == KD - 1))
                    last.then_inc(logits, 1)

                def turn_and_choose(b, s, nxt, prev):
                    if nxt:
                        turn_x(*nxt)
                    choose(b, s)

                pipeline(pe, turn_x, turn_and_choose, lambda b, s: None)

                def count(r):
                    pe.wait_ge(compared, r + 1)
                    for t in range(NT):
                        last = pe.matmul(turn[:, 0:3 * E1], ones[:, :], above[:, t, :, :],
                                         start=(t == 0), stop=(t == NT - 1))
                    last.then_inc(counted, 1)

                def shared(b, s):
                    at = b * T
                    pe.wait_ge(xt_kept, b + 1)
                    for i in range(KS):
                        n = KS * b + i
                        over(pe, sh_act, n - 1)
                        for part in range(2):
                            for k in range(KD):
                                rhs = xt_all[:, k, bass.ds(at, T)] if not isinstance(b, int) else xt_all[:, k, at:at + T]
                                last = pe.matmul(pgu[i % 2][:, part * T:(part + 1) * T],
                                                 m.ws_gu[:, part, k, i * P:(i + 1) * P], rhs,
                                                 start=(k == 0), stop=(k == KD - 1))
                        last.then_inc(sh_gu, 1)
                        if i < rounds_of(b):
                            count(2 * b + i)
                    pe.wait_ge(sh_act, KS * (b + 1))
                    over(pe, sh_y, b)
                    for t in range(TT):
                        for k in range(KS):
                            last = pe.matmul(pd0[:, t * D:(t + 1) * D], act_s[:, s, k, t * P:(t + 1) * P],
                                             m.ws_d[:, k, :], start=(k == 0), stop=(k == KS - 1))
                    last.then_inc(sh_down, 1)

                shared(0, 0)
                shared(1, 1)
                with pe.Fori(1, B // 2 - 1) as j:
                    shared(j * 2, 0)
                    shared(j * 2 + 1, 1)
                shared(B - 2, 0)
                shared(B - 1, 1)

                def prefix(bank, src):
                    flat = src[:, :, :].rearrange("p t e -> p (t e)")
                    pe.matmul(bank[:, 0:NT * E1], m.below[:, :], flat, start=True, stop=False, skip_group_check=True)
                    for t in range(NT - 1):
                        last = pe.matmul(bank[:, (t + 1) * E1:NT * E1], ones[:, :], wide(src[:, t, :], 1, NT - 1 - t),
                                         start=False, stop=(t == NT - 2), skip_group_check=True)
                    return last

                pe.wait_ge(picked, 2)
                for t in range(NT):
                    pe.matmul(turn[:, 0:E1], ones[:, :], gt[:, t, :], start=(t == 0), stop=(t == NT - 1))
                prefix(pl, eq).then_inc(prefixed, 1)
                pe.wait_ge(picked, 3)
                prefix(pd1, sel).then_inc(prefixed, 1)

                def find(e, s):
                    pe.wait_ge(hot, e + 1)
                    over(pe, id_ready, e)
                    for h in range(TT):
                        for t in range(NT):
                            last = pe.matmul(pl[:, h:h + 1], onehot[:, t, h * P:(h + 1) * P], m.token_id[:, t, :],
                                             start=(t == 0), stop=(t == NT - 1))
                    last.then_inc(id_sums, 1)

                def turn_in(e, s):
                    pe.wait_ge(x_gathered[s], used(e, s) * 2 + 32)
                    over(pe, xgt_ready, e)
                    for h in range(TT):
                        for k in range(KD):
                            last = pe.transpose(turn[0:C, k * CAP + h * P:k * CAP + (h + 1) * P],
                                                xg[:, s, h, k * C:(k + 1) * C], m.ident[:, :])
                    last.then_inc(xg_turned, 1)

                def front(e, s):
                    find(e, s)
                    turn_in(e, s)

                def gate_up(e, s, i):
                    n = KF * e + i
                    over(pe, act_done, n - 1)
                    for part in range(2):
                        for k in range(KD):
                            last = pe.matmul(pgu[i % 2][:, part * CAP:(part + 1) * CAP],
                                             wgu[:, s, part, k, i * P:(i + 1) * P], xgt[:, s, k, :],
                                             start=(k == 0), stop=(k == KD - 1))
                    last.then_inc(gu_done, 1)

                def down(e, s, i):
                    pe.wait_ge(act_done, KF * e + i + 1)
                    if i == 0:
                        pe.wait_ge(wd_in[s], used(e, s) + 16)
                        over(pe, y_ready, e - 1)
                    for h in range(TT):
                        last = pe.matmul((pd0, pd1, pd2, pd3)[2 * s + h][:, 0:D], act_e[:, s, i, h * P:(h + 1) * P],
                                         wd[:, s, i, :], start=(i == 0), stop=(i == KF - 1))
                    if i == KF - 1:
                        last.then_inc(down_done, 1)

                def main(e, s, nxt, prev):
                    pe.wait_ge(xgt_ready, e + 1)
                    pe.wait_ge(wgu_in[s], used(e, s) + 16)
                    for i in range(KF):
                        gate_up(e, s, i)
                        if i >= 1:
                            down(e, s, i - 1)
                        if i == 1 and nxt:
                            find(*nxt)
                        if i == 4 and nxt:
                            turn_in(*nxt)
                    down(e, s, KF - 1)

                pipeline(pe, front, main, lambda e, s: None, E1)

            @block.scalar
            def _(act):
                def copy_xt(b, s):
                    over(act, xt_kept, b - 1)
                    over(act, logits, b - 1)
                    norm.act(act, b, s, turn, m.xt[:, s, :, :])

                def choose(b, s):
                    act.wait_ge(logits, b + 1)
                    over(act, scored, b - 1)
                    act.activation(expn[:, s, :, :], pl[:, 0:TT * E1].rearrange("p (t e) -> p t e", t=TT),
                                   ACT.Exp, scale=-1.0).then_inc(exped, 1)

                def copy_and_choose(b, s, nxt, prev):
                    if nxt:
                        copy_xt(*nxt)
                    choose(b, s)

                pipeline(act, copy_xt, copy_and_choose, lambda b, s: None)

                def shared(b, s):
                    for i in range(KS):
                        n = KS * b + i
                        act.wait_ge(sh_gu, n + 1)
                        over(act, sh_act, n - 1)
                        act.activation(silu[:, (i + s) % 2, :], pgu[i % 2][:, 0:T], ACT.Silu).then_inc(sh_silu, 1)

                shared(0, 0)
                shared(1, 1)
                with act.Fori(1, B // 2) as j:
                    shared(j * 2, 0)
                    shared(j * 2 + 1, 1)

                def copy_xgt(e, s):
                    act.wait_ge(xg_turned, e + 1)
                    over(act, gu_done, KF * (e - 1))
                    act.activation(xgt[:, s, :, :], turn[0:C, :].rearrange("p (k n) -> p k n", k=KD),
                                   ACT.Copy).then_inc(xgt_ready, 1)

                def main(e, s, nxt, prev):
                    for i in range(KF):
                        n = KF * e + i
                        act.wait_ge(gu_done, n + 1)
                        over(act, act_done, n - 1)
                        act.activation(silu[:, i % 2, :], pgu[i % 2][:, 0:CAP], ACT.Silu).then_inc(silu_done, 1)
                        if i == 4 and nxt:
                            copy_xgt(*nxt)

                act.wait_ge(sh_act, KS * B)
                pipeline(act, copy_xgt, main, lambda e, s: None, E1)

            @block.vector
            def _(dve):
                m.wait_load(dve, 4)
                dve.wait_ge(setup, 2)

                def apply(b, s):
                    over(dve, x_stored[s], used(b, s))
                    norm.dve_apply(dve, b, s)

                def choose(b, s):
                    dve.wait_ge(exped, b + 1)
                    st = Steps(dve, score_steps, SCORE, b)
                    over(dve, s_stored[s], used(b, s))
                    st.mark(dve.tensor_scalar(expn[:, s, :, :], expn[:, s, :, :], 1.0, None, ALU.add))
                    st.wait()
                    st.mark(dve.reciprocal(srow[:, s, :, :], expn[:, s, :, :]))
                    st.end()
                    st.wait()
                    dve.tensor_copy(tiles(score, b), srow[:, s, :, :]).then_inc(scored, 1)

                def apply_and_choose(b, s, nxt, prev):
                    if nxt:
                        norm.dve_stats(dve, *nxt)
                    apply(b, s)
                    if prev:
                        choose(*prev)

                pipeline(dve, lambda b, s: norm.dve_stats(dve, b, s), apply_and_choose, choose)

                def try_bits(r):
                    st = Steps(dve, round_steps, ROUND, r)
                    if isinstance(r, int) and r == 0:
                        dve.wait_ge(scored, B)
                    else:
                        dve.wait_ge(round_steps, ROUND * r)
                    st.mark(dve.tensor_tensor(trial[:, :, :], wide(thr[:, :], 1, 3),
                                              m.bits[:, :, :], ALU.bitwise_or))
                    st.wait()
                    over(dve, counted, r)
                    dve.tensor_tensor(above[:, :, :, :], wide(score[:, :, :], 2, 3),
                                      wide(trial[:, :, :].bitcast(F32), 1, NT), ALU.is_ge).then_inc(compared, 1)

                def take_bits(r):
                    st = Steps(dve, round_steps, ROUND, r)
                    st.n = 1
                    dve.wait_ge(counted, r + 1)
                    cnt = turn[:, 0:3 * E1].rearrange("p (j e) -> p j e", j=3)
                    st.mark(dve.tensor_scalar(enough[:, :, :], cnt, float(CAP), None, ALU.is_ge))
                    st.mark(dve.tensor_scalar(m.bits[:, :, :], m.bits[:, :, :], 2, None, ALU.logical_shift_right))
                    st.wait(2)
                    st.mark(dve.tensor_reduce(passed[:, :], enough[:, :, :].rearrange("p j e -> p e j"), AX_X, ALU.add))
                    st.wait()
                    st.mark(dve.tensor_scalar(grow[:, :], passed[:, :], m.bit_value[:, 0:1], None, ALU.mult))
                    st.wait()
                    dve.tensor_scalar(m.bit_value[:, :], m.bit_value[:, :], 0.25, None, ALU.mult).then_inc(bit_scaled, 1)
                    st.mark(dve.tensor_tensor(thr[:, :], thr[:, :], grow[:, :], ALU.bitwise_or))
                    st.end()
                    dve.wait_ge(bit_scaled, r + 1)

                def multiply(b, s, i):
                    n = KS * b + i
                    dve.wait_ge(sh_silu, n + 1)
                    over(dve, sh_down, b - 1)
                    dve.tensor_tensor(act_s[:, s, i, :], silu[:, (i + s) % 2, :], pgu[i % 2][:, T:2 * T],
                                      ALU.mult).then_inc(sh_act, 1)

                def shared(b, s):
                    for i in range(KS):
                        if i < rounds_of(b):
                            try_bits(2 * b + i)
                        multiply(b, s, i)
                        if i < rounds_of(b):
                            take_bits(2 * b + i)
                    dve.wait_ge(sh_down, b + 1)
                    over(dve, y_stored[s], used(b, s))
                    dve.tensor_tensor(y[:, s, :, :], tiles(m.h, b), pd0[:, 0:TT * D].rearrange("p (t n) -> p t n", t=TT),
                                      ALU.add).then_inc(sh_y, 1)

                shared(0, 0)
                shared(1, 1)
                with dve.Fori(1, B // 2 - 1) as j:
                    shared(j * 2, 0)
                    shared(j * 2 + 1, 1)
                shared(B - 2, 0)
                shared(B - 1, 1)

                limit = wide(thr[:, :].bitcast(F32), 1, NT)
                dve.wait_ge(round_steps, ROUND * ROUNDS)
                dve.tensor_tensor(gt[:, :, :], score[:, :, :], limit, ALU.is_gt).then_inc(picked, 1)
                dve.tensor_tensor(eq[:, :, :], score[:, :, :], limit, ALU.is_equal).then_inc(picked, 1)
                dve.wait_ge(prefixed, 1)
                st = Steps(dve, placed, 3, 0)
                st.mark(dve.tensor_scalar(room[:, :], turn[:, 0:E1], -1.0, float(CAP), ALU.mult, ALU.add))
                st.wait()
                before = pl[:, 0:NT * E1].rearrange("p (t e) -> p t e", t=NT)
                st.mark(dve.tensor_tensor(place[:, :, :], before, wide(room[:, :], 1, NT), ALU.is_lt))
                st.wait()
                st.mark(dve.tensor_tensor(place[:, :, :], place[:, :, :], eq[:, :, :], ALU.mult))
                st.wait()
                dve.tensor_tensor(sel[:, :, :], place[:, :, :], gt[:, :, :], ALU.add).then_inc(picked, 1)
                dve.wait_ge(prefixed, 2)
                dve.wait_ge(picked, 3)
                before = pd1[:, 0:NT * E1].rearrange("p (t e) -> p t e", t=NT)
                dve.scalar_tensor_tensor(out=place[:, :, :], in0=before, scalar=1.0, in1=sel[:, :, :],
                                         op0=ALU.add, op1=ALU.mult).then_inc(place_ready, 1)
                dve.wait_ge(place_ready, 1)

                def mark_places(e, s):
                    over(dve, id_sums, e)
                    for t in range(NT):
                        ins = dve.tensor_scalar(onehot[:, t, :], m.iota1[:, :], place[:, t, bass.ds(e, 1)] if
                                                not isinstance(e, int) else place[:, t, e:e + 1], None, ALU.is_equal)
                    ins.then_inc(hot, 1)

                def take_ids(e, s):
                    dve.wait_ge(id_sums, e + 1)
                    over(dve, y_added[s], used(e, s) * 2)
                    dve.tensor_copy(ids[:, s, :], pl[:, 0:TT]).then_inc(id_ready, 1)

                def take_scores(e, s):
                    dve.wait_ge(x_gathered[s], used(e, s) * 2 + 32)
                    over(dve, y_ready, e - 1)
                    at = D + e
                    src = xg[:, s, :, bass.ds(at, 1)] if not isinstance(e, int) else xg[:, s, :, at:at + 1]
                    dve.tensor_copy(topscore[:, s, :].unsqueeze(2), src).then_inc(score_ready, 1)

                def front(e, s):
                    mark_places(e, s)
                    take_ids(e, s)
                    take_scores(e, s)

                def main(e, s, nxt, prev):
                    for i in range(KF):
                        n = KF * e + i
                        dve.wait_ge(silu_done, n + 1)
                        over(dve, down_done, e - 1)
                        dve.tensor_tensor(act_e[:, s, i, :], silu[:, i % 2, :], pgu[i % 2][:, CAP:2 * CAP],
                                          ALU.mult).then_inc(act_done, 1)
                        if i == 0 and nxt:
                            mark_places(*nxt)
                        if i == 2 and nxt:
                            take_ids(*nxt)
                        if i == 5 and nxt:
                            take_scores(*nxt)
                    dve.wait_ge(down_done, e + 1)
                    dve.wait_ge(score_ready, e + 1)
                    over(dve, y_added[s], used(e, s) * 2)
                    for h in range(TT):
                        ins = dve.tensor_scalar(y[:, s, h, :], (pd0, pd1, pd2, pd3)[2 * s + h][:, 0:D],
                                                topscore[:, s, h:h + 1], None, ALU.mult)
                    ins.then_inc(y_ready, 1)

                for k in range(2):
                    dve.wait_ge(y_stored[k], 8 * B)
                pipeline(dve, front, main, lambda e, s: None, E1)


def build(nc, a, out, stop=4):
    a = dict(a, xrows=nc.dram_tensor("xrows", (N, XROW), F32).ap())
    with ExitStack() as ctx:
        m = Memory(nc, ctx)
        sb, sem = m.sb, m.lasting_sem
        m.banks = [ctx.enter_context(nc.psum_tensor(f"bank{i}", [P, 512], F32)) for i in range(8)]
        m.h = sb("h", [P, NT, D])
        m.ids = sb("ids", [P, NT], I32)
        m.xt = sb("xt", [C, 2, KD, T])
        m.xn = sb("xn", [P, 2, TT, D])
        m.stats = sb("stats", [P, 2, TT, 6])
        m.moments = sb("moments", [P, 2, TT, 2])
        m.vareps = sb("vareps", [P, 2, TT])
        m.rstd = sb("rstd", [P, 2, TT])
        m.neg_half = sb("neg_half", [P, 2 * 9])
        m.gathers = [sem(f"gathered_{t}") for t in range(NT)]
        m.gathered = sem("gathered")
        m.gate = sem("gate_passed")
        m.loads = [[] for _ in range(5)]
        m.loaded = [sem(f"loaded_for_stage{k}") for k in range(5)]

        def load(name, shape, dt=F32, stage=None, sb=sb):
            t = sb(name, shape, dt)
            stage = m.stage if stage is None else stage
            flat = t[:] if len(shape) == 2 else t[:].rearrange(
                {3: "p a b -> p (a b)", 4: "p a b c -> p (a b c)"}[len(shape)])
            m.loads[stage].append((flat, a[name]))
            return t

        m.load = load
        m.wait_load = lambda eng, stage: eng.wait_ge(m.loaded[stage], 16 * len(m.loads[stage]))
        m.loads[0].append((m.ids[:, :], a["ids"]))
        m.stage = 1
        m.ident = load("ident", [P, P])
        m.wqT = load("wqT", [C, KD, D])
        m.wkT = load("wkT", [C, KD, D])
        m.wvT = load("wvT", [C, KD, D])
        m.head_mask = load("head_mask", [C, AHC])
        m.causal = load("causal", [P, TT, T])
        m.sum_rows = load("sum_rows", [P, C])
        m.woT = load("woT", [C, KD, D])
        m.stage = 2
        m.wrT = load("wrT", [C, KD, E0])
        m.bias8 = load("bias8", [P, TT, E0])
        m.rank8 = load("rank8", [P, TT, E0])
        m.w1 = load("w1", [C, KD, E0A * D])
        m.w2 = load("w2", [C, E0A, KD, D])
        m.stage = 3
        m.wgate = load("wgate", [C, 3 * KI, GATE_W])
        m.wq_turned = load("wq_turned", [C, KI, INNER])
        m.wk_turned = load("wk_turned", [C, KI, INNER])
        m.wv_turned = load("wv_turned", [C, KI, INNER])
        m.wup = load("wup", [C, KD, 2 * INNER])
        m.conv_w = load("conv_w", [C, KI, CONV_K])
        m.conv_b = load("conv_b", [C, KI])
        m.gate_b = load("gate_b", [GATE_W, 1])
        m.wq = load("wq", [C, KI, MG * GR])
        m.wk = load("wk", [C, KI, MG * GR])
        m.wv = load("wv", [C, KI, INNER])
        m.head_mask36 = load("head_mask36", [GR, MGH])
        m.pick_head = load("pick_head", [C, MH, P], BF16)
        m.ident_bf = load("ident_bf", [P, P], BF16)
        m.future = load("future", [P, P], BF16)
        m.skip = load("skip", [C, 1])
        m.norm_w = load("norm_w", [C, KI])
        m.wdown = load("wdown", [C, KI, D])

        taylor_attention(nc, m, None, a)
        m.end_stage()
        if stop >= 2:
            shared_and_routed_experts(nc, m)
            m.end_stage()
        if stop >= 3:
            mlstm(nc, m)
            m.end_stage()
        if stop >= 4:
            expert_choice(nc, m, a, out)
        if stop < 4:
            dump(nc, m, out)


def dump(nc, m, out):
    done = m.sem("dumped")
    with nc.Block() as block:
        @block.sync
        def _(sp):
            sp.dma_start(out.rearrange("(t p) d -> p t d", p=P), m.h[:, :, :]).then_inc(done, 16)
            sp.wait_ge(done, 16)


def host_layout(np, x, L0_tok_embed_matrix, L0_attn_Wq, L0_attn_Wk, L0_attn_Wv, L0_attn_Wo, L0_ffn_w_fc_sh,
                L0_ffn_w_proj_sh, L0_ffn_w1, L0_ffn_w2, L0_ffn_router_w, L0_ffn_balance_bias, L1_attn_W_up,
                L1_attn_conv_w, L1_attn_conv_b, L1_attn_Wq, L1_attn_Wk, L1_attn_Wv, L1_attn_Wi, L1_attn_bi,
                L1_attn_Wf, L1_attn_bf, L1_attn_norm_w, L1_attn_skip, L1_attn_W_down,
                L1_ffn_gate_weight, L1_ffn_Wg, L1_ffn_Wu, L1_ffn_Wd, L1_ffn_Ws_g, L1_ffn_Ws_u, L1_ffn_Ws_d):
    f = np.float32

    def rows(w, c=C):
        k, n = w.shape
        return np.ascontiguousarray(w.reshape(k // c, c, n).transpose(1, 0, 2).reshape(c, -1))

    p = np.arange(P)
    tok = np.arange(T)
    A = {}
    A["ids"] = np.ascontiguousarray(np.asarray(x).reshape(NT, P).T)
    A["embed"] = np.asarray(L0_tok_embed_matrix)
    A["ident"] = np.eye(P, dtype=f)
    A["wqT"] = rows(np.asarray(L0_attn_Wq).T)
    A["wkT"] = rows(np.asarray(L0_attn_Wk).T)
    A["wvT"] = rows(np.asarray(L0_attn_Wv).T)
    A["woT"] = rows(np.asarray(L0_attn_Wo).T)
    A["head_mask"] = (np.arange(C)[:, None] // AF == np.arange(AHC)[None]).astype(f)
    A["sum_rows"] = ((p[:, None] - C) == (np.arange(C)[None] // AF)).astype(f)
    A["causal"] = np.concatenate([1.0 + ((t * P + p)[:, None] <= tok[None]) for t in range(TT)], 1).astype(f)
    A["wrT"] = rows(np.asarray(L0_ffn_router_w).T)
    A["bias8"] = np.ascontiguousarray(np.broadcast_to(np.asarray(L0_ffn_balance_bias), (P, TT, E0))).reshape(P, -1)
    A["rank8"] = np.ascontiguousarray(np.broadcast_to(np.arange(E0, 0, -1, dtype=f), (P, TT, E0))).reshape(P, -1)
    w1 = np.concatenate([np.asarray(L0_ffn_w1).transpose(1, 0, 2).reshape(D, E0 * D), np.asarray(L0_ffn_w_fc_sh)], 1)
    A["w1"] = rows(w1)
    w2 = np.concatenate([np.asarray(L0_ffn_w2), np.asarray(L0_ffn_w_proj_sh)[None]], 0)
    A["w2"] = np.ascontiguousarray(w2.reshape(E0A, KD, C, D).transpose(2, 0, 1, 3)).reshape(C, -1)

    def per_channel(v):
        v = np.asarray(v).reshape(KI, C, -1)
        return np.ascontiguousarray(v.transpose(1, 0, 2)).reshape(C, -1)

    def grouped(w):
        return np.concatenate([w, np.zeros((INNER, MG * GR - INNER), f)], 1)

    gate_w = np.zeros((3 * INNER, GATE_W), f)
    gate_w[:, 0:MH] = L1_attn_Wi
    gate_w[:, 32:32 + MH] = L1_attn_Wf
    A["wgate"] = rows(gate_w)
    gate_b = np.zeros((GATE_W, 1), f)
    gate_b[0:MH, 0] = L1_attn_bi
    gate_b[32:32 + MH, 0] = L1_attn_bf
    A["gate_b"] = gate_b
    wq, wk, wv = np.asarray(L1_attn_Wq), np.asarray(L1_attn_Wk), np.asarray(L1_attn_Wv)
    A["wq_turned"], A["wk_turned"], A["wv_turned"] = rows(wq.T), rows(wk.T), rows(wv.T)
    A["wup"] = rows(np.asarray(L1_attn_W_up))
    A["conv_w"] = per_channel(L1_attn_conv_w)
    A["conv_b"] = per_channel(L1_attn_conv_b)
    A["wq"], A["wk"], A["wv"] = rows(grouped(wq)), rows(grouped(wk)), rows(wv)
    A["head_mask36"] = (np.arange(GR)[:, None] // MD == np.arange(MGH)[None]).astype(f)
    c = np.arange(C)[:, None, None]
    bf = mybir.dt.np(BF16)
    A["pick_head"] = np.ascontiguousarray(np.broadcast_to(c % 32 == np.arange(MH)[None, :, None], (C, MH, P))).astype(bf).reshape(C, -1)
    A["ident_bf"] = np.eye(P, dtype=f).astype(bf)
    A["future"] = np.where(p[:, None] > p[None], f(-1e30), f(0)).astype(bf)
    A["skip"] = np.ascontiguousarray(np.broadcast_to(np.asarray(L1_attn_skip), (C, 1)))
    A["norm_w"] = per_channel(L1_attn_norm_w)
    A["wdown"] = rows(np.asarray(L1_attn_W_down))
    A["gate1T"] = rows(np.asarray(L1_ffn_gate_weight).T)
    A["ws_gu"] = np.concatenate([rows(np.asarray(w).T) for w in (L1_ffn_Ws_g, L1_ffn_Ws_u)], 1)
    A["ws_d"] = rows(np.asarray(L1_ffn_Ws_d).T, P)
    wgu = np.stack([np.asarray(L1_ffn_Wg), np.asarray(L1_ffn_Wu)], 1).reshape(E1, 2, F1, KD, C)
    A["wgu"] = np.ascontiguousarray(wgu.transpose(0, 4, 1, 3, 2)).reshape(E1, C, -1)
    wd = np.asarray(L1_ffn_Wd).reshape(E1, D, KF, P)
    A["wd"] = np.ascontiguousarray(wd.transpose(0, 3, 2, 1)).reshape(E1, P, -1)
    A["below"] = (p[:, None] < p[None]).astype(f).astype(bf)
    A["token_id"] = (np.arange(NT)[None, :] * P + p[:, None]).astype(np.float16)
    bits = np.arange(1, 4, dtype=np.int32)[None, :, None] << np.int32(2 * ROUNDS - 2)
    A["bits"] = np.ascontiguousarray(np.broadcast_to(bits, (P, 3, E1))).astype(np.int32).reshape(P, -1)
    A["bit_value"] = np.full((P, 1), 2.0 ** (2 * ROUNDS - 2), f)
    A["iota1"] = np.ascontiguousarray(np.broadcast_to(np.arange(1, CAP + 1, dtype=f), (P, CAP))).astype(bf)
    return A


def kernel(**inputs):
    import numpy as np
    import concourse.bacc as bacc
    from concourse.bass_utils import run_bass_kernel_spmd

    nc = bacc.Bacc("TRN2", target_bir_lowering=False, num_devices=1)
    arrays = {f"in_{k}": v for k, v in host_layout(np, **inputs).items()}
    a = {k[3:]: nc.dram_tensor(k, v.shape, mybir.dt.from_np(v.dtype), kind="ExternalInput").ap()
         for k, v in arrays.items()}
    out = nc.dram_tensor("out", (N, D), F32, kind="ExternalOutput").ap()
    build(nc, a, out)
    r = run_bass_kernel_spmd(nc, [arrays], core_ids=[0])
    return np.asarray(r.results[0]["out"]).reshape(B, T, D)
```

```python
from contextlib import ExitStack

import concourse.bass as bass
from concourse import mybir

ALU = mybir.AluOpType
ACT = mybir.ActivationFunctionType
AX_X = mybir.AxisListType.X
F32 = mybir.dt.float32
BF16 = mybir.dt.bfloat16
F16 = mybir.dt.float16
F32R = mybir.dt.float32r
I32 = mybir.dt.int32

P = 128
B, T = 8, 256
N = B * T
NT = N // P
TT = T // P
D = 192
C = 96
KD = D // C
LN_EPS = 1e-5

AH, AF = 12, 16
AHC = C // AF
AOUT = C + AHC
ASTEP = AOUT + AF

E0 = 8
E0A = E0 + 1

INNER, MH, MD = 288, 8, 36
KI = INNER // C
MG, MGH = 3, 3
GR = MGH * MD
MOUT = GR + MGH
MSTEP = MOUT + MD
CONV_K = 4
GATE_W = 40
TRI = T + P

E1, F1, FS = 16, 768, 384
CAP = 256
KF, KS = F1 // P, FS // P
XROW = D + E1
ROUNDS = 15


def over(eng, sem, value):
    assert isinstance(value, int) or value.min_val >= 0
    if not isinstance(value, int) or value > 0:
        eng.wait_ge(sem, value)


def pass_gate(eng, m):
    eng.sem_inc(m.gate, 1)


class Steps:

    def __init__(self, eng, sem, per, b):
        self.eng, self.sem, self.per, self.b, self.n = eng, sem, per, b, 0

    def mark(self, ins):
        ins.then_inc(self.sem, 1)
        self.n += 1
        assert self.n <= self.per
        return self.n

    def wait(self, k=None):
        self.eng.wait_ge(self.sem, self.b * self.per + (self.n if k is None else k))

    def end(self):
        assert self.n == self.per, (self.n, self.per)


def pipeline(eng, front, main, back, n=B):
    front(0, 0)
    main(0, 0, (1, 1), None)
    main(1, 1, (2, 0), (0, 0))
    with eng.Fori(1, n // 2 - 1) as j:
        main(j * 2, 0, (j * 2 + 1, 1), (j * 2 - 1, 1))
        main(j * 2 + 1, 1, (j * 2 + 2, 0), (j * 2, 0))
    main(n - 2, 0, (n - 1, 1), (n - 3, 1))
    main(n - 1, 1, None, (n - 2, 0))
    back(n - 1, 1)


def pipeline_ahead(eng, early, late, main, back, n=B):
    early(0, 0)
    late(0, 0, (1, 1))
    main(0, 0, (1, 1), (2, 0), None)
    main(1, 1, (2, 0), (3, 1), (0, 0))
    with eng.Fori(1, n // 2 - 1) as j:
        main(j * 2, 0, (j * 2 + 1, 1), (j * 2 + 2, 0), (j * 2 - 1, 1))
        main(j * 2 + 1, 1, (j * 2 + 2, 0), (j * 2 + 3, 1), (j * 2, 0))
    main(n - 2, 0, (n - 1, 1), None, (n - 3, 1))
    main(n - 1, 1, None, None, (n - 2, 0))
    back(n - 1, 1)



def matmul_split(pe, out, lhs, rhs, start, stop):
    for i, (a, b) in enumerate(((0, 0), (1, 0), (0, 1))):
        last = pe.matmul(out, lhs[a], rhs[b], start=(start and i == 0),
                         stop=(stop and i == 2))
    return last


def tiles(h, b):
    if isinstance(b, int):
        return h[:, TT * b:TT * b + TT, :]
    return h[:, bass.ds(b * TT, TT), :]


class Norm:

    def __init__(self, m, stage):
        self.m = m
        sem = m.sem
        self.root_in = sem(f"s{stage}_variance_ready")
        self.root = sem(f"s{stage}_rstd_ready")
        self.xn = sem(f"s{stage}_xn_ready")
        self.turned = sem(f"s{stage}_xn_turned")
        self.xt_ready = sem(f"s{stage}_xt_ready")
        self.stats_steps = sem(f"s{stage}_norm_stats_steps")
        self.apply_steps = sem(f"s{stage}_norm_apply_steps")

    def dve_stats(self, dve, b, s):
        m = self.m
        st = Steps(dve, self.stats_steps, 2 * TT, b)
        h = tiles(m.h, b)
        for t in range(TT):
            st.mark(dve.bn_stats(m.stats[:, s, t, :], h[:, t, :]))
        for t in range(TT):
            st.wait(t + 1)
            pass_gate(dve, m)
            st.mark(dve.bn_aggr(m.moments[:, s, t, :], m.stats[:, s, t, :]))
        st.end()
        st.wait()
        dve.tensor_scalar(m.vareps[:, s, :], m.moments[:, s, :, 1], LN_EPS, None, ALU.add).then_inc(self.root_in, 1)

    def dve_apply(self, dve, b, s):
        m = self.m
        st = Steps(dve, self.apply_steps, TT, b)
        h = tiles(m.h, b)
        dve.wait_ge(self.root, b + 1)
        over(dve, self.turned, b - 1)
        for t in range(TT):
            st.mark(dve.tensor_scalar(m.xn[:, s, t, :], h[:, t, :], m.moments[:, s, t, 0:1], m.rstd[:, s, t:t + 1],
                                      ALU.subtract, ALU.mult))
        st.end()
        st.wait()
        dve.sem_inc(self.xn, 1)

    def dve(self, dve, b, s):
        self.dve_stats(dve, b, s)
        self.dve_apply(dve, b, s)

    def pool(self, pool, b, s):
        m = self.m
        pool.wait_ge(self.root_in, b + 1)
        pool.tensor_tensor(m.rstd[:, s, :], m.vareps[:, s, :], m.neg_half[:, 0:TT], ALU.pow).then_inc(self.root, 1)

    def pe(self, pe, b, s, bank):
        m = self.m
        pe.wait_ge(self.xn, b + 1)
        out = bank[0:C, :].rearrange("p (k n) -> p k n", k=KD)
        for t in range(TT):
            for k in range(KD):
                last = pe.transpose(out[:, k, t * P:(t + 1) * P], m.xn[:, s, t, k * C:(k + 1) * C], m.ident[:, :])
        last.then_inc(self.turned, 1)

    def act(self, act, b, s, bank, xt):
        act.wait_ge(self.turned, b + 1)
        act.activation(xt, bank[0:C, :].rearrange("p (k n) -> p k n", k=KD), ACT.Copy).then_inc(self.xt_ready, 1)


class Memory:

    def __init__(self, nc, ctx):
        self.nc, self.ctx, self.stage_sems = nc, ctx, []

    def lasting_sem(self, name):
        return self.ctx.enter_context(self.nc.semaphore(name))

    def sem(self, name):
        self.stage_sems.append(self.nc.alloc_semaphore(name))
        return self.stage_sems[-1]

    def end_stage(self):
        self.nc.clear_and_free_semaphores(self.stage_sems)
        self.nc.all_engine_barrier()
        self.stage_sems = []

    def sb(self, name, shape, dt=F32):
        return self.ctx.enter_context(self.nc.sbuf_tensor(name, shape, dt))


def taylor_attention(nc, m, a):
    sem = m.sem
    with ExitStack() as ctx:
        def sb(name, shape, dt=F32):
            return ctx.enter_context(nc.sbuf_tensor("ta_" + name, shape, dt))

        parts = sb("parts", [C, 2, 3, KD, T], BF16)
        rest = sb("rest", [C, 2, KD, T])
        qs = sb("qs", [C, 2, AH, T], BF16)
        ks = sb("ks", [C, 2, AH, T], BF16)
        VW = AH * AOUT + AHC * AF + AF
        v_diag = sb("v_diag", [P, 2, TT, VW])
        sq = sb("sq", [P, 3, TT, T])
        o_sb = sb("o_sb", [P, 2, KD, T])
        rz = sb("rz", [P, 2, KD, T])
        o_norm = sb("o_norm", [C, 2, KD, T])
        turn, pq, pk, pv, ps0, ps1, po0, po1 = m.banks
        pscore, pout = (ps0, ps1), (po0, po1)

        norm = Norm(m, 1)
        qk_proj = sem("ta_qk_projected")
        v_proj = sem("ta_v_projected")
        part0 = sem("ta_first_parts")
        rested = sem("ta_rests")
        part1 = sem("ta_second_parts")
        part2 = sem("ta_third_parts")
        parts_stored = sem("ta_parts_stored")
        qk_loaded = [sem(f"ta_qk_loaded{s}") for s in range(2)]
        v_spread = sem("ta_v_spread")
        v_clear = sem("ta_v_diag_cleared")
        scored = sem("ta_scored")
        squared = sem("ta_squared")
        weighted = sem("ta_weighted")
        summed = sem("ta_summed")
        o_copied = sem("ta_o_copied")
        z_inv = sem("ta_sums_inverted")
        z_bcast = sem("ta_sums_broadcast")
        o_normed = sem("ta_o_normed")
        projected = sem("ta_projected")
        h_added = sem("ta_h_added")

        def diag(tile, c, off, width):
            at = c * AHC * AOUT + off
            step = ASTEP if width == AF else AOUT + 1
            return tile[:, at:at + AHC * step].rearrange("p (i w) -> p i w", w=step)[:, :, 0:width]

        Q_PART, K_PART = (0, 0, 1, 0, 2, 1), (0, 1, 0, 2, 0, 1)
        LOADS = 16 * 2 * len(Q_PART)
        loaded_in_slot = lambda b, s: (b - s) * (LOADS // 2) + LOADS

        with nc.Block() as block:
            @block.sync
            def _(sp):
                def load_stage(stage):
                    for dst, src in m.loads[stage]:
                        sp.dma_start(dst, src).then_inc(m.loaded[stage], 16)

                def place_parts(b, s):
                    if not isinstance(b, int) or b > 0:
                        sp.wait_ge(qk_loaded[1 - s], (b + s) * (LOADS // 2))
                        pass_gate(sp, m)
                    for x in range(2):
                        sp.wait_ge(part2, 2 * b + x + 1)
                        sp.dma_start(a["qk_parts"][x, :, :, :].rearrange("j (k c) t -> c j k t", k=KD),
                                     parts[:, x, :, :, :]).then_inc(parts_stored, 16)
                        pass_gate(sp, m)
                    sp.wait_ge(parts_stored, 32 * (b + 1))
                    pass_gate(sp, m)
                    over(sp, scored, AH * (b - 1))
                    for x, (dst, order) in enumerate(((qs, Q_PART), (ks, K_PART))):
                        for j, part in enumerate(order):
                            sp.dma_start(dst[j * AF:(j + 1) * AF, s, :, :],
                                         a["qk_parts"][x, part, :, :].rearrange("(h f) t -> f h t", f=AF)
                                         ).then_inc(qk_loaded[s], 16)

                load_stage(0)
                load_stage(1)
                place_parts(0, 0)
                load_stage(2)
                place_parts(1, 1)
                load_stage(3)
                with sp.Fori(1, B // 2) as j:
                    place_parts(j * 2, 0)
                    place_parts(j * 2 + 1, 1)

            @block.gpsimd
            def _(pool):
                m.wait_load(pool, 0)

                def gather(first, end):
                    for t in range(first, end):
                        pool.indirect_dma_start(m.h[:, t, :], None, a["embed"][:, :],
                                                bass.IndirectOffsetOnAxis(ap=m.ids[:, t:t + 1], axis=0)
                                                ).then_inc(m.gathers[t], 16)

                def confirm(first, end):
                    for t in range(first, end):
                        pool.wait_ge(m.gathers[t], 16)
                    pool.sem_inc(m.gathered, 1)

                gather(0, 2 * TT)
                pool.wait_ge(v_clear, 1)
                confirm(0, TT)
                norm.pool(pool, 0, 0)
                gather(2 * TT, 4 * TT)
                confirm(TT, 2 * TT)

                def early(b, s):
                    norm.pool(pool, b, s)

                def split(b, s):
                    for x in range(2):
                        pool.wait_ge(part1, 2 * b + x + 1)
                        pool.tensor_tensor(parts[:, x, 2, :, :], rest[:, x, :, :], parts[:, x, 1, :, :],
                                           ALU.subtract).then_inc(part2, 1)

                def first_late(b, s, ahead):
                    split(b, s)
                    early(*ahead)
                    gather(4 * TT, NT)
                    confirm(2 * TT, NT)

                def main(b, s, nxt, ahead, prev):
                    if nxt:
                        split(*nxt)
                    if ahead:
                        early(*ahead)

                pipeline_ahead(pool, lambda b, s: None, first_late, main, lambda b, s: None)

            @block.tensor
            def _(pe):
                m.wait_load(pe, 1)

                def turn_in(b, s):
                    over(pe, o_normed, 2 * (b - 2) if not isinstance(b, int) or b > 2 else 0)
                    over(pe, norm.xt_ready, b)
                    norm.pe(pe, b, s, turn)

                def project(b, s):
                    pe.wait_ge(norm.xt_ready, b + 1)
                    over(pe, rested, 2 * b)
                    for bank, wt in ((pq, m.wqT), (pk, m.wkT)):
                        for c in range(KD):
                            for k in range(KD):
                                last = pe.matmul(bank[0:C, c * T:(c + 1) * T], wt[:, k, c * C:(c + 1) * C],
                                                 m.xt[:, s, k, :], start=(k == 0), stop=(k == KD - 1))
                        last.then_inc(qk_proj, 1)
                    over(pe, v_spread, b)
                    over(pe, h_added, b - 2 if not isinstance(b, int) or b > 2 else 0)
                    for t in range(TT):
                        for k in range(KD):
                            last = pe.matmul(pv[:, t * D:(t + 1) * D], m.xt[:, s, k, t * P:(t + 1) * P],
                                             m.wvT[:, k, :], start=(k == 0), stop=(k == KD - 1))
                    last.then_inc(v_proj, 1)

                def broadcast_sums(b, s):
                    pe.wait_ge(z_inv, b + 1)
                    over(pe, norm.xt_ready, b + 3 if not isinstance(b, int) or b < B - 2 else B)
                    for c in range(KD):
                        last = pe.matmul(turn[0:C, c * T:(c + 1) * T], m.sum_rows[C:AOUT, :], rz[C:AOUT, s, c, :],
                                         start=True, stop=True)
                    last.then_inc(z_bcast, 1)

                def out_project(b, s):
                    pe.wait_ge(o_normed, 2 * b + 2)
                    over(pe, v_spread, b + 3 if not isinstance(b, int) or b < B - 2 else B)
                    over(pe, h_added, b)
                    for t in range(TT):
                        for c in range(KD):
                            last = pe.matmul(pv[:, t * D:(t + 1) * D], o_norm[:, s, c, t * P:(t + 1) * P],
                                             m.woT[:, c, :], start=(c == 0), stop=(c == KD - 1))
                    last.then_inc(projected, 1)

                def front(b, s):
                    turn_in(b, s)
                    project(b, s)

                def back(b, s):
                    broadcast_sums(b, s)
                    out_project(b, s)

                def score(b, s, hd):
                    n = AH * b + hd
                    over(pe, squared, n - 1)
                    for t in range(TT):
                        last = pe.matmul(pscore[hd % 2][:, t * T:(t + 1) * T],
                                         ks[:, s, hd, t * P:(t + 1) * P], qs[:, s, hd, :],
                                         start=True, stop=True)
                    last.then_inc(scored, 1)

                def attend(b, s, hd):
                    c = hd // AHC
                    pe.wait_ge(weighted, AH * b + hd + 1)
                    if hd % AHC == 0:
                        over(pe, o_copied, 2 * b - 1 + c)
                    for t in range(TT):
                        last = pe.matmul(pout[c][0:AOUT, 0:T], v_diag[:, s, t, hd * AOUT:(hd + 1) * AOUT],
                                         sq[:, hd % 3, t, :], start=(hd % AHC == 0 and t == 0),
                                         stop=(hd % AHC == AHC - 1 and t == TT - 1))
                    last.then_inc(summed, 1)

                def main(b, s, nxt, prev):
                    for hd in range(AH):
                        if hd == 0:
                            pe.wait_ge(qk_loaded[s], loaded_in_slot(b, s))
                            pe.wait_ge(v_spread, b + 1)
                            pe.wait_ge(v_clear, 2 + 2 * TT * KD)
                        score(b, s, hd)
                        if hd >= 2:
                            attend(b, s, hd - 2)
                        if hd == 0 and nxt:
                            turn_in(*nxt)
                        if hd == 1 and nxt:
                            project(*nxt)
                        if hd == 4 and prev:
                            broadcast_sums(*prev)
                        if hd == 6 and prev:
                            out_project(*prev)
                    attend(b, s, AH - 2)
                    attend(b, s, AH - 1)

                pipeline(pe, front, main, back)

            @block.scalar
            def _(act):
                def copy_xt(b, s):
                    over(act, v_proj, b - 1)
                    norm.act(act, b, s, turn, m.xt[:, s, :, :])

                def first_parts(b, s):
                    over(act, parts_stored, 32 * b)
                    pass_gate(act, m)
                    for x, bank in enumerate((pq, pk)):
                        act.wait_ge(qk_proj, 2 * b + x + 1)
                        act.activation(parts[:, x, 0, :, :], bank[0:C, :].rearrange("p (c n) -> p c n", c=KD),
                                       ACT.Copy).then_inc(part0, 1)

                def second_parts(b, s):
                    for x in range(2):
                        act.wait_ge(rested, 2 * b + x + 1)
                        act.activation(parts[:, x, 1, :, :], rest[:, x, :, :], ACT.Copy).then_inc(part1, 1)

                def copy_out(b, s, c):
                    act.wait_ge(summed, AH * b + AHC * (c + 1))
                    over(act, o_normed, 2 * (b - 1))
                    act.activation(o_sb[0:AOUT, s, c, :], pout[c][0:AOUT, 0:T], ACT.Copy).then_inc(o_copied, 1)

                def front(b, s):
                    copy_xt(b, s)
                    first_parts(b, s)
                    second_parts(b, s)

                def square(b, s, hd):
                    n = AH * b + hd
                    act.wait_ge(scored, n + 1)
                    over(act, summed, n - 2)
                    act.activation(sq[:, hd % 3, :, :], pscore[hd % 2][:, :].rearrange("p (t n) -> p t n", t=TT),
                                   ACT.Square, bias=1.0, scale=0.25).then_inc(squared, 1)

                def main(b, s, nxt, prev):
                    for hd in range(AH):
                        square(b, s, hd)
                        if hd == 8:
                            copy_out(b, s, 0)
                        if hd == 0 and nxt:
                            copy_xt(*nxt)
                        if hd == 2 and nxt:
                            first_parts(*nxt)
                        if hd == 3 and nxt:
                            second_parts(*nxt)
                    copy_out(b, s, 1)

                pipeline(act, front, main, lambda b, s: None)

            @block.vector
            def _(dve):
                dve.memset(m.neg_half[:, :], -0.5).then_inc(v_clear, 1)
                dve.memset(v_diag[:, :, :, :], 0.0).then_inc(v_clear, 1)
                dve.wait_ge(v_clear, 2)
                for s in range(2):
                    for t in range(TT):
                        for c in range(KD):
                            dve.memset(diag(v_diag[:, s, t, :], c, C, 1), 1.0).then_inc(v_clear, 1)
                dve.wait_ge(m.gathered, 1)

                def spread(b, s):
                    dve.wait_ge(v_clear, 2 + 2 * TT * KD)
                    dve.wait_ge(v_proj, b + 1)
                    over(dve, summed, AH * (b - 1))
                    for t in range(TT):
                        for c in range(KD):
                            at = t * D + c * C
                            ins = dve.tensor_copy(diag(v_diag[:, s, t, :], c, 0, AF),
                                                  pv[:, at:at + C].rearrange("p (i w) -> p i w", w=AF))
                    ins.then_inc(v_spread, 1)

                def invert(b, s):
                    dve.wait_ge(o_copied, 2 * b + 2)
                    over(dve, z_bcast, b - 1)
                    dve.reciprocal(rz[C:AOUT, s, :, :], o_sb[C:AOUT, s, :, :]).then_inc(z_inv, 1)

                def normalise(b, s):
                    dve.wait_ge(z_bcast, b + 1)
                    over(dve, projected, b - 1)
                    for c in range(KD):
                        dve.tensor_tensor(o_norm[:, s, c, :], o_sb[0:C, s, c, :], turn[0:C, c * T:(c + 1) * T],
                                          ALU.mult).then_inc(o_normed, 1)

                def add(b, s):
                    dve.wait_ge(projected, b + 1)
                    h = tiles(m.h, b)
                    dve.tensor_tensor(h, h, pv[:, 0:TT * D].rearrange("p (t n) -> p t n", t=TT),
                                      ALU.add).then_inc(h_added, 1)

                def take_rest(b, s):
                    over(dve, part2, 2 * b)
                    pass_gate(dve, m)
                    for x, bank in enumerate((pq, pk)):
                        dve.wait_ge(part0, 2 * b + x + 1)
                        dve.tensor_tensor(rest[:, x, :, :], bank[0:C, :].rearrange("p (c n) -> p c n", c=KD),
                                          parts[:, x, 0, :, :], ALU.subtract).then_inc(rested, 1)

                def early(b, s):
                    norm.dve(dve, b, s)

                def late(b, s, ahead):
                    m.wait_load(dve, 1)
                    take_rest(b, s)
                    spread(b, s)
                    dve.wait_ge(m.gathered, 2)
                    early(*ahead)
                    dve.wait_ge(m.gathered, 3)

                def back(b, s):
                    invert(b, s)
                    normalise(b, s)
                    add(b, s)

                def main(b, s, nxt, ahead, prev):
                    for hd in range(AH):
                        n = AH * b + hd
                        dve.wait_ge(squared, n + 1)
                        dve.scalar_tensor_tensor(out=sq[:, hd % 3, :, :], in0=sq[:, hd % 3, :, :], scalar=1.0,
                                                 in1=m.causal[:, :, :], op0=ALU.add, op1=ALU.mult).then_inc(weighted, 1)
                        if hd == 0 and prev:
                            invert(*prev)
                        if hd == 2 and nxt:
                            take_rest(*nxt)
                        if hd == 3 and nxt:
                            spread(*nxt)
                        if hd == 4 and prev:
                            normalise(*prev)
                        if hd == 6 and prev:
                            add(*prev)
                        if hd == 7 and ahead:
                            norm.dve_stats(dve, *ahead)
                        if hd == 8 and ahead:
                            norm.dve_apply(dve, *ahead)

                pipeline_ahead(dve, early, late, main, back)


def wide(ap, axis, n):
    u = ap.unsqueeze(axis)
    shape = list(u.shape)
    shape[axis] = n
    return u.broadcast_to(shape)


def shared_and_routed_experts(nc, m):
    sem = m.sem
    with ExitStack() as ctx:
        def sb(name, shape, dt=F32):
            return ctx.enter_context(nc.sbuf_tensor("re_" + name, shape, dt))

        w1_high = sb("w1_high", [C, KD, E0A * D], F32R)
        w1_low = sb("w1_low", [C, KD, E0A * D], F32R)
        x_high = sb("x_high", [C, 2, KD, T], F32R)
        x_low = sb("x_low", [C, 2, KD, T], F32R)
        relu = sb("relu", [C, 2, KD, T])
        hid = sb("hid", [C, 2, KD, T])
        expn = sb("expn", [P, 2, TT, E0])
        score = sb("score", [P, 2, TT, E0])
        biased = sb("biased", [P, 2, TT, E0])
        found = sb("found", [P, 2, TT, E0])
        cand = sb("cand", [P, 2, TT, E0])
        pick1 = sb("pick1", [P, 2, TT, E0])
        pick2 = sb("pick2", [P, 2, TT, E0])
        best = sb("best", [P, 2, TT])
        total = sb("total", [P, 2, TT])
        comb = sb("comb", [P, 2, TT, E0])
        turn, plog, pf0, pf1, py0, py1 = m.banks[0:6]
        pfc, pproj = (pf0, pf1), (py0, py1)

        norm = Norm(m, 2)
        w_raised = sem("re_w1_high_ready")
        w_split = sem("re_w1_split")
        x_raised = sem("re_x_high_ready")
        x_split = sem("re_x_split")
        logits = sem("re_logits_ready")
        exped = sem("re_exp_ready")
        route_steps = sem("re_route_steps")
        fc_done = sem("re_fc_done")
        relu_done = sem("re_relu_done")
        hid_done = sem("re_hid_done")
        proj_done = sem("re_proj_done")
        combined = sem("re_combined")
        ORDER = [E0] + list(range(E0))
        ROUTE = 20
        PER = 1 + TT * E0

        def w1_of(i):
            at = ORDER[i] * D
            return [x[:, :, at:at + D] for x in (m.w1, w1_high, w1_low)]

        with nc.Block() as block:
            @block.gpsimd
            def _(pool):
                def front(b, s):
                    norm.pool(pool, b, s)

                def main(b, s, nxt, prev):
                    if nxt:
                        front(*nxt)

                pipeline(pool, front, main, lambda b, s: None)

            @block.tensor
            def _(pe):
                m.wait_load(pe, 2)

                def turn_in(b, s):
                    over(pe, x_raised, b)
                    norm.pe(pe, b, s, turn)

                def route(b, s):
                    pe.wait_ge(norm.xt_ready, b + 1)
                    over(pe, exped, b)
                    for t in range(TT):
                        for k in range(KD):
                            last = pe.matmul(plog[:, t * E0:(t + 1) * E0], m.xt[:, s, k, t * P:(t + 1) * P],
                                             m.wrT[:, k, :], start=(k == 0), stop=(k == KD - 1))
                    last.then_inc(logits, 1)

                def front(b, s):
                    turn_in(b, s)
                    route(b, s)

                def fc(b, s, i):
                    n = E0A * b + i
                    over(pe, relu_done, n - 1)
                    if i == 0:
                        pe.wait_ge(x_split, b + 1)
                    if isinstance(b, int) and b == 0:
                        pe.wait_ge(w_split, i + 1)
                    w, high, low = w1_of(i)
                    for c in range(KD):
                        f = slice(c * C, (c + 1) * C)
                        for k in range(KD):
                            last = matmul_split(pe, pfc[i % 2][0:C, c * T:(c + 1) * T], (high[:, k, f], low[:, k, f]),
                                                (x_high[:, s, k, :], x_low[:, s, k, :]),
                                                start=(k == 0), stop=(k == KD - 1))
                    last.then_inc(fc_done, 1)

                def proj(b, s, i):
                    pe.wait_ge(hid_done, E0A * b + i + 1)
                    over(pe, combined, PER * b + (1 + TT * (i - 2)) if i >= 2 else PER * (b - 1) + 1 + TT * (E0A + i - 3))
                    for t in range(TT):
                        for c in range(KD):
                            last = pe.matmul(pproj[i % 2][:, t * D:(t + 1) * D], hid[:, i % 2, c, t * P:(t + 1) * P],
                                             m.w2[:, ORDER[i], c, :], start=(c == 0), stop=(c == KD - 1))
                    last.then_inc(proj_done, 1)

                def main(b, s, nxt, prev):
                    for i in range(E0A):
                        fc(b, s, i)
                        if i >= 1:
                            proj(b, s, i - 1)
                        if i == 3 and nxt:
                            turn_in(*nxt)
                        if i == 5 and nxt:
                            route(*nxt)
                    proj(b, s, E0A - 1)

                pipeline(pe, front, main, lambda b, s: None)

            @block.scalar
            def _(act):
                m.wait_load(act, 2)
                for i in range(E0A):
                    w, high, low = w1_of(i)
                    act.activation(high, w, ACT.Copy).then_inc(w_raised, 1)

                def copy_xt(b, s):
                    over(act, fc_done, E0A * (b - 1))
                    norm.act(act, b, s, turn, m.xt[:, s, :, :])
                    act.activation(x_high[:, s, :, :], turn[0:C, :].rearrange("p (k n) -> p k n", k=KD),
                                   ACT.Copy).then_inc(x_raised, 1)

                def exp_logits(b, s):
                    act.wait_ge(logits, b + 1)
                    over(act, route_steps, ROUTE * (b - 1))
                    act.activation(expn[:, s, :, :], plog[:, 0:TT * E0].rearrange("p (t e) -> p t e", t=TT),
                                   ACT.Exp, scale=-1.0).then_inc(exped, 1)

                def front(b, s):
                    copy_xt(b, s)
                    exp_logits(b, s)

                def main(b, s, nxt, prev):
                    for i in range(E0A):
                        n = E0A * b + i
                        act.wait_ge(fc_done, n + 1)
                        over(act, hid_done, n - 1)
                        act.activation(relu[:, i % 2, :, :], pfc[i % 2][0:C, :].rearrange("p (c n) -> p c n", c=KD),
                                       ACT.Relu).then_inc(relu_done, 1)
                        if i == 4 and nxt:
                            copy_xt(*nxt)
                        if i == 5 and nxt:
                            exp_logits(*nxt)

                pipeline(act, front, main, lambda b, s: None)

            @block.vector
            def _(dve):
                m.wait_load(dve, 2)

                def pick(st, src, out, s):
                    st.mark(dve.tensor_reduce(best[:, s, :], src, AX_X, ALU.max))
                    st.wait()
                    st.mark(dve.tensor_tensor(found[:, s, :, :], src, wide(best[:, s, :], 2, E0), ALU.is_equal))
                    st.wait()
                    st.mark(dve.tensor_tensor(cand[:, s, :, :], found[:, s, :, :], m.rank8[:, :, :], ALU.mult))
                    st.wait()
                    st.mark(dve.tensor_reduce(best[:, s, :], cand[:, s, :, :], AX_X, ALU.max))
                    st.wait()
                    st.mark(dve.tensor_tensor(out, cand[:, s, :, :], wide(best[:, s, :], 2, E0), ALU.is_equal))
                    st.wait()

                def steps_from(b, n):
                    st = Steps(dve, route_steps, ROUTE, b)
                    st.n = n
                    if n:
                        st.wait()
                    return st

                def score_experts(b, s):
                    dve.wait_ge(exped, b + 1)
                    st = steps_from(b, 0)
                    sc, bi = score[:, s, :, :], biased[:, s, :, :]
                    st.mark(dve.tensor_scalar(sc, expn[:, s, :, :], 1.0, None, ALU.add))
                    st.wait()
                    st.mark(dve.reciprocal(sc, sc))
                    st.wait()
                    st.mark(dve.tensor_tensor(bi, sc, m.bias8[:, :, :], ALU.add))

                def pick_first(b, s):
                    st = steps_from(b, 3)
                    bi = biased[:, s, :, :]
                    pick(st, bi, pick1[:, s, :, :], s)
                    st.mark(dve.scalar_tensor_tensor(out=bi, in0=pick1[:, s, :, :], scalar=-1e30, in1=bi,
                                                     op0=ALU.mult, op1=ALU.add))

                def pick_second(b, s):
                    pick(steps_from(b, 9), biased[:, s, :, :], pick2[:, s, :, :], s)

                def weigh_experts(b, s):
                    st = steps_from(b, 14)
                    st.mark(dve.tensor_tensor(found[:, s, :, :], pick1[:, s, :, :], pick2[:, s, :, :], ALU.add))
                    st.wait()
                    st.mark(dve.tensor_tensor(found[:, s, :, :], found[:, s, :, :], score[:, s, :, :], ALU.mult))
                    st.wait()
                    st.mark(dve.tensor_reduce(total[:, s, :], found[:, s, :, :], AX_X, ALU.add))
                    st.wait()
                    st.mark(dve.tensor_scalar(total[:, s, :], total[:, s, :], 1e-20, None, ALU.add))
                    st.wait()
                    st.mark(dve.reciprocal(total[:, s, :], total[:, s, :]))
                    st.wait()
                    st.mark(dve.tensor_tensor(comb[:, s, :, :], found[:, s, :, :], wide(total[:, s, :], 2, E0), ALU.mult))
                    st.end()

                def lower_x(b, s):
                    dve.wait_ge(x_raised, b + 1)
                    dve.tensor_tensor(x_low[:, s, :, :], m.xt[:, s, :, :], x_high[:, s, :, :],
                                      ALU.subtract).then_inc(x_split, 1)

                def front(b, s):
                    norm.dve(dve, b, s)
                    for i in range(E0A):
                        dve.wait_ge(w_raised, i + 1)
                        w, high, low = w1_of(i)
                        dve.tensor_tensor(low, w, high, ALU.subtract).then_inc(w_split, 1)
                        if i == 0:
                            lower_x(b, s)
                    score_experts(b, s)
                    pick_first(b, s)
                    pick_second(b, s)
                    weigh_experts(b, s)

                def combine(b, s, i, st):
                    h = tiles(m.h, b)
                    dve.wait_ge(proj_done, E0A * b + i + 1)
                    y = pproj[i % 2][:, 0:TT * D].rearrange("p (t n) -> p t n", t=TT)
                    if i == 0:
                        st.mark(dve.tensor_tensor(h, h, y, ALU.add))
                        return
                    if i == 1:
                        dve.wait_ge(route_steps, ROUTE * (b + 1))
                    st.wait()
                    for t in range(TT):
                        st.mark(dve.scalar_tensor_tensor(out=h[:, t, :], in0=y[:, t, :],
                                                         scalar=comb[:, s, t, ORDER[i]:ORDER[i] + 1],
                                                         in1=h[:, t, :], op0=ALU.mult, op1=ALU.add))

                def main(b, s, nxt, prev):
                    st = Steps(dve, combined, PER, b)
                    for i in range(E0A):
                        n = E0A * b + i
                        dve.wait_ge(relu_done, n + 1)
                        over(dve, proj_done, n - 1)
                        dve.tensor_tensor(hid[:, i % 2, :, :], relu[:, i % 2, :, :], relu[:, i % 2, :, :],
                                          ALU.mult).then_inc(hid_done, 1)
                        if i >= 1:
                            combine(b, s, i - 1, st)
                        if i == 0 and nxt:
                            norm.dve_stats(dve, *nxt)
                        if i == 1 and nxt:
                            norm.dve_apply(dve, *nxt)
                        if i == 5 and nxt:
                            lower_x(*nxt)
                        if i == 6 and nxt:
                            score_experts(*nxt)
                            pick_first(*nxt)
                        if i == 7 and nxt:
                            pick_second(*nxt)
                        if i == 8 and nxt:
                            weigh_experts(*nxt)
                    combine(b, s, E0A - 1, st)
                    st.end()

                pipeline(dve, front, main, lambda b, s: None)


def mlstm(nc, m):
    sem = m.sem
    with ExitStack() as ctx:
        def sb(name, shape, dt=F32):
            return ctx.enter_context(nc.sbuf_tensor("ml_" + name, shape, dt))

        XP = CONV_K - 1 + T
        xm = sb("xm", [C, 2, KI, XP])
        xc = sb("xc", [C, KI, T])
        xconv = sb("xconv", [C, 2, KI, T])
        turned = [m.w_turned[:, i, :].rearrange("p (k n) -> p k n", k=KI) for i in range(3)]
        reused = m.w_turned[:, :, :].rearrange("p a n -> p (a n)")
        skipped = reused[:, 0:2 * KI * T].rearrange("p (s k n) -> p s k n", s=2, k=KI)
        gated = reused[:, 2 * KI * T:3 * KI * T].rearrange("p (k n) -> p k n", k=KI)
        x_high = sb("x_high", [C, KD, T], F32R)
        x_low = sb("x_low", [C, KD, T], F32R)
        xconv_high = sb("xconv_high", [C, KI, T], F32R)
        xconv_low = sb("xconv_low", [C, KI, T], F32R)
        wup_high = sb("wup_high", [C, KD, 2 * INNER], F32R)
        wup_low = sb("wup_low", [C, KD, 2 * INNER], F32R)
        wqk_high = sb("wqk_high", [C, 2, KI, MG * GR], F32R)
        wqk_low = sb("wqk_low", [C, 2, KI, MG * GR], F32R)
        z = sb("z", [C, 2, KI, T])
        zact = sb("zact", [C, 2, KI, T])
        qT = sb("qT", [GR, MG, T])
        kT = sb("kT", [GR, 2, MG, T])
        qm = sb("qm", [GR, 2, MH, T])
        v_diag = sb("v_diag", [P, 2, TT, MH * MOUT + MOUT + 1])
        gw = sb("gw", [C, 2, KI, GATE_W])
        gates = sb("gates", [GATE_W, T])
        nabs = sb("nabs", [GATE_W, T])
        lnf = sb("lnf", [GATE_W, T])
        ones = sb("ones", [GATE_W, T])
        cs = sb("cs", [MH, T])
        top = sb("top", [MH, T])
        rest1 = sb("rest1", [MH, T])
        rest2 = sb("rest2", [MH, T])
        mid = sb("mid", [MH, T], BF16)
        mld = sb("mld", [MH, T])
        parts = sb("parts", [C, 2, T], BF16)
        rows = sb("rows", [64, 2, T])
        cols = sb("cols", [P, 2, TT, 64])
        decay = sb("decay", [P, 3, TRI])
        ct = sb("ct", [P, 3, TRI])
        ot = sb("ot", [MOUT, 2, MG, T])
        den = sb("den", [P, TT, 9])
        rden = sb("rden", [P, TT, 9])
        hn = sb("hn", [P, TT, 9, MD])
        hc = sb("hc", [P, TT, 9, MD])
        hsq = sb("hsq", [P, TT, 9, MD])
        hsum = sb("hsum", [P, TT, 9])
        hvar = sb("hvar", [P, TT * 9])
        hrstd = sb("hrstd", [P, TT * 9])
        hln = sb("hln", [P, TT, INNER])
        misc, w0, w1, pa0, pa1, ps0, ps1, po = m.banks
        parg, pscore = (pa0, pa1), (ps0, ps1)

        norm = Norm(m, 3)
        setup = sem("ml_setup")
        gw_made = sem("ml_gate_weights_made")
        gw_copied = sem("ml_gate_weights_copied")
        w_raised = sem("ml_weights_high_ready")
        w_split = sem("ml_weights_split")
        x_raised = sem("ml_x_high_ready")
        x_split = sem("ml_x_split")
        xconv_raised = sem("ml_xconv_high_ready")
        xconv_split = sem("ml_xconv_split")
        up_done = sem("ml_up_done")
        x_copied = sem("ml_x_copied")
        z_copied = sem("ml_z_copied")
        conv_steps = sem("ml_conv_steps")
        x_act = sem("ml_x_activated")
        z_act = sem("ml_z_activated")
        x_skip = sem("ml_x_skipped")
        gates_done = sem("ml_gates_projected")
        gate_steps = sem("ml_gate_steps")
        f_abs = sem("ml_f_abs")
        f_exp = sem("ml_f_exp")
        f_ln = sem("ml_f_ln")
        mld_ready = sem("ml_max_log_d_ready")
        e_ready = sem("ml_floor_ready")
        parts_ready = sem("ml_parts_ready")
        rows_turned = sem("ml_rows_turned")
        cols_ready = sem("ml_cols_ready")
        qk_done = sem("ml_qk_projected")
        q_copied = sem("ml_q_copied")
        k_copied = sem("ml_k_copied")
        q_masked = sem("ml_q_masked")
        v_done = sem("ml_v_projected")
        v_spread = sem("ml_v_spread")
        argued = sem("ml_args_ready")
        scored = sem("ml_scored")
        decayed = sem("ml_decayed")
        weighted = sem("ml_weighted")
        summed = sem("ml_summed")
        o_copied = sem("ml_o_copied")
        o_turned = sem("ml_o_turned")
        head_steps = sem("ml_head_norm_steps")
        head_var = sem("ml_head_var")
        head_rstd = sem("ml_head_rstd")
        hln_ready = sem("ml_head_norm_ready")
        hln_turned = sem("ml_head_norm_turned")
        out_steps = sem("ml_out_steps")
        gated_ready = sem("ml_gated_ready")
        down_done = sem("ml_down_done")
        h_added = sem("ml_h_added")
        CONV, GATE, HEAD, OUTS = KI * CONV_K, 10, 13, KI
        SETUP = 8

        to_split = ((m.wup[:, :, :], wup_high[:, :, :], wup_low[:, :, :]),
                    (m.wq[:, :, :], wqk_high[:, 0, :, :], wqk_low[:, 0, :, :]),
                    (m.wk[:, :, :], wqk_high[:, 1, :, :], wqk_low[:, 1, :, :]))

        def diag(tile, g, off, width):
            heads = min(MGH, MH - g * MGH)
            at = g * MGH * MOUT + off
            step = MSTEP if width == MD else MOUT + 1
            return tile[:, at:at + heads * step].rearrange("p (i w) -> p i w", w=step)[:, :, 0:width]

        with nc.Block() as block:
            @block.gpsimd
            def _(pool):
                pool.memset(v_diag[:, :, :, :], 0.0).then_inc(setup, 1)
                pool.memset(xm[:, :, :, 0:CONV_K - 1], 0.0).then_inc(setup, 1)
                pool.memset(parts[:, :, :], 0.0).then_inc(setup, 1)
                pool.memset(rows[:, :, :], 0.0).then_inc(setup, 1)
                pool.memset(ones[:, :], 1.0).then_inc(setup, 1)
                pool.wait_ge(setup, 5)
                for s in range(2):
                    for t in range(TT):
                        for g in range(MG):
                            pool.memset(diag(v_diag[:, s, t, :], g, GR, 1), 1.0).then_inc(setup, 1)
                m.wait_load(pool, 3)

                def skip(b, s):
                    pool.wait_ge(x_act, b + 1)
                    over(pool, out_steps, OUTS * (b - 1))
                    pass_gate(pool, m)
                    pool.tensor_scalar(skipped[:, s, :, :], xconv[:, s, :, :], m.skip[:, 0:1], 1.0,
                                       ALU.mult, ALU.mult).then_inc(x_skip, 1)

                def mask(b, s):
                    pool.wait_ge(q_copied, b + 1)
                    over(pool, scored, MH * (b - 1))
                    pass_gate(pool, m)
                    for hd in range(MH):
                        ins = pool.tensor_scalar(qm[:, s, hd, :], qT[:, hd // MGH, :],
                                                 m.head_mask36[:, hd % MGH:hd % MGH + 1], 1.0, ALU.mult, ALU.mult)
                    ins.then_inc(q_masked, 1)

                def early(b, s):
                    norm.pool(pool, b, s)

                def late(b, s, ahead):
                    skip(b, s)
                    early(*ahead)
                    mask(b, s)

                def back(b, s):
                    pool.wait_ge(head_var, b + 1)
                    pool.tensor_tensor(hrstd[:, :], hvar[:, :], m.neg_half[:, 0:TT * 9], ALU.pow).then_inc(head_rstd, 1)

                def main(b, s, nxt, ahead, prev):
                    if prev:
                        back(*prev)
                    if nxt:
                        skip(*nxt)
                    if ahead:
                        early(*ahead)
                    if nxt:
                        mask(*nxt)

                pipeline_ahead(pool, early, late, main, back)

            @block.tensor
            def _(pe):
                m.wait_load(pe, 3)
                for part, weights in enumerate((turned[0:2], turned[2:3])):
                    for i in range(KI):
                        o = w0[0:C, (part * KI + i) * GATE_W:(part * KI + i + 1) * GATE_W]
                        n = len(weights) * KI
                        for j in range(n):
                            wt, k = weights[j // KI], j % KI
                            row = (2 * KI if part else 0) + j
                            last = pe.matmul(o, wt[:, k, i * C:(i + 1) * C], m.wgate[:, row, :],
                                             start=(j == 0), stop=(j == n - 1))
                last.then_inc(gw_made, 1)

                def turn_in(b, s):
                    over(pe, q_copied, b)
                    over(pe, h_added, b - 2 if not isinstance(b, int) or b > 2 else 0)
                    norm.pe(pe, b, s, misc)

                def up(b, s):
                    pe.wait_ge(x_split, b + 1)
                    over(pe, v_spread, b)
                    if isinstance(b, int) and b == 0:
                        pe.wait_ge(gw_copied, 1)
                        pe.wait_ge(w_split, 1)
                    for pair, bank in enumerate((w0, w1, misc)):
                        for j in range(2):
                            i = 2 * pair + j
                            f = slice(i * C, (i + 1) * C)
                            for k in range(KD):
                                last = matmul_split(pe, bank[0:C, j * T:(j + 1) * T],
                                                    (wup_high[:, k, f], wup_low[:, k, f]),
                                                    (x_high[:, k, :], x_low[:, k, :]),
                                                    start=(k == 0), stop=(k == KD - 1))
                        last.then_inc(up_done, 1)

                def gate_proj(b, s):
                    pe.wait_ge(x_act, b + 1)
                    pe.wait_ge(z_copied, 2 * b + 2)
                    over(pe, cols_ready, b)
                    for j in range(2 * KI):
                        part, i = j // KI, j % KI
                        rhs = xm[:, s, i, CONV_K - 1:XP] if part else xconv[:, s, i, :]
                        last = pe.matmul(misc[0:GATE_W, 0:T], gw[:, part, i, :], rhs,
                                         start=(j == 0), stop=(j == 2 * KI - 1))
                    last.then_inc(gates_done, 1)

                def qk(b, s, between=None):
                    for pair, bank in enumerate((misc, w0, w1)):
                        if pair == 0:
                            pe.wait_ge(gate_steps, GATE * b + 1)
                            pe.wait_ge(xconv_split, b + 1)
                            if isinstance(b, int) and b == 0:
                                pe.wait_ge(w_split, 3)
                        if pair == 1:
                            if between:
                                between()
                            over(pe, out_steps, OUTS * (b - 1))
                        for j in range(2):
                            g = (2 * pair + j) % MG
                            wt = (2 * pair + j) // MG
                            f = slice(g * GR, (g + 1) * GR)
                            for i in range(KI):
                                last = matmul_split(pe, bank[0:GR, j * T:(j + 1) * T],
                                                    (wqk_high[:, wt, i, f], wqk_low[:, wt, i, f]),
                                                    (xconv_high[:, i, :], xconv_low[:, i, :]),
                                                    start=(i == 0), stop=(i == KI - 1))
                        last.then_inc(qk_done, 1)

                def v(b, s):
                    pe.wait_ge(k_copied, b + 1)
                    for t, bank in enumerate((w0, w1)):
                        at = CONV_K - 1 + t * P
                        for i in range(KI):
                            last = pe.matmul(bank[:, 0:INNER], xm[:, s, i, at:at + P], m.wv[:, i, :],
                                             start=(i == 0), stop=(i == KI - 1))
                    last.then_inc(v_done, 1)

                def turn_rows(b, s):
                    pe.wait_ge(e_ready, b + 1)
                    pe.wait_ge(gate_steps, GATE * b + GATE)
                    pe.wait_ge(z_copied, 2 * b + 4 if not isinstance(b, int) or b < B - 1 else 2 * B)
                    over(pe, h_added, b - 1)
                    pass_gate(pe, m)
                    for t in range(TT):
                        last = pe.transpose(misc[:, t * 64:(t + 1) * 64], rows[:, s, t * P:(t + 1) * P], m.ident[0:64, 0:64])
                    last.then_inc(rows_turned, 1)

                def turn_out(b, s):
                    pe.wait_ge(o_copied, MG * (b + 1))
                    pe.wait_ge(z_copied, 2 * b + 5 if not isinstance(b, int) or b < B - 2 else 2 * B)
                    over(pe, out_steps, OUTS * b)
                    for t, bank in enumerate((w0, w1)):
                        for g in range(MG):
                            last = pe.transpose(bank[:, g * MOUT:(g + 1) * MOUT], ot[:, s, g, t * P:(t + 1) * P],
                                                m.ident[0:MOUT, 0:MOUT])
                    last.then_inc(o_turned, 1)

                def turn_back(b, s):
                    pe.wait_ge(hln_ready, b + 1)
                    for i in range(KI):
                        for t in range(TT):
                            o = (w0 if i < 2 else w1)[0:C, (i % 2) * T + t * P:(i % 2) * T + (t + 1) * P]
                            last = pe.transpose(o, hln[:, t, i * C:(i + 1) * C], m.ident[:, :])
                    last.then_inc(hln_turned, 1)

                def down(b, s):
                    pe.wait_ge(gated_ready, b + 1)
                    pe.wait_ge(q_copied, b + 3 if not isinstance(b, int) or b < B - 2 else B)
                    over(pe, h_added, b)
                    for t in range(TT):
                        for i in range(KI):
                            last = pe.matmul(misc[:, t * D:(t + 1) * D], gated[:, i, t * P:(t + 1) * P],
                                             m.wdown[:, i, :], start=(i == 0), stop=(i == KI - 1))
                    last.then_inc(down_done, 1)

                def early(b, s):
                    turn_in(b, s)
                    up(b, s)

                def late(b, s, ahead):
                    gate_proj(b, s)
                    qk(b, s)
                    v(b, s)
                    early(*ahead)
                    turn_rows(b, s)

                def back(b, s):
                    turn_out(b, s)
                    turn_back(b, s)
                    down(b, s)

                def argue(b, s, hd):
                    n = MH * b + hd
                    over(pe, decayed, 2 * (n - 1))
                    o = parg[hd % 2]
                    pe.matmul(o[:, 0:T], m.pick_head[:, hd, :], parts[:, s, :], start=True, stop=False,
                              skip_group_check=True)
                    pe.matmul(o[:, T:TRI], m.pick_head[:, hd, :], parts[:, s, P:T], start=False, stop=False,
                              skip_group_check=True)
                    pe.matmul(o[:, 0:P], m.ident_bf[:, :], m.future[:, :], start=False, stop=False,
                              skip_group_check=True)
                    pe.matmul(o[:, T:TRI], m.ident_bf[:, :], m.future[:, :], start=False, stop=True,
                              skip_group_check=True).then_inc(argued, 1)

                def score(b, s, hd):
                    n = MH * b + hd
                    over(pe, weighted, n - 1)
                    g = hd // MGH
                    pe.matmul(pscore[hd % 2][:, 0:T], kT[:, s, g, 0:P], qm[:, s, hd, :], start=True, stop=True)
                    pe.matmul(pscore[hd % 2][:, T:TRI], kT[:, s, g, P:T], qm[:, s, hd, P:T],
                              start=True, stop=True).then_inc(scored, 1)

                def attend(b, s, hd):
                    g = hd // MGH
                    pe.wait_ge(weighted, MH * b + hd + 1)
                    if hd % MGH == 0:
                        over(pe, o_copied, MG * b + g)
                    end = hd % MGH == MGH - 1 or hd == MH - 1
                    va = v_diag[:, s, :, hd * MOUT:(hd + 1) * MOUT]
                    pe.matmul(po[0:MOUT, 0:T], va[:, 0, :], ct[:, hd % 3, 0:T], start=(hd % MGH == 0), stop=False,
                              skip_group_check=True)
                    pe.matmul(po[0:MOUT, P:T], va[:, 1, :], ct[:, hd % 3, T:TRI], start=False, stop=end,
                              skip_group_check=True).then_inc(summed, 1)

                def main(b, s, nxt, ahead, prev):
                    pe.wait_ge(q_masked, b + 1)
                    pe.wait_ge(cols_ready, b + 1)
                    pe.wait_ge(parts_ready, b + 1)
                    pe.wait_ge(v_spread, b + 1)
                    pe.wait_ge(setup, 5 + 2 * TT * MG)
                    for hd in range(MH):
                        argue(b, s, hd)
                        score(b, s, hd)
                        if hd >= 2:
                            attend(b, s, hd - 2)
                        if hd == 0 and prev:
                            turn_out(*prev)
                        if hd == 3 and nxt:
                            gate_proj(*nxt)
                        if hd == 4 and prev and not nxt:
                            turn_back(*prev)
                        if hd == 4 and nxt:
                            qk(*nxt, between=(lambda: turn_back(*prev)) if prev else None)
                        if hd == 5 and nxt:
                            v(*nxt)
                        if hd == 5 and prev:
                            down(*prev)
                        if hd == 6 and ahead:
                            turn_in(*ahead)
                        if hd == 7 and ahead:
                            up(*ahead)
                    attend(b, s, MH - 2)
                    attend(b, s, MH - 1)
                    if nxt:
                        turn_rows(*nxt)

                pipeline_ahead(pe, early, late, main, back)

            @block.scalar
            def _(act):
                act.wait_ge(gw_made, 1)
                act.activation(gw[:, :, :, :], w0[0:C, 0:2 * KI * GATE_W].rearrange("p (a b c) -> p a b c", a=2, b=KI),
                               ACT.Copy).then_inc(gw_copied, 1)

                m.wait_load(act, 3)
                for w, high, low in to_split:
                    act.activation(high, w, ACT.Copy).then_inc(w_raised, 1)

                def pair(bank, rows_, n=2):
                    return bank[0:rows_, 0:n * T].rearrange("p (j n) -> p j n", j=n)

                def copy_up(b, s):
                    over(act, v_done, b - 1)
                    act.wait_ge(up_done, 3 * b + 1)
                    act.activation(xm[:, s, 0:2, CONV_K - 1:XP], pair(w0, C), ACT.Copy)
                    act.wait_ge(up_done, 3 * b + 2)
                    act.activation(xm[:, s, 2, CONV_K - 1:XP], w1[0:C, 0:T], ACT.Copy).then_inc(x_copied, 1)
                    over(act, z_act, b - 1)
                    act.activation(z[:, s, 0, :], w1[0:C, T:2 * T], ACT.Copy).then_inc(z_copied, 1)
                    act.wait_ge(up_done, 3 * b + 3)
                    act.activation(z[:, s, 1:3, :], pair(misc, C), ACT.Copy).then_inc(z_copied, 1)

                def activate_x(b, s):
                    act.wait_ge(conv_steps, CONV * (b + 1))
                    over(act, x_skip, b - 1)
                    over(act, qk_done, 3 * (b - 1))
                    act.activation(xconv[:, s, :, :], xc[:, :, :], ACT.Silu).then_inc(x_act, 1)

                def raise_xconv(b, s):
                    act.wait_ge(x_act, b + 1)
                    over(act, qk_done, 3 * b)
                    act.activation(xconv_high[:, :, :], xconv[:, s, :, :], ACT.Copy).then_inc(xconv_raised, 1)

                def activate_z(b, s):
                    act.wait_ge(z_copied, 2 * b + 2)
                    over(act, gated_ready, b - 1)
                    act.activation(zact[:, s, :, :], z[:, s, :, :], ACT.Silu).then_inc(z_act, 1)

                def copy_qk(b, s):
                    over(act, q_masked, b)
                    act.wait_ge(qk_done, 3 * b + 1)
                    act.activation(qT[:, 0:2, :], pair(misc, GR), ACT.Copy)
                    act.wait_ge(qk_done, 3 * b + 2)
                    act.activation(qT[:, 2, :], w0[0:GR, 0:T], ACT.Copy).then_inc(q_copied, 1)
                    over(act, scored, MH * (b - 1))
                    act.activation(kT[:, s, 0, :], w0[0:GR, T:2 * T], ACT.Copy, scale=MD ** -0.5)
                    act.wait_ge(qk_done, 3 * b + 3)
                    act.activation(kT[:, s, 1:3, :], pair(w1, GR), ACT.Copy, scale=MD ** -0.5).then_inc(k_copied, 1)

                def log_forget(b, s):
                    act.wait_ge(f_abs, b + 1)
                    act.activation(lnf[32:GATE_W, :], nabs[32:GATE_W, :], ACT.Exp).then_inc(f_exp, 1)
                    act.wait_ge(f_exp, b + 1)
                    act.activation(lnf[32:GATE_W, :], lnf[32:GATE_W, :], ACT.Ln, bias=1.0).then_inc(f_ln, 1)

                def floor(b, s):
                    act.wait_ge(mld_ready, b + 1)
                    over(act, rows_turned, b - 1)
                    act.activation(rows[32:GATE_W, s, :], mld[:, :], ACT.Exp, scale=-1.0).then_inc(e_ready, 1)

                def copy_cols(b, s):
                    act.wait_ge(rows_turned, b + 1)
                    over(act, head_steps, HEAD * (b - 1))
                    act.activation(cols[:, s, :, :], misc[:, 0:TT * 64].rearrange("p (t n) -> p t n", t=TT),
                                   ACT.Copy).then_inc(cols_ready, 1)

                def copy_xt(b, s):
                    over(act, up_done, 3 * b)
                    act.wait_ge(norm.turned, b + 1)
                    act.activation(x_high[:, :, :], pair(misc, C), ACT.Copy).then_inc(x_raised, 1)

                def early(b, s):
                    copy_xt(b, s)
                    copy_up(b, s)

                def late(b, s, ahead):
                    activate_x(b, s)
                    raise_xconv(b, s)
                    log_forget(b, s)
                    copy_qk(b, s)
                    floor(b, s)
                    early(*ahead)
                    copy_cols(b, s)

                def decays(b, s, hd):
                    n = MH * b + hd
                    act.wait_ge(argued, n + 1)
                    over(act, weighted, n - 2)
                    act.activation(decay[:, hd % 3, 0:T], parg[hd % 2][:, 0:T], ACT.Exp,
                                   bias=cols[:, s, 0, hd:hd + 1]).then_inc(decayed, 1)
                    act.activation(decay[:, hd % 3, T:TRI], parg[hd % 2][:, T:TRI], ACT.Exp,
                                   bias=cols[:, s, 1, hd:hd + 1]).then_inc(decayed, 1)

                def copy_out(b, s, g):
                    act.wait_ge(summed, MH * b + min(MGH * (g + 1), MH))
                    over(act, o_turned, b - 1)
                    act.activation(ot[:, s, g, :], po[0:MOUT, 0:T], ACT.Copy).then_inc(o_copied, 1)

                def main(b, s, nxt, ahead, prev):
                    act.wait_ge(cols_ready, b + 1)
                    for hd in range(MH):
                        decays(b, s, hd)
                        if hd == 1 and nxt:
                            activate_x(*nxt)
                        if hd == 1:
                            activate_z(b, s)
                        if hd == 1 and nxt:
                            raise_xconv(*nxt)
                        if hd == 3 and nxt:
                            log_forget(*nxt)
                        if hd == 4:
                            copy_out(b, s, 0)
                        if hd == 4 and nxt:
                            copy_qk(*nxt)
                        if hd == 5 and nxt:
                            floor(*nxt)
                        if hd == 7:
                            copy_out(b, s, 1)
                        if hd == 6 and ahead:
                            copy_xt(*ahead)
                        if hd == 7 and ahead:
                            copy_up(*ahead)
                    copy_out(b, s, 2)
                    if nxt:
                        copy_cols(*nxt)

                pipeline_ahead(act, early, late, main, lambda b, s: None)

            @block.vector
            def _(dve):
                m.wait_load(dve, 3)
                dve.wait_ge(setup, 5 + 2 * TT * MG)

                def lower_weights():
                    for i, (w, high, low) in enumerate(to_split):
                        dve.wait_ge(w_raised, i + 1)
                        dve.tensor_tensor(low, w, high, ALU.subtract).then_inc(w_split, 1)

                def lower_x(b, s):
                    dve.wait_ge(x_raised, b + 1)
                    dve.tensor_tensor(x_low[:, :, :], misc[0:C, :].rearrange("p (k n) -> p k n", k=KD),
                                      x_high[:, :, :], ALU.subtract).then_inc(x_split, 1)

                def lower_xconv(b, s):
                    dve.wait_ge(xconv_raised, b + 1)
                    dve.tensor_tensor(xconv_low[:, :, :], xconv[:, s, :, :], xconv_high[:, :, :],
                                      ALU.subtract).then_inc(xconv_split, 1)

                def conv(b, s):
                    dve.wait_ge(x_copied, b + 1)
                    over(dve, x_act, b)
                    st = Steps(dve, conv_steps, CONV, b)
                    for j in range(CONV_K):
                        for i in range(KI):
                            src = xm[:, s, i, j:j + T]
                            if j == 0:
                                st.mark(dve.tensor_scalar(xc[:, i, :], src, m.conv_w[:, i, j:j + 1],
                                                          m.conv_b[:, i:i + 1], ALU.mult, ALU.add))
                            else:
                                st.wait(st.n - KI + 1)
                                st.mark(dve.scalar_tensor_tensor(out=xc[:, i, :], in0=src,
                                                                 scalar=m.conv_w[:, i, j:j + 1], in1=xc[:, i, :],
                                                                 op0=ALU.mult, op1=ALU.add))
                    st.end()

                def gate_logs(b, s):
                    dve.wait_ge(gates_done, b + 1)
                    st = Steps(dve, gate_steps, GATE, b)
                    st.mark(dve.tensor_scalar(gates[:, :], misc[0:GATE_W, 0:T], m.gate_b[:, 0:1], None, ALU.add))
                    st.wait()
                    f = gates[32:GATE_W, :]
                    dve.scalar_tensor_tensor(out=nabs[32:GATE_W, :], in0=f, scalar=-1.0, in1=f, op0=ALU.mult,
                                             op1=ALU.min).then_inc(f_abs, 1)
                    return st

                def gate_scans(b, s):
                    st = Steps(dve, gate_steps, GATE, b)
                    st.n = 1
                    f = gates[32:GATE_W, :]
                    dve.wait_ge(f_ln, b + 1)
                    st.mark(dve.scalar_tensor_tensor(out=lnf[32:GATE_W, :], in0=f, scalar=0.0, in1=lnf[32:GATE_W, :],
                                                     op0=ALU.min, op1=ALU.subtract))
                    st.wait()
                    st.mark(dve.tensor_tensor_scan(cs[:, :], ones[32:GATE_W, :], lnf[32:GATE_W, :], 0.0,
                                                   ALU.mult, ALU.add))
                    st.wait()
                    over(dve, rows_turned, b - 1)
                    a = rows[0:MH, s, :]
                    st.mark(dve.tensor_tensor(a, gates[0:MH, :], cs[:, :], ALU.subtract))
                    st.wait()
                    st.mark(dve.tensor_tensor_scan(top[:, :], a, a, -3e38, ALU.max, ALU.max))
                    st.wait()
                    over(dve, e_ready, b)
                    st.mark(dve.tensor_tensor(mld[:, :], cs[:, :], top[:, :], ALU.add))
                    st.wait()
                    dve.tensor_scalar(mld[:, :], mld[:, :], -87.0, None, ALU.max).then_inc(mld_ready, 1)
                    over(dve, argued, MH * (b - 1))
                    st.mark(dve.tensor_scalar(parts[0:MH, s, :], top[:, :], -1.0, None, ALU.mult))
                    st.wait()
                    st.mark(dve.scalar_tensor_tensor(out=rest1[:, :], in0=top[:, :], scalar=-1.0,
                                                     in1=parts[0:MH, s, :], op0=ALU.mult, op1=ALU.subtract))
                    st.wait()
                    dve.tensor_copy(parts[32:32 + MH, s, :], rest1[:, :])
                    st.mark(dve.tensor_copy(mid[:, :], rest1[:, :]))
                    st.wait()
                    st.mark(dve.tensor_tensor(rest2[:, :], rest1[:, :], mid[:, :], ALU.subtract))
                    st.wait()
                    dve.tensor_copy(parts[64:64 + MH, s, :], rest2[:, :]).then_inc(parts_ready, 1)
                    st.end()

                def spread(b, s):
                    dve.wait_ge(v_done, b + 1)
                    over(dve, summed, MH * (b - 1))
                    for t, bank in enumerate((w0, w1)):
                        for g in range(MG):
                            cols_ = min(GR, INNER - g * GR)
                            ins = dve.tensor_copy(diag(v_diag[:, s, t, :], g, 0, MD),
                                                  bank[:, g * GR:g * GR + cols_].rearrange("p (i w) -> p i w", w=MD))
                    ins.then_inc(v_spread, 1)

                def head_stats(b, s):
                    dve.wait_ge(o_turned, b + 1)
                    st = Steps(dve, head_steps, HEAD, b)
                    for t, bank in enumerate((w0, w1)):
                        raw = bank[:, 0:MG * MOUT].rearrange("p (g w) -> p g w", g=MG)
                        st.mark(dve.scalar_tensor_tensor(
                            out=den[:, t, :].rearrange("p (g i) -> p g i", g=MG), in0=raw[:, :, GR:MOUT], scalar=-1.0,
                            in1=cols[:, s, t, 32:41].rearrange("p (g i) -> p g i", g=MG),
                            op0=ALU.mult, op1=ALU.max))
                    for t, bank in enumerate((w0, w1)):
                        raw = bank[:, 0:MG * MOUT].rearrange("p (g w) -> p g w", g=MG)
                        st.wait(t + 1)
                        d = den[:, t, :].rearrange("p (g i) -> p g i", g=MG)
                        st.mark(dve.tensor_tensor(d, raw[:, :, GR:MOUT], d, ALU.max))
                    st.wait()
                    st.mark(dve.tensor_scalar(den[:, :, :], den[:, :, :], 1e-6, None, ALU.add))
                    st.wait()
                    st.mark(dve.reciprocal(rden[:, :, :], den[:, :, :]))
                    st.wait()
                    for t, bank in enumerate((w0, w1)):
                        raw = bank[:, 0:MG * MOUT].rearrange("p (g w) -> p g w", g=MG)[:, :, 0:GR]
                        st.mark(dve.tensor_tensor(hn[:, t, :, :].rearrange("p (g i) c -> p g i c", g=MG),
                                                  raw.rearrange("p g (i c) -> p g i c", c=MD),
                                                  wide(rden[:, t, :].rearrange("p (g i) -> p g i", g=MG), 3, MD),
                                                  ALU.mult))

                def head_center(b, s):
                    st = Steps(dve, head_steps, HEAD, b)
                    st.n = 8
                    st.wait()
                    st.mark(dve.tensor_reduce(hsum[:, :, :], hn[:, :, :, :], AX_X, ALU.add))
                    st.wait()
                    flat = lambda x: x[:, :, :, :].rearrange("p t g c -> p (t g) c")
                    st.mark(dve.scalar_tensor_tensor(
                        out=flat(hc), in0=wide(hsum[:, :, :].rearrange("p t g -> p (t g)"), 2, MD), scalar=-1.0 / MD,
                        in1=flat(hn), op0=ALU.mult, op1=ALU.add))
                    st.wait()
                    st.mark(dve.tensor_tensor(flat(hsq), flat(hc), flat(hc), ALU.mult))
                    st.wait()
                    st.mark(dve.tensor_reduce(hsum[:, :, :], hsq[:, :, :, :], AX_X, ALU.add))
                    st.wait()
                    dve.tensor_scalar(hvar[:, :], hsum[:, :, :].rearrange("p t g -> p (t g)"), 1.0 / MD, LN_EPS,
                                      ALU.mult, ALU.add).then_inc(head_var, 1)

                def head_scale(b, s):
                    st = Steps(dve, head_steps, HEAD, b)
                    st.n = HEAD - 1
                    dve.wait_ge(head_rstd, b + 1)
                    over(dve, hln_turned, b)
                    rs = hrstd[:, :].rearrange("p (t g) -> p t g", t=TT)[:, :, 0:MH]
                    st.mark(dve.tensor_tensor(hln[:, :, :].rearrange("p t (g c) -> p t g c", c=MD),
                                              hc[:, :, 0:MH, :], wide(rs, 3, MD), ALU.mult))
                    st.end()
                    st.wait()
                    dve.sem_inc(hln_ready, 1)

                def gate_out(b, s):
                    dve.wait_ge(hln_turned, b + 1)
                    dve.wait_ge(x_skip, b + 1)
                    dve.wait_ge(z_act, b + 1)
                    over(dve, down_done, b)
                    st = Steps(dve, out_steps, OUTS, b)
                    for i in range(KI):
                        src = (w0 if i < 2 else w1)[0:C, (i % 2) * T:(i % 2 + 1) * T]
                        st.mark(dve.scalar_tensor_tensor(out=gated[:, i, :], in0=src, scalar=m.norm_w[:, i:i + 1],
                                                         in1=skipped[:, s, i, :], op0=ALU.mult, op1=ALU.add))
                    st.end()
                    st.wait()
                    dve.tensor_tensor(gated[:, :, :], gated[:, :, :], zact[:, s, :, :], ALU.mult).then_inc(gated_ready, 1)

                def add(b, s):
                    dve.wait_ge(down_done, b + 1)
                    h = tiles(m.h, b)
                    dve.tensor_tensor(h, h, misc[:, 0:TT * D].rearrange("p (t n) -> p t n", t=TT),
                                      ALU.add).then_inc(h_added, 1)

                def early(b, s):
                    norm.dve(dve, b, s)
                    if b == 0:
                        lower_weights()
                    lower_x(b, s)
                    conv(b, s)

                def late(b, s, ahead):
                    lower_xconv(b, s)
                    gate_logs(b, s)
                    gate_scans(b, s)
                    spread(b, s)
                    early(*ahead)

                def back(b, s):
                    head_stats(b, s)
                    head_center(b, s)
                    head_scale(b, s)
                    gate_out(b, s)
                    add(b, s)

                def main(b, s, nxt, ahead, prev):
                    for hd in range(MH):
                        n = MH * b + hd
                        dve.wait_ge(decayed, 2 * n + 2)
                        dve.wait_ge(scored, n + 1)
                        over(dve, summed, n - 2)
                        dve.tensor_tensor(ct[:, hd % 3, :], pscore[hd % 2][:, 0:TRI], decay[:, hd % 3, :],
                                          ALU.mult).then_inc(weighted, 1)
                        if hd == 0 and prev:
                            head_stats(*prev)
                        if hd == 1 and prev:
                            head_center(*prev)
                        if hd == 3 and nxt:
                            gate_logs(*nxt)
                        if hd == 2 and nxt:
                            lower_xconv(*nxt)
                        if hd == 3 and prev:
                            head_scale(*prev)
                        if hd == 3 and prev:
                            gate_out(*prev)
                        if hd == 4 and nxt:
                            gate_scans(*nxt)
                        if hd == 4 and ahead:
                            norm.dve_stats(dve, *ahead)
                        if hd == 5 and ahead:
                            norm.dve_apply(dve, *ahead)
                        if hd == 5 and prev:
                            add(*prev)
                        if hd == 6 and nxt:
                            spread(*nxt)
                        if hd == 6 and ahead:
                            lower_x(*ahead)
                        if hd == 7 and ahead:
                            conv(*ahead)
                pipeline_ahead(dve, early, late, main, back)


def expert_choice(nc, m, a, out):
    sem = m.sem
    ROWS = out.rearrange("(t p) d -> p t d", p=P)
    XROWS = a["xrows"].rearrange("(t p) d -> p t d", p=P)
    with ExitStack() as ctx:
        def sb(name, shape, dt=F32):
            return ctx.enter_context(nc.sbuf_tensor("ec_" + name, shape, dt))

        xt_all = sb("xt_all", [C, KD, N])
        expn = sb("expn", [P, 2, TT, E1])
        srow = sb("srow", [P, 2, TT, E1])
        score = sb("score", [P, NT, E1])
        thr = sb("thr", [P, E1], I32)
        trial = sb("trial", [P, 3, E1], I32)
        above = sb("above", [P, NT, 3, E1], BF16)
        enough = sb("enough", [P, 3, E1])
        passed = sb("passed", [P, E1])
        grow = sb("grow", [P, E1], I32)
        gt = sb("gt", [P, NT, E1], BF16)
        eq = sb("eq", [P, NT, E1], BF16)
        sel = sb("sel", [P, NT, E1], BF16)
        room = sb("room", [P, E1])
        place = sb("place", [P, NT, E1])
        ones = sb("ones", [P, P], BF16)
        onehot = sb("onehot", [P, NT, CAP], BF16)
        gather_ids = sb("gather_ids", [P, 2, TT], I32)
        ids = sb("ids", [P, 2, TT], I32)
        xg = sb("xg", [P, 2, TT, XROW])
        topscore = sb("topscore", [P, 2, TT])
        xgt_high = sb("xgt_high", [C, 2, KD, CAP], F32R)
        xgt_low = sb("xgt_low", [C, 2, KD, CAP], F32R)
        wgu = sb("wgu", [C, 2, 2, KD, F1])
        wgu_high = sb("wgu_high", [C, 2, KD, F1], F32R)
        wgu_low = sb("wgu_low", [C, 2, KD, F1], F32R)
        wd = sb("wd", [P, 2, KF, D])
        silu = sb("silu", [P, 2, T])
        act_e = sb("act_e", [P, 2, KF, CAP])
        act_s = act_e[:, :, 0:KS, :]
        y = sb("y", [P, 2, TT, D])
        turn, pl, pg0, pg1, pd0, pd1, pd2, pd3 = m.banks
        pgu = (pg0, pg1)

        m.gate1T = m.load("gate1T", [C, KD, E1], stage=4, sb=sb)
        ws_flat = wgu[:, 1, :, :, :].rearrange("p a k f -> p (a k f)")[:, 0:2 * KD * FS]
        m.ws_gu = ws_flat.rearrange("p (a k f) -> p a k f", a=2, k=KD)
        m.loads[4].append((ws_flat, a["ws_gu"]))
        m.ws_d = m.load("ws_d", [P, KS, D], stage=4, sb=sb)
        m.below = m.load("below", [P, P], BF16, stage=4, sb=sb)
        m.token_id = m.load("token_id", [P, NT, 1], F16, stage=4, sb=sb)
        m.bits = m.load("bits", [P, 3, E1], I32, stage=4, sb=sb)
        m.bit_value = m.load("bit_value", [P, 1], stage=4, sb=sb)
        m.iota1 = m.load("iota1", [P, CAP], BF16, stage=4, sb=sb)

        norm = Norm(m, 4)
        setup = sem("ec_setup")
        logits = sem("ec_logits")
        exped = sem("ec_exp_ready")
        score_steps = sem("ec_score_steps")
        scored = sem("ec_scored")
        xt_kept = sem("ec_xt_kept")
        x_stored = [sem(f"ec_x_stored{s}") for s in range(2)]
        s_stored = [sem(f"ec_scores_stored{s}") for s in range(2)]
        sh_gu = sem("ec_shared_gate_up")
        sh_silu = sem("ec_shared_silu")
        sh_act = sem("ec_shared_act")
        sh_down = sem("ec_shared_down")
        sh_y = sem("ec_shared_y")
        y_stored = [sem(f"ec_y_stored{s}") for s in range(2)]
        compared = sem("ec_compared")
        counted = sem("ec_counted")
        round_steps = sem("ec_round_steps")
        bit_scaled = sem("ec_bit_scaled")
        place_ready = sem("ec_place_ready")
        picked = sem("ec_picked")
        prefixed = sem("ec_prefixed")
        placed = sem("ec_placed")
        hot = sem("ec_onehot_ready")
        id_sums = sem("ec_id_sums")
        id_ready = sem("ec_ids_ready")
        ids_kept = sem("ec_ids_kept")
        x_gathered = [sem(f"ec_gathered{s}") for s in range(2)]
        xg_turned = sem("ec_xg_turned")
        score_ready = sem("ec_topscore_ready")
        x_high = sem("ec_x_high")
        x_split = sem("ec_x_split")
        w_high = sem("ec_w_high")
        w_split, w_split_pool = sem("ec_w_split"), sem("ec_w_split_pool")
        gu_done = sem("ec_gate_up")
        silu_done = sem("ec_silu")
        act_done = sem("ec_act")
        down_done = sem("ec_down")
        y_ready = sem("ec_y_ready")
        y_added = [sem(f"ec_y_added{s}") for s in range(2)]
        wgu_in = [sem(f"ec_wgu_loaded{s}") for s in range(2)]
        wd_in = [sem(f"ec_wd_loaded{s}") for s in range(2)]
        SCORE = 2
        ON_POOL = (1, 5)
        ON_DVE = [i for i in range(KF) if i not in ON_POOL]
        TURN = 3
        AHEAD = KF // 2
        ROUND = 6
        used = lambda b, s: (b - s) * 8

        def weights_of(s, i):
            f = slice(i * P, (i + 1) * P)
            return wgu[:, s, :, :, f], wgu_high[:, :, :, f], wgu_low[:, :, :, f]

        def by_pairs(eng, body, n):
            with eng.Fori(0, n // 2) as j:
                body(j * 2, 0)
                body(j * 2 + 1, 1)

        def rounds_of(b):
            return 1 if isinstance(b, int) and b == B - 1 else 2

        with nc.Block() as block:
            @block.sync
            def _(sp):
                def load_gate_up(e, s):
                    wg_src = a["wgu"][bass.ds(e, 1), :, :] if not isinstance(e, int) else a["wgu"][e:e + 1, :, :]
                    sp.dma_start(wgu[:, s, :, :, :].rearrange("p a k f -> p (a k f)"),
                                 wg_src.rearrange("e p f -> p (e f)")).then_inc(wgu_in[s], 16)

                def load_down(e, s):
                    wd_src = a["wd"][bass.ds(e, 1), :, :] if not isinstance(e, int) else a["wd"][e:e + 1, :, :]
                    sp.dma_start(wd[:, s, :, :].rearrange("p k d -> p (k d)"),
                                 wd_src.rearrange("e p f -> p (e f)")).then_inc(wd_in[s], 16)

                def store_x(b, s):
                    sp.wait_ge(norm.xn, b + 1)
                    sp.dma_start(tiles(XROWS, b)[:, :, 0:D], m.xn[:, s, :, :]).then_inc(x_stored[s], 16)

                def store_scores(b, s):
                    sp.wait_ge(scored, b + 1)
                    sp.dma_start(tiles(XROWS, b)[:, :, D:XROW], srow[:, s, :, :]).then_inc(s_stored[s], 16)

                def store_y(b, s):
                    sp.wait_ge(sh_y, b + 1)
                    sp.dma_start(tiles(ROWS, b), y[:, s, :, :]).then_inc(y_stored[s], 16)

                for dst, src in m.loads[4]:
                    sp.dma_start(dst, src).then_inc(m.loaded[4], 16)

                def store_rows(b, s, nxt, prev):
                    if nxt:
                        store_x(*nxt)
                    if prev:
                        store_scores(*prev)

                pipeline(sp, store_x, store_rows, store_scores)
                load_gate_up(0, 0)
                load_down(0, 0)
                load_down(1, 1)
                by_pairs(sp, store_y, B)
                load_gate_up(1, 1)

                def refill(e, s):
                    sp.wait_ge(w_split, len(ON_DVE) * (e + 1))
                    pass_gate(sp, m)
                    sp.wait_ge(w_split_pool, len(ON_POOL) * (e + 1))
                    load_gate_up(e + 2, s)
                    sp.wait_ge(down_done, e + 1)
                    load_down(e + 2, s)

                by_pairs(sp, refill, E1 - 2)

            @block.gpsimd
            def _(pool):
                pool.memset(thr[:, :], 0).then_inc(setup, 1)
                pool.memset(ones[:, :], 1.0).then_inc(setup, 1)

                by_pairs(pool, lambda b, s: norm.pool(pool, b, s), B)

                def gather(e, s):
                    pool.wait_ge(id_ready, e + 1)
                    if isinstance(e, int) and e == 0:
                        for k in range(2):
                            pool.wait_ge(x_stored[k], 8 * B)
                            pool.wait_ge(s_stored[k], 8 * B)
                    over(pool, xg_turned, e - 1)
                    over(pool, score_ready, e - 1)
                    pass_gate(pool, m)
                    for t in range(TT):
                        pool.indirect_dma_start(xg[:, s, t, :], None, a["xrows"][:, :],
                                                bass.IndirectOffsetOnAxis(ap=gather_ids[:, s, t:t + 1], axis=0)
                                                ).then_inc(x_gathered[s], 16)

                def scatter(e, s):
                    pool.wait_ge(y_ready, e + 1)
                    pool.wait_ge(ids_kept, e + 1)
                    if isinstance(e, int) and e == 0:
                        for k in range(2):
                            pool.wait_ge(y_stored[k], 8 * B)
                    else:
                        pool.wait_ge(y_added[1 - s], (e + s) * 16)
                    pass_gate(pool, m)
                    for t in range(TT):
                        pool.indirect_dma_start(out[:, :], bass.IndirectOffsetOnAxis(ap=ids[:, s, t:t + 1], axis=0),
                                                y[:, s, t, :], None, compute_op=ALU.add).then_inc(y_added[s], 16)

                def lower_weights(e, s, i):
                    pool.wait_ge(w_high, KF * e + i + 1)
                    w_, high, low = weights_of(s, i)
                    pool.tensor_tensor(low, w_, high, ALU.subtract).then_inc(w_split_pool, 1)

                def front(e, s):
                    gather(e, s)
                    lower_weights(e, s, 1)

                def main(e, s, nxt, prev):
                    if nxt:
                        gather(*nxt)
                    lower_weights(e, s, 5)
                    if nxt:
                        lower_weights(*nxt, 1)
                    scatter(e, s)

                pipeline(pool, front, main, lambda e, s: None, E1)
                for s in range(2):
                    pool.wait_ge(y_added[s], 16 * E1)

            @block.tensor
            def _(pe):
                def turn_x(b, s):
                    over(pe, xt_kept, b)
                    norm.pe(pe, b, s, turn)

                def choose(b, s):
                    pe.wait_ge(norm.xt_ready, b + 1)
                    over(pe, exped, b)
                    for t in range(TT):
                        for k in range(KD):
                            last = pe.matmul(pl[:, t * E1:(t + 1) * E1], m.xt[:, s, k, t * P:(t + 1) * P],
                                             m.gate1T[:, k, :], start=(k == 0), stop=(k == KD - 1))
                    last.then_inc(logits, 1)

                def turn_and_choose(b, s, nxt, prev):
                    if nxt:
                        turn_x(*nxt)
                    choose(b, s)

                def turn_first(b, s):
                    turn_x(b, s)
                    m.wait_load(pe, 4)
                    pe.wait_ge(setup, 2)

                pipeline(pe, turn_first, turn_and_choose, lambda b, s: None)

                def count(r):
                    pe.wait_ge(compared, r + 1)
                    for t in range(NT):
                        last = pe.matmul(turn[:, 0:3 * E1], ones[:, :], above[:, t, :, :],
                                         start=(t == 0), stop=(t == NT - 1))
                    last.then_inc(counted, 1)

                def shared(b, s, nxt, prev):
                    at = b * T
                    pe.wait_ge(xt_kept, b + 1)
                    for i in range(KS):
                        n = KS * b + i
                        over(pe, sh_act, n - 1)
                        for part in range(2):
                            for k in range(KD):
                                rhs = xt_all[:, k, bass.ds(at, T)] if not isinstance(b, int) else xt_all[:, k, at:at + T]
                                last = pe.matmul(pgu[(i + s) % 2][:, part * T:(part + 1) * T],
                                                 m.ws_gu[:, part, k, i * P:(i + 1) * P], rhs,
                                                 start=(k == 0), stop=(k == KD - 1))
                        last.then_inc(sh_gu, 1)
                        if i < rounds_of(b):
                            count(2 * b + i)
                        if i == 0 and prev:
                            shared_down(*prev)

                def shared_down(b, s):
                    pe.wait_ge(sh_act, KS * (b + 1))
                    over(pe, sh_y, b)
                    for t in range(TT):
                        for k in range(KS):
                            last = pe.matmul(pd0[:, t * D:(t + 1) * D], act_s[:, s, k, t * P:(t + 1) * P],
                                             m.ws_d[:, k, :], start=(k == 0), stop=(k == KS - 1))
                    last.then_inc(sh_down, 1)

                pipeline(pe, lambda b, s: None, shared, shared_down)

                def prefix(bank, src):
                    flat = src[:, :, :].rearrange("p t e -> p (t e)")
                    pe.matmul(bank[:, 0:NT * E1], m.below[:, :], flat, start=True, stop=False, skip_group_check=True)
                    for t in range(NT - 1):
                        last = pe.matmul(bank[:, (t + 1) * E1:NT * E1], ones[:, :], wide(src[:, t, :], 1, NT - 1 - t),
                                         start=False, stop=(t == NT - 2), skip_group_check=True)
                    return last

                pe.wait_ge(picked, 2)
                for t in range(NT):
                    pe.matmul(turn[:, 0:E1], ones[:, :], gt[:, t, :], start=(t == 0), stop=(t == NT - 1))
                prefix(pl, eq).then_inc(prefixed, 1)
                pe.wait_ge(picked, 3)
                prefix(pd1, sel).then_inc(prefixed, 1)

                def find(e, s):
                    pe.wait_ge(hot, e + 1)
                    over(pe, id_ready, e)
                    for h in range(TT):
                        for t in range(NT):
                            last = pe.matmul(pl[:, h:h + 1], onehot[:, t, h * P:(h + 1) * P], m.token_id[:, t, :],
                                             start=(t == 0), stop=(t == NT - 1))
                    last.then_inc(id_sums, 1)

                def turn_in(e, s):
                    pe.wait_ge(x_gathered[s], used(e, s) * 2 + 32)
                    over(pe, x_split, e)
                    for h in range(TT):
                        for k in range(KD):
                            last = pe.transpose(turn[0:C, k * CAP + h * P:k * CAP + (h + 1) * P],
                                                xg[:, s, h, k * C:(k + 1) * C], m.ident[:, :])
                    last.then_inc(xg_turned, 1)

                def front(e, s):
                    find(e, s)
                    turn_in(e, s)
                    gate_up(e, s, 0)

                def gate_up(e, s, i):
                    n = KF * e + i
                    if i == 0:
                        pe.wait_ge(x_split, e + 1)
                    over(pe, act_done, n - 1)
                    if i in ON_POOL:
                        pe.wait_ge(w_split_pool, len(ON_POOL) * e + ON_POOL.index(i) + 1)
                    else:
                        pe.wait_ge(w_split, len(ON_DVE) * e + ON_DVE.index(i) + 1)
                    for part in range(2):
                        for k in range(KD):
                            f = slice(i * P, (i + 1) * P)
                            last = matmul_split(pe, pgu[i % 2][:, part * CAP:(part + 1) * CAP],
                                                (wgu_high[:, part, k, f], wgu_low[:, part, k, f]),
                                                (xgt_high[:, s, k, :], xgt_low[:, s, k, :]),
                                                start=(k == 0), stop=(k == KD - 1))
                    last.then_inc(gu_done, 1)

                def down(e, s, i):
                    pe.wait_ge(act_done, KF * e + i + 1)
                    if i == 0:
                        pe.wait_ge(wd_in[s], used(e, s) + 16)
                        over(pe, y_ready, e - 1)
                    for h in range(TT):
                        last = pe.matmul((pd0, pd1, pd2, pd3)[2 * s + h][:, 0:D], act_e[:, s, i, h * P:(h + 1) * P],
                                         wd[:, s, i, :], start=(i == 0), stop=(i == KF - 1))
                    if i == KF - 1:
                        last.then_inc(down_done, 1)

                def main(e, s, nxt, prev):
                    for i in range(KF):
                        if i >= 1:
                            gate_up(e, s, i)
                            down(e, s, i - 1)
                        if i == 0 and nxt:
                            find(*nxt)
                        if i == TURN and nxt:
                            turn_in(*nxt)
                    if nxt:
                        gate_up(*nxt, 0)
                    down(e, s, KF - 1)

                pipeline(pe, front, main, lambda e, s: None, E1)

            @block.scalar
            def _(act):
                def copy_xt(b, s):
                    over(act, logits, b - 1)
                    norm.act(act, b, s, turn, m.xt[:, s, :, :])
                    at = b * T
                    dst = xt_all[:, :, bass.ds(at, T)] if not isinstance(b, int) else xt_all[:, :, at:at + T]
                    act.activation(dst, turn[0:C, :].rearrange("p (k n) -> p k n", k=KD), ACT.Copy).then_inc(xt_kept, 1)

                def choose(b, s):
                    act.wait_ge(logits, b + 1)
                    over(act, scored, b - 1)
                    act.activation(expn[:, s, :, :], pl[:, 0:TT * E1].rearrange("p (t e) -> p t e", t=TT),
                                   ACT.Exp, scale=-1.0).then_inc(exped, 1)

                def copy_and_choose(b, s, nxt, prev):
                    if nxt:
                        copy_xt(*nxt)
                    choose(b, s)

                pipeline(act, copy_xt, copy_and_choose, lambda b, s: None)

                def shared(b, s):
                    for i in range(KS):
                        n = KS * b + i
                        act.wait_ge(sh_gu, n + 1)
                        over(act, sh_act, n - 1)
                        act.activation(silu[:, (i + s) % 2, :], pgu[(i + s) % 2][:, 0:T], ACT.Silu).then_inc(sh_silu, 1)

                shared(0, 0)
                shared(1, 1)
                with act.Fori(1, B // 2) as j:
                    shared(j * 2, 0)
                    shared(j * 2 + 1, 1)

                def raise_weights(e, s, i):
                    act.wait_ge(wgu_in[s], used(e, s) + 16)
                    over(act, gu_done, KF * (e - 1) + i + 1 if not isinstance(e, int) or e > 0 else 0)
                    w_, high, low = weights_of(s, i)
                    act.activation(high, w_, ACT.Copy).then_inc(w_high, 1)

                def front(e, s):
                    for i in range(AHEAD):
                        raise_weights(e, s, i)
                    raise_x(e, s)

                def raise_x(e, s):
                    act.wait_ge(xg_turned, e + 1)
                    over(act, gu_done, KF * (e - 1))
                    act.activation(xgt_high[:, s, :, :], turn[0:C, :].rearrange("p (k n) -> p k n", k=KD),
                                   ACT.Copy).then_inc(x_high, 1)

                def main(e, s, nxt, prev):
                    for i in range(KF):
                        n = KF * e + i
                        act.wait_ge(gu_done, n + 1)
                        over(act, act_done, n - 1)
                        act.activation(silu[:, i % 2, :], pgu[i % 2][:, 0:CAP], ACT.Silu).then_inc(silu_done, 1)
                        if i == TURN and nxt:
                            raise_x(*nxt)
                        if i < KF - AHEAD:
                            raise_weights(e, s, i + AHEAD)
                        elif nxt:
                            raise_weights(*nxt, i + AHEAD - KF)
                    act.wait_ge(down_done, e + 1)
                    act.wait_ge(score_ready, e + 1)
                    over(act, y_added[s], used(e, s) * 2)
                    pass_gate(act, m)
                    for h in range(TT):
                        ins = act.activation(y[:, s, h, :], (pd0, pd1, pd2, pd3)[2 * s + h][:, 0:D], ACT.Copy,
                                             scale=topscore[:, s, h:h + 1])
                    ins.then_inc(y_ready, 1)

                act.wait_ge(sh_act, KS * B)
                for k in range(2):
                    act.wait_ge(y_stored[k], 8 * B)
                pipeline(act, front, main, lambda e, s: None, E1)

            @block.vector
            def _(dve):
                def apply(b, s):
                    over(dve, x_stored[s], used(b, s))
                    norm.dve_apply(dve, b, s)

                def choose(b, s):
                    dve.wait_ge(exped, b + 1)
                    st = Steps(dve, score_steps, SCORE, b)
                    over(dve, s_stored[s], used(b, s))
                    st.mark(dve.tensor_scalar(expn[:, s, :, :], expn[:, s, :, :], 1.0, None, ALU.add))
                    st.wait()
                    st.mark(dve.reciprocal(srow[:, s, :, :], expn[:, s, :, :]))
                    st.end()
                    st.wait()
                    dve.tensor_copy(tiles(score, b), srow[:, s, :, :]).then_inc(scored, 1)

                def early(b, s):
                    norm.dve_stats(dve, b, s)

                def late(b, s, ahead):
                    apply(b, s)
                    norm.dve_stats(dve, *ahead)

                def normalise_and_choose(b, s, nxt, ahead, prev):
                    if nxt:
                        apply(*nxt)
                    if ahead:
                        norm.dve_stats(dve, *ahead)
                    if prev:
                        choose(*prev)

                pipeline_ahead(dve, early, late, normalise_and_choose, choose)
                m.wait_load(dve, 4)
                dve.wait_ge(setup, 2)

                def try_bits(r):
                    st = Steps(dve, round_steps, ROUND, r)
                    if isinstance(r, int) and r == 0:
                        dve.wait_ge(scored, B)
                    else:
                        dve.wait_ge(round_steps, ROUND * r)
                    st.mark(dve.tensor_tensor(trial[:, :, :], wide(thr[:, :], 1, 3),
                                              m.bits[:, :, :], ALU.bitwise_or))
                    st.wait()
                    over(dve, counted, r)
                    dve.tensor_tensor(above[:, :, :, :], wide(score[:, :, :], 2, 3),
                                      wide(trial[:, :, :].bitcast(F32), 1, NT), ALU.is_ge).then_inc(compared, 1)

                def take_bits(r):
                    st = Steps(dve, round_steps, ROUND, r)
                    st.n = 1
                    dve.wait_ge(counted, r + 1)
                    cnt = turn[:, 0:3 * E1].rearrange("p (j e) -> p j e", j=3)
                    st.mark(dve.tensor_scalar(enough[:, :, :], cnt, float(CAP), None, ALU.is_ge))
                    st.mark(dve.tensor_scalar(m.bits[:, :, :], m.bits[:, :, :], 2, None, ALU.logical_shift_right))
                    st.wait(2)
                    st.mark(dve.tensor_reduce(passed[:, :], enough[:, :, :].rearrange("p j e -> p e j"), AX_X, ALU.add))
                    st.wait()
                    st.mark(dve.tensor_scalar(grow[:, :], passed[:, :], m.bit_value[:, 0:1], None, ALU.mult))
                    st.wait()
                    dve.tensor_scalar(m.bit_value[:, :], m.bit_value[:, :], 0.25, None, ALU.mult).then_inc(bit_scaled, 1)
                    st.mark(dve.tensor_tensor(thr[:, :], thr[:, :], grow[:, :], ALU.bitwise_or))
                    st.end()
                    dve.wait_ge(bit_scaled, r + 1)

                def multiply(b, s, i):
                    n = KS * b + i
                    dve.wait_ge(sh_silu, n + 1)
                    over(dve, sh_down, b - 1)
                    dve.tensor_tensor(act_s[:, s, i, :], silu[:, (i + s) % 2, :], pgu[(i + s) % 2][:, T:2 * T],
                                      ALU.mult).then_inc(sh_act, 1)

                def shared(b, s, nxt, prev):
                    for i in range(KS):
                        if i < rounds_of(b):
                            try_bits(2 * b + i)
                        multiply(b, s, i)
                        if i < rounds_of(b):
                            take_bits(2 * b + i)
                        if i == 1 and prev:
                            sum_up(*prev)

                def sum_up(b, s):
                    dve.wait_ge(sh_down, b + 1)
                    over(dve, y_stored[s], used(b, s))
                    dve.tensor_tensor(y[:, s, :, :], tiles(m.h, b), pd0[:, 0:TT * D].rearrange("p (t n) -> p t n", t=TT),
                                      ALU.add).then_inc(sh_y, 1)

                pipeline(dve, lambda b, s: None, shared, sum_up)

                limit = wide(thr[:, :].bitcast(F32), 1, NT)
                dve.wait_ge(round_steps, ROUND * ROUNDS)
                dve.tensor_tensor(gt[:, :, :], score[:, :, :], limit, ALU.is_gt).then_inc(picked, 1)
                dve.tensor_tensor(eq[:, :, :], score[:, :, :], limit, ALU.is_equal).then_inc(picked, 1)
                dve.wait_ge(prefixed, 1)
                st = Steps(dve, placed, 3, 0)
                st.mark(dve.tensor_scalar(room[:, :], turn[:, 0:E1], -1.0, float(CAP), ALU.mult, ALU.add))
                st.wait()
                before = pl[:, 0:NT * E1].rearrange("p (t e) -> p t e", t=NT)
                st.mark(dve.tensor_tensor(place[:, :, :], before, wide(room[:, :], 1, NT), ALU.is_lt))
                st.wait()
                st.mark(dve.tensor_tensor(place[:, :, :], place[:, :, :], eq[:, :, :], ALU.mult))
                st.wait()
                dve.tensor_tensor(sel[:, :, :], place[:, :, :], gt[:, :, :], ALU.add).then_inc(picked, 1)
                dve.wait_ge(prefixed, 2)
                dve.wait_ge(picked, 3)
                before = pd1[:, 0:NT * E1].rearrange("p (t e) -> p t e", t=NT)
                dve.scalar_tensor_tensor(out=place[:, :, :], in0=before, scalar=1.0, in1=sel[:, :, :],
                                         op0=ALU.add, op1=ALU.mult).then_inc(place_ready, 1)
                dve.wait_ge(place_ready, 1)

                def mark_places(e, s):
                    over(dve, id_sums, e)
                    for t in range(NT):
                        ins = dve.tensor_scalar(onehot[:, t, :], m.iota1[:, :], place[:, t, bass.ds(e, 1)] if
                                                not isinstance(e, int) else place[:, t, e:e + 1], None, ALU.is_equal)
                    ins.then_inc(hot, 1)

                def take_ids(e, s):
                    dve.wait_ge(id_sums, e + 1)
                    dve.tensor_copy(gather_ids[:, s, :], pl[:, 0:TT]).then_inc(id_ready, 1)

                def take_scores(e, s):
                    dve.wait_ge(x_gathered[s], used(e, s) * 2 + 32)
                    over(dve, y_ready, e - 1)
                    at = D + e
                    src = xg[:, s, :, bass.ds(at, 1)] if not isinstance(e, int) else xg[:, s, :, at:at + 1]
                    dve.tensor_copy(topscore[:, s, :].unsqueeze(2), src).then_inc(score_ready, 1)

                def keep_ids(e, s):
                    dve.wait_ge(id_ready, e + 1)
                    over(dve, y_added[s], used(e, s) * 2)
                    dve.tensor_copy(ids[:, s, :], gather_ids[:, s, :]).then_inc(ids_kept, 1)

                def lower_weights(e, s, i):
                    if i in ON_DVE:
                        dve.wait_ge(w_high, KF * e + i + 1)
                        w_, high, low = weights_of(s, i)
                        dve.tensor_tensor(low, w_, high, ALU.subtract).then_inc(w_split, 1)

                def lower_x(e, s):
                    dve.wait_ge(x_high, e + 1)
                    dve.tensor_tensor(xgt_low[:, s, :, :], turn[0:C, :].rearrange("p (k n) -> p k n", k=KD),
                                      xgt_high[:, s, :, :], ALU.subtract).then_inc(x_split, 1)

                def late(e, s, ahead):
                    take_ids(e, s)
                    mark_places(*ahead)
                    for i in range(AHEAD):
                        lower_weights(e, s, i)
                    keep_ids(e, s)
                    take_scores(e, s)
                    lower_x(e, s)

                def main(e, s, nxt, ahead, prev):
                    for i in range(KF):
                        n = KF * e + i
                        dve.wait_ge(silu_done, n + 1)
                        over(dve, down_done, e - 1)
                        dve.tensor_tensor(act_e[:, s, i, :], silu[:, i % 2, :], pgu[i % 2][:, CAP:2 * CAP],
                                          ALU.mult).then_inc(act_done, 1)
                        if i == 0 and nxt:
                            take_ids(*nxt)
                        if i == TURN + 1 and nxt:
                            take_scores(*nxt)
                            lower_x(*nxt)
                            keep_ids(*nxt)
                        if i < KF - AHEAD:
                            lower_weights(e, s, i + AHEAD)
                        elif nxt:
                            lower_weights(*nxt, i + AHEAD - KF)
                        if i == 2 and ahead:
                            mark_places(*ahead)

                pipeline_ahead(dve, mark_places, late, main, lambda e, s: None, E1)


def build(nc, a, out, stop=4):
    a = dict(a, xrows=nc.dram_tensor("xrows", (N, XROW), F32).ap(),
             qk_parts=nc.dram_tensor("qk_parts", (2, 3, D, T), BF16).ap())
    with ExitStack() as ctx:
        m = Memory(nc, ctx)
        sb, sem = m.sb, m.lasting_sem
        m.banks = [ctx.enter_context(nc.psum_tensor(f"bank{i}", [P, 512], F32)) for i in range(8)]
        m.h = sb("h", [P, NT, D])
        m.ids = sb("ids", [P, NT], I32)
        m.xt = sb("xt", [C, 2, KD, T])
        m.xn = sb("xn", [P, 2, TT, D])
        m.stats = sb("stats", [P, 2, TT, 6])
        m.moments = sb("moments", [P, 2, TT, 2])
        m.vareps = sb("vareps", [P, 2, TT])
        m.rstd = sb("rstd", [P, 2, TT])
        m.neg_half = sb("neg_half", [P, 2 * 9])
        m.gathers = [sem(f"gathered_{t}") for t in range(NT)]
        m.gathered = sem("gathered")
        m.gate = sem("gate_passed")
        m.loads = [[] for _ in range(5)]
        m.loaded = [sem(f"loaded_for_stage{k}") for k in range(5)]

        def load(name, shape, dt=F32, stage=None, sb=sb):
            t = sb(name, shape, dt)
            stage = m.stage if stage is None else stage
            flat = t[:] if len(shape) == 2 else t[:].rearrange(
                {3: "p a b -> p (a b)", 4: "p a b c -> p (a b c)"}[len(shape)])
            m.loads[stage].append((flat, a[name]))
            return t

        m.load = load
        m.wait_load = lambda eng, stage: eng.wait_ge(m.loaded[stage], 16 * len(m.loads[stage]))
        m.loads[0].append((m.ids[:, :], a["ids"]))
        m.stage = 1
        m.ident = load("ident", [P, P])
        m.wqT = load("wqT", [C, KD, D])
        m.wkT = load("wkT", [C, KD, D])
        m.wvT = load("wvT", [C, KD, D])
        m.causal = load("causal", [P, TT, T])
        m.sum_rows = load("sum_rows", [P, C])
        m.woT = load("woT", [C, KD, D])
        m.stage = 3
        m.wgate = load("wgate", [C, 3 * KI, GATE_W])
        m.w_turned = load("w_turned", [C, 3, KI * INNER])
        m.wup = load("wup", [C, KD, 2 * INNER])
        m.conv_w = load("conv_w", [C, KI, CONV_K])
        m.conv_b = load("conv_b", [C, KI])
        m.gate_b = load("gate_b", [GATE_W, 1])
        m.wq = load("wq", [C, KI, MG * GR])
        m.wk = load("wk", [C, KI, MG * GR])
        m.wv = load("wv", [C, KI, INNER])
        m.head_mask36 = load("head_mask36", [GR, MGH])
        m.pick_head = load("pick_head", [C, MH, P], BF16)
        m.ident_bf = load("ident_bf", [P, P], BF16)
        m.future = load("future", [P, P], BF16)
        m.skip = load("skip", [C, 1])
        m.norm_w = load("norm_w", [C, KI])
        m.wdown = load("wdown", [C, KI, D])

        with ExitStack() as until_stage3:
            def sb_early(name, shape, dt=F32):
                return until_stage3.enter_context(nc.sbuf_tensor(name, shape, dt))

            m.stage = 2
            m.wrT = load("wrT", [C, KD, E0], sb=sb_early)
            m.bias8 = load("bias8", [P, TT, E0], sb=sb_early)
            m.rank8 = load("rank8", [P, TT, E0], sb=sb_early)
            m.w1 = load("w1", [C, KD, E0A * D], sb=sb_early)
            m.w2 = load("w2", [C, E0A, KD, D], sb=sb_early)

            taylor_attention(nc, m, a)
            m.end_stage()
            if stop >= 2:
                shared_and_routed_experts(nc, m)
                m.end_stage()
        if stop >= 3:
            mlstm(nc, m)
            m.end_stage()
        if stop >= 4:
            expert_choice(nc, m, a, out)
        if stop < 4:
            dump(nc, m, out)


def dump(nc, m, out):
    done = m.sem("dumped")
    with nc.Block() as block:
        @block.sync
        def _(sp):
            sp.dma_start(out.rearrange("(t p) d -> p t d", p=P), m.h[:, :, :]).then_inc(done, 16)
            sp.wait_ge(done, 16)


def host_layout(np, x, L0_tok_embed_matrix, L0_attn_Wq, L0_attn_Wk, L0_attn_Wv, L0_attn_Wo, L0_ffn_w_fc_sh,
                L0_ffn_w_proj_sh, L0_ffn_w1, L0_ffn_w2, L0_ffn_router_w, L0_ffn_balance_bias, L1_attn_W_up,
                L1_attn_conv_w, L1_attn_conv_b, L1_attn_Wq, L1_attn_Wk, L1_attn_Wv, L1_attn_Wi, L1_attn_bi,
                L1_attn_Wf, L1_attn_bf, L1_attn_norm_w, L1_attn_skip, L1_attn_W_down,
                L1_ffn_gate_weight, L1_ffn_Wg, L1_ffn_Wu, L1_ffn_Wd, L1_ffn_Ws_g, L1_ffn_Ws_u, L1_ffn_Ws_d):
    f = np.float32

    def rows(w, c=C):
        k, n = w.shape
        return np.ascontiguousarray(w.reshape(k // c, c, n).transpose(1, 0, 2).reshape(c, -1))

    p = np.arange(P)
    tok = np.arange(T)
    A = {}
    A["ids"] = np.ascontiguousarray(np.asarray(x).reshape(NT, P).T)
    A["embed"] = np.asarray(L0_tok_embed_matrix)
    A["ident"] = np.eye(P, dtype=f)
    A["wqT"] = rows(np.asarray(L0_attn_Wq).T)
    A["wkT"] = rows(np.asarray(L0_attn_Wk).T)
    A["wvT"] = rows(np.asarray(L0_attn_Wv).T)
    A["woT"] = rows(np.asarray(L0_attn_Wo).T)
    A["sum_rows"] = ((p[:, None] - C) == (np.arange(C)[None] // AF)).astype(f)
    A["causal"] = np.concatenate([1.0 + ((t * P + p)[:, None] <= tok[None]) for t in range(TT)], 1).astype(f)
    A["wrT"] = rows(np.asarray(L0_ffn_router_w).T)
    A["bias8"] = np.ascontiguousarray(np.broadcast_to(np.asarray(L0_ffn_balance_bias), (P, TT, E0))).reshape(P, -1)
    A["rank8"] = np.ascontiguousarray(np.broadcast_to(np.arange(E0, 0, -1, dtype=f), (P, TT, E0))).reshape(P, -1)
    w1 = np.concatenate([np.asarray(L0_ffn_w1).transpose(1, 0, 2).reshape(D, E0 * D), np.asarray(L0_ffn_w_fc_sh)], 1)
    A["w1"] = rows(w1)
    w2 = np.concatenate([np.asarray(L0_ffn_w2), np.asarray(L0_ffn_w_proj_sh)[None]], 0)
    A["w2"] = np.ascontiguousarray(w2.reshape(E0A, KD, C, D).transpose(2, 0, 1, 3)).reshape(C, -1)

    def per_channel(v):
        v = np.asarray(v).reshape(KI, C, -1)
        return np.ascontiguousarray(v.transpose(1, 0, 2)).reshape(C, -1)

    def grouped(w):
        return np.concatenate([w, np.zeros((INNER, MG * GR - INNER), f)], 1)

    gate_w = np.zeros((3 * INNER, GATE_W), f)
    gate_w[:, 0:MH] = L1_attn_Wi
    gate_w[:, 32:32 + MH] = L1_attn_Wf
    A["wgate"] = rows(gate_w)
    gate_b = np.zeros((GATE_W, 1), f)
    gate_b[0:MH, 0] = L1_attn_bi
    gate_b[32:32 + MH, 0] = L1_attn_bf
    A["gate_b"] = gate_b
    wq, wk, wv = np.asarray(L1_attn_Wq), np.asarray(L1_attn_Wk), np.asarray(L1_attn_Wv)
    A["w_turned"] = np.concatenate([rows(w.T) for w in (wq, wk, wv)], 1)
    A["wup"] = rows(np.asarray(L1_attn_W_up))
    A["conv_w"] = per_channel(L1_attn_conv_w)
    A["conv_b"] = per_channel(L1_attn_conv_b)
    A["wq"], A["wk"], A["wv"] = rows(grouped(wq)), rows(grouped(wk)), rows(wv)
    A["head_mask36"] = (np.arange(GR)[:, None] // MD == np.arange(MGH)[None]).astype(f)
    c = np.arange(C)[:, None, None]
    bf = mybir.dt.np(BF16)
    A["pick_head"] = np.ascontiguousarray(np.broadcast_to(c % 32 == np.arange(MH)[None, :, None], (C, MH, P))).astype(bf).reshape(C, -1)
    A["ident_bf"] = np.eye(P, dtype=f).astype(bf)
    A["future"] = np.where(p[:, None] > p[None], f(-1e30), f(0)).astype(bf)
    A["skip"] = np.ascontiguousarray(np.broadcast_to(np.asarray(L1_attn_skip), (C, 1)))
    A["norm_w"] = per_channel(L1_attn_norm_w)
    A["wdown"] = rows(np.asarray(L1_attn_W_down))
    A["gate1T"] = rows(np.asarray(L1_ffn_gate_weight).T)
    A["ws_gu"] = np.concatenate([rows(np.asarray(w).T) for w in (L1_ffn_Ws_g, L1_ffn_Ws_u)], 1)
    A["ws_d"] = rows(np.asarray(L1_ffn_Ws_d).T, P)
    wgu = np.stack([np.asarray(L1_ffn_Wg), np.asarray(L1_ffn_Wu)], 1).reshape(E1, 2, F1, KD, C)
    A["wgu"] = np.ascontiguousarray(wgu.transpose(0, 4, 1, 3, 2)).reshape(E1, C, -1)
    wd = np.asarray(L1_ffn_Wd).reshape(E1, D, KF, P)
    A["wd"] = np.ascontiguousarray(wd.transpose(0, 3, 2, 1)).reshape(E1, P, -1)
    A["below"] = (p[:, None] < p[None]).astype(f).astype(bf)
    A["token_id"] = (np.arange(NT)[None, :] * P + p[:, None]).astype(np.float16)
    bits = np.arange(1, 4, dtype=np.int32)[None, :, None] << np.int32(2 * ROUNDS - 2)
    A["bits"] = np.ascontiguousarray(np.broadcast_to(bits, (P, 3, E1))).astype(np.int32).reshape(P, -1)
    A["bit_value"] = np.full((P, 1), 2.0 ** (2 * ROUNDS - 2), f)
    A["iota1"] = np.ascontiguousarray(np.broadcast_to(np.arange(1, CAP + 1, dtype=f), (P, CAP))).astype(bf)
    return A


def kernel(**inputs):
    import numpy as np
    import concourse.bacc as bacc
    from concourse.bass_utils import run_bass_kernel_spmd

    nc = bacc.Bacc("TRN2", target_bir_lowering=False, num_devices=1)
    arrays = {f"in_{k}": v for k, v in host_layout(np, **inputs).items()}
    a = {k[3:]: nc.dram_tensor(k, v.shape, mybir.dt.from_np(v.dtype), kind="ExternalInput").ap()
         for k, v in arrays.items()}
    out = nc.dram_tensor("out", (N, D), F32, kind="ExternalOutput").ap()
    build(nc, a, out)
    r = run_bass_kernel_spmd(nc, [arrays], core_ids=[0])
    return np.asarray(r.results[0]["out"]).reshape(B, T, D)
```
